# Optimizing a Trainium2 kernel written in Bass

```python
import numpy as np
import jax
import jax.numpy as jnp

def _softmax(x, axis=-1):
    return jax.nn.softmax(x, axis=axis)

def _gelu(x):
    return jax.nn.gelu(x, approximate=True)

def _silu(x):
    return jax.nn.silu(x)

def _sigmoid(x):
    return jax.nn.sigmoid(x)

def _layernorm(x, axis=-1, eps=1e-05):
    m = jnp.mean(x, axis=axis, keepdims=True)
    v = jnp.var(x, axis=axis, keepdims=True)
    return (x - m) / jnp.sqrt(v + eps)

def _scatter_add(tgt, idx, src, axis=0):
    return tgt.at[idx].add(src)

def _segment_sum(src, seg, n):
    return jax.ops.segment_sum(src, seg, n)
kernel_name = 'mk_gnn_resnorm_d4_gnn_r8_206097'

def setup_inputs(seed: int=0):
    np.random.seed(seed)
    _w = jnp.asarray

    def _rec_inputs():
        import jax
        import jax.numpy as jnp
        _gk = jax.random.key(seed)
        x = -0.000202 + 1 * jax.random.normal(jax.random.fold_in(_gk, 1), (6250, 128), jnp.float32)
        _s = jax.random.randint(jax.random.fold_in(_gk, 2), (50000,), 0, 6250, jnp.int32)
        _d = jax.random.randint(jax.random.fold_in(_gk, 3), (50000,), 0, 6250, jnp.int32)
        _loop = jnp.arange(6250, dtype=jnp.int32)
        src = jnp.concatenate([_s, _d, _loop])
        dst = jnp.concatenate([_d, _s, _loop])
        _o = jnp.argsort(dst, stable=True)
        src = src[_o]
        dst = dst[_o]
        edge_attr_4 = -0.000149047 + 1.00006 * jax.random.normal(jax.random.fold_in(_gk, 12), (106250, 4), jnp.float32)
        edge_attr_8 = jax.random.uniform(jax.random.fold_in(_gk, 13), (106250, 8), jnp.float32, 0.0, 0.999999)
        edge_type_8 = jax.random.randint(jax.random.fold_in(_gk, 15), (106250,), 0, 8, jnp.int32)
        return (x, src, dst, edge_attr_4, edge_attr_8, edge_type_8)
    x, src, dst, edge_attr_4, edge_attr_8, edge_type_8 = _rec_inputs()

    def _L0_gnn_setup():
        import jax, jax.numpy as jnp
        import numpy as np
        N_NODES = 6250
        N_EDGES = 100000
        IN_DIM = 128
        HID_DIM = 256
        OUT_DIM = 128

        def _sage_conv(x, edge_index, W_l, b_l, W_r):
            src, dst = (edge_index[0], edge_index[1])
            n = x.shape[0]
            msg_sum = jax.ops.segment_sum(x[src], dst, num_segments=n)
            deg = jax.ops.segment_sum(jnp.ones((src.shape[0],), dtype=x.dtype), dst, num_segments=n)
            msg_mean = msg_sum / jnp.maximum(deg, 1.0)[:, None]
            return msg_mean @ W_l.T + b_l + x @ W_r.T
        key = jax.random.key(seed)
        ks = jax.random.split(key, 8)
        x = jax.random.normal(ks[0], (N_NODES, IN_DIM), dtype=jnp.float32)
        edge_index = jax.random.randint(ks[1], (2, N_EDGES), 0, N_NODES, dtype=jnp.int64)

        def w(k, shape):
            fan_in = shape[-1]
            return jax.random.normal(k, shape, dtype=jnp.float32) / np.sqrt(fan_in)
        W1_l = w(ks[2], (HID_DIM, IN_DIM))
        W1_r = w(ks[3], (HID_DIM, IN_DIM))
        b1 = jnp.zeros((HID_DIM,), dtype=jnp.float32)
        W2_l = w(ks[4], (OUT_DIM, HID_DIM))
        W2_r = w(ks[5], (OUT_DIM, HID_DIM))
        b2 = jnp.zeros((OUT_DIM,), dtype=jnp.float32)
        return {'x': x, 'edge_index': edge_index, 'W1_l': W1_l, 'b1': b1, 'W1_r': W1_r, 'W2_l': W2_l, 'b2': b2, 'W2_r': W2_r}
    _L0_gnn_all = _L0_gnn_setup()
    _L0_gnn_in = {k: v for k, v in _L0_gnn_all.items() if k in ('W1_l', 'b1', 'W1_r', 'W2_l', 'b2', 'W2_r')}
    del _L0_gnn_all

    def _L1_gnn_setup():
        import jax, jax.numpy as jnp
        import numpy as np
        N_NODES = 1250
        N_EDGES = 40000
        MUL = 32
        RADIAL = 8
        HID = 64
        NUM_NEIGHBORS = 32.0
        MIX = np.pi / 8.0
        INV_SQRT2 = 1.0 / np.sqrt(2.0)
        INV_SQRT3 = 1.0 / np.sqrt(3.0)

        def _forward(node_input, edge_attr, edge_scalar_attr, W1_0e, W1_1o, W_mlp1, W_mlp2, Wp_00, Wp_01, Wp_10, Wp_11, W2_0e, W2_1o, edge_src, edge_dst):
            N = node_input.shape[0]
            x0 = node_input[:, :MUL]
            x1 = node_input[:, MUL:].reshape(N, MUL, 3)
            f0 = x0 @ W1_0e / np.sqrt(MUL)
            f1 = jnp.einsum('nui,uw->nwi', x1, W1_1o) / np.sqrt(MUL)
            feat0, self0 = (f0[:, :MUL], f0[:, MUL:])
            feat1, self1 = (f1[:, :MUL], f1[:, MUL:])
            e0 = feat0[edge_src]
            e1 = feat1[edge_src]
            ea0 = edge_attr[:, :1]
            ea1 = edge_attr[:, 1:4]
            h = jax.nn.gelu(edge_scalar_attr @ W_mlp1 / np.sqrt(RADIAL))
            h = jax.nn.gelu(h @ W_mlp2 / np.sqrt(HID))
            w00 = h @ Wp_00
            w01 = h @ Wp_01
            w10 = h @ Wp_10
            w11 = h @ Wp_11
            out0_a = w00 * e0 * ea0
            out0_b = w11 * jnp.sum(e1 * ea1[:, None, :], -1) * INV_SQRT3
            out1_a = (w01 * e0)[:, :, None] * ea1[:, None, :]
            out1_b = w10[:, :, None] * e1 * ea0[:, :, None]
            mid0 = jnp.concatenate([out0_a, out0_b], axis=1) * INV_SQRT2
            mid1 = jnp.concatenate([out1_a, out1_b], axis=1) * INV_SQRT2
            n0 = jax.ops.segment_sum(mid0, edge_dst, num_segments=N) / np.sqrt(NUM_NEIGHBORS)
            n1 = jax.ops.segment_sum(mid1, edge_dst, num_segments=N) / np.sqrt(NUM_NEIGHBORS)
            conv0 = n0 @ W2_0e / np.sqrt(2 * MUL)
            conv1 = jnp.einsum('nui,uw->nwi', n1, W2_1o) / np.sqrt(2 * MUL)
            c, s = (np.cos(MIX), np.sin(MIX))
            y0 = c * self0 + s * conv0
            y1 = c * self1 + s * conv1
            return jnp.concatenate([y0, y1.reshape(N, MUL * 3)], axis=1)
        key = jax.random.key(seed)
        ks = jax.random.split(key, 16)
        inp = {'node_input': jax.random.normal(ks[0], (N_NODES, 4 * MUL), jnp.float32), 'edge_attr': jax.random.normal(ks[1], (N_EDGES, 4), jnp.float32), 'edge_scalar_attr': jax.random.uniform(ks[2], (N_EDGES, RADIAL), jnp.float32), 'W1_0e': jax.random.normal(ks[3], (MUL, 2 * MUL), jnp.float32), 'W1_1o': jax.random.normal(ks[4], (MUL, 2 * MUL), jnp.float32), 'W_mlp1': jax.random.normal(ks[5], (RADIAL, HID), jnp.float32), 'W_mlp2': jax.random.normal(ks[6], (HID, HID), jnp.float32), 'Wp_00': jax.random.normal(ks[7], (HID, MUL), jnp.float32), 'Wp_01': jax.random.normal(ks[8], (HID, MUL), jnp.float32), 'Wp_10': jax.random.normal(ks[9], (HID, MUL), jnp.float32), 'Wp_11': jax.random.normal(ks[10], (HID, MUL), jnp.float32), 'W2_0e': jax.random.normal(ks[11], (2 * MUL, MUL), jnp.float32), 'W2_1o': jax.random.normal(ks[12], (2 * MUL, MUL), jnp.float32), 'edge_src': jax.random.randint(ks[13], (N_EDGES,), 0, N_NODES, jnp.int32), 'edge_dst': jax.random.randint(ks[14], (N_EDGES,), 0, N_NODES, jnp.int32)}
        return inp
    _L1_gnn_all = _L1_gnn_setup()
    _L1_gnn_in = {k: v for k, v in _L1_gnn_all.items() if k in ('W1_0e', 'W1_1o', 'W_mlp1', 'W_mlp2', 'Wp_00', 'Wp_01', 'Wp_10', 'Wp_11', 'W2_0e', 'W2_1o')}
    del _L1_gnn_all

    def _L2_gnn_setup():
        import jax, jax.numpy as jnp
        import numpy as np
        N = 6250
        E = 100000
        D = 128
        R = 8
        EPS = 1e-05

        def _mk_mlp(key, din, dh, dout, n):
            k1, k2 = jax.random.split(key)
            W1 = jax.random.normal(k1, (n, din, dh), jnp.float32) / np.sqrt(din)
            b1 = jnp.zeros((n, dh), jnp.float32)
            gamma = jnp.ones((n, dh), jnp.float32)
            beta = jnp.zeros((n, dh), jnp.float32)
            W2 = jax.random.normal(k2, (n, dh, dout), jnp.float32) / np.sqrt(dh)
            b2 = jnp.zeros((n, dout), jnp.float32)
            return (W1, b1, gamma, beta, W2, b2)

        def _rgin_conv(x, src, dst, et, W1, b1, gamma, beta, W2, b2, bias):
            n = x.shape[0]
            xs = x[src]
            seg = dst * R + et
            h = jax.ops.segment_sum(xs, seg, num_segments=n * R)
            h = h.reshape(n, R, -1).transpose(1, 0, 2)
            inp = jnp.concatenate([h, x[None]], axis=0)
            z = jnp.einsum('rnd,rdh->rnh', inp, W1) + b1[:, None, :]
            mu = z.mean(axis=1, keepdims=True)
            var = z.var(axis=1, keepdims=True)
            zn = (z - mu) * jax.lax.rsqrt(var + EPS) * gamma[:, None, :] + beta[:, None, :]
            a = jax.nn.relu(zn)
            o = jnp.einsum('rnh,rho->rno', a, W2) + b2[:, None, :]
            return o.sum(axis=0) + bias
        key = jax.random.key(seed)
        ks = jax.random.split(key, 8)
        inp = {'x': jax.random.normal(ks[0], (N, D), jnp.float32), 'edge_index': jax.random.randint(ks[1], (2, E), 0, N, dtype=jnp.int64), 'edge_type': jax.random.randint(ks[2], (E,), 0, R, dtype=jnp.int64)}
        for li, k in [(0, ks[3]), (1, ks[4])]:
            W1, b1, g, be, W2, b2 = _mk_mlp(k, D, D, D, R + 1)
            inp[f'l{li}_W1'] = W1
            inp[f'l{li}_b1'] = b1
            inp[f'l{li}_gamma'] = g
            inp[f'l{li}_beta'] = be
            inp[f'l{li}_W2'] = W2
            inp[f'l{li}_b2'] = b2
            inp[f'l{li}_bias'] = jnp.zeros((D,), jnp.float32)
        return inp
    _L2_gnn_all = _L2_gnn_setup()
    _L2_gnn_in = {k: v for k, v in _L2_gnn_all.items() if k in ('l0_W1', 'l0_b1', 'l0_gamma', 'l0_beta', 'l0_W2', 'l0_b2', 'l0_bias', 'l1_W1', 'l1_b1', 'l1_gamma', 'l1_beta', 'l1_W2', 'l1_b2', 'l1_bias')}
    del _L2_gnn_all

    def _L3_gnn_setup():
        import jax, jax.numpy as jnp
        import numpy as np
        N_NODES = 12500
        N_EDGES = 200000
        D_IN = 128
        D_HID = 128
        D_OUT = 128

        def _sage_conv(x, src, dst, Wl, bl, Wr, n_nodes):
            msg = x[src]
            agg = jax.ops.segment_sum(msg, dst, num_segments=n_nodes)
            cnt = jax.ops.segment_sum(jnp.ones((src.shape[0],), x.dtype), dst, num_segments=n_nodes)[:, None]
            mean = jnp.where(cnt > 0, agg / jnp.maximum(cnt, 1), 0.0)
            return mean @ Wl.T + bl + x @ Wr.T

        def _prelu(x, w):
            return jnp.where(x > 0, x, w * x)
        key = jax.random.key(seed)
        ks = jax.random.split(key, 10)
        x = jax.random.normal(ks[0], (N_NODES, D_IN), dtype=jnp.float32)
        edge_index = jax.random.randint(ks[1], (2, N_EDGES), 0, N_NODES, dtype=jnp.int64)

        def lin(k, out_d, in_d):
            s = 1.0 / np.sqrt(in_d)
            return jax.random.uniform(k, (out_d, in_d), jnp.float32, -s, s)
        return {'x': x, 'edge_index': edge_index, 'batch_size': N_NODES, 'framework': 1, 'W1l': lin(ks[2], D_HID, D_IN), 'b1': jnp.zeros((D_HID,), jnp.float32), 'W1r': lin(ks[3], D_HID, D_IN), 'W2l': lin(ks[4], D_HID, D_HID), 'b2': jnp.zeros((D_HID,), jnp.float32), 'W2r': lin(ks[5], D_HID, D_HID), 'W3l': lin(ks[6], D_OUT, D_HID), 'b3': jnp.zeros((D_OUT,), jnp.float32), 'W3r': lin(ks[7], D_OUT, D_HID), 'prelu_w': jnp.asarray(0.25, jnp.float32)}
    _L3_gnn_all = _L3_gnn_setup()
    _L3_gnn_in = {k: v for k, v in _L3_gnn_all.items() if k in ('W1l', 'b1', 'W1r', 'W2l', 'b2', 'W2r', 'W3l', 'b3', 'W3r', 'prelu_w')}
    del _L3_gnn_all
    return {'x': x, 'src': src, 'dst': dst, 'edge_attr_4': edge_attr_4, 'edge_attr_8': edge_attr_8, 'edge_type_8': edge_type_8, 'L0_gnn_W1_l': _L0_gnn_in['W1_l'], 'L0_gnn_b1': _L0_gnn_in['b1'], 'L0_gnn_W1_r': _L0_gnn_in['W1_r'], 'L0_gnn_W2_l': _L0_gnn_in['W2_l'], 'L0_gnn_b2': _L0_gnn_in['b2'], 'L0_gnn_W2_r': _L0_gnn_in['W2_r'], 'L1_gnn_W1_0e': _L1_gnn_in['W1_0e'], 'L1_gnn_W1_1o': _L1_gnn_in['W1_1o'], 'L1_gnn_W_mlp1': _L1_gnn_in['W_mlp1'], 'L1_gnn_W_mlp2': _L1_gnn_in['W_mlp2'], 'L1_gnn_Wp_00': _L1_gnn_in['Wp_00'], 'L1_gnn_Wp_01': _L1_gnn_in['Wp_01'], 'L1_gnn_Wp_10': _L1_gnn_in['Wp_10'], 'L1_gnn_Wp_11': _L1_gnn_in['Wp_11'], 'L1_gnn_W2_0e': _L1_gnn_in['W2_0e'], 'L1_gnn_W2_1o': _L1_gnn_in['W2_1o'], 'L2_gnn_l0_W1': _L2_gnn_in['l0_W1'], 'L2_gnn_l0_b1': _L2_gnn_in['l0_b1'], 'L2_gnn_l0_gamma': _L2_gnn_in['l0_gamma'], 'L2_gnn_l0_beta': _L2_gnn_in['l0_beta'], 'L2_gnn_l0_W2': _L2_gnn_in['l0_W2'], 'L2_gnn_l0_b2': _L2_gnn_in['l0_b2'], 'L2_gnn_l0_bias': _L2_gnn_in['l0_bias'], 'L2_gnn_l1_W1': _L2_gnn_in['l1_W1'], 'L2_gnn_l1_b1': _L2_gnn_in['l1_b1'], 'L2_gnn_l1_gamma': _L2_gnn_in['l1_gamma'], 'L2_gnn_l1_beta': _L2_gnn_in['l1_beta'], 'L2_gnn_l1_W2': _L2_gnn_in['l1_W2'], 'L2_gnn_l1_b2': _L2_gnn_in['l1_b2'], 'L2_gnn_l1_bias': _L2_gnn_in['l1_bias'], 'L3_gnn_W1l': _L3_gnn_in['W1l'], 'L3_gnn_b1': _L3_gnn_in['b1'], 'L3_gnn_W1r': _L3_gnn_in['W1r'], 'L3_gnn_W2l': _L3_gnn_in['W2l'], 'L3_gnn_b2': _L3_gnn_in['b2'], 'L3_gnn_W2r': _L3_gnn_in['W2r'], 'L3_gnn_W3l': _L3_gnn_in['W3l'], 'L3_gnn_b3': _L3_gnn_in['b3'], 'L3_gnn_W3r': _L3_gnn_in['W3r'], 'L3_gnn_prelu_w': _L3_gnn_in['prelu_w']}

def reference(x, src, dst, edge_attr_4, edge_attr_8, edge_type_8, L0_gnn_W1_l, L0_gnn_b1, L0_gnn_W1_r, L0_gnn_W2_l, L0_gnn_b2, L0_gnn_W2_r, L1_gnn_W1_0e, L1_gnn_W1_1o, L1_gnn_W_mlp1, L1_gnn_W_mlp2, L1_gnn_Wp_00, L1_gnn_Wp_01, L1_gnn_Wp_10, L1_gnn_Wp_11, L1_gnn_W2_0e, L1_gnn_W2_1o, L2_gnn_l0_W1, L2_gnn_l0_b1, L2_gnn_l0_gamma, L2_gnn_l0_beta, L2_gnn_l0_W2, L2_gnn_l0_b2, L2_gnn_l0_bias, L2_gnn_l1_W1, L2_gnn_l1_b1, L2_gnn_l1_gamma, L2_gnn_l1_beta, L2_gnn_l1_W2, L2_gnn_l1_b2, L2_gnn_l1_bias, L3_gnn_W1l, L3_gnn_b1, L3_gnn_W1r, L3_gnn_W2l, L3_gnn_b2, L3_gnn_W2r, L3_gnn_W3l, L3_gnn_b3, L3_gnn_W3r, L3_gnn_prelu_w):
    import jax
    import jax.numpy as jnp

    def _L0_gnn_ref(x, edge_index, W1_l, b1, W1_r, W2_l, b2, W2_r):
        import jax, jax.numpy as jnp
        import numpy as np
        N_NODES = 6250
        N_EDGES = 100000
        IN_DIM = 128
        HID_DIM = 256
        OUT_DIM = 128

        def _sage_conv(x, edge_index, W_l, b_l, W_r):
            src, dst = (edge_index[0], edge_index[1])
            n = x.shape[0]
            msg_sum = jax.ops.segment_sum(x[src], dst, num_segments=n)
            deg = jax.ops.segment_sum(jnp.ones((src.shape[0],), dtype=x.dtype), dst, num_segments=n)
            msg_mean = msg_sum / jnp.maximum(deg, 1.0)[:, None]
            return msg_mean @ W_l.T + b_l + x @ W_r.T
        h = _sage_conv(x, edge_index, W1_l, b1, W1_r)
        h = jax.nn.relu(h)
        out = _sage_conv(h, edge_index, W2_l, b2, W2_r)
        return out

    def _L1_gnn_ref(node_input, edge_attr, edge_scalar_attr, W1_0e, W1_1o, W_mlp1, W_mlp2, Wp_00, Wp_01, Wp_10, Wp_11, W2_0e, W2_1o, edge_src, edge_dst):
        import jax, jax.numpy as jnp
        import numpy as np
        N_NODES = 1250
        N_EDGES = 40000
        MUL = 32
        RADIAL = 8
        HID = 64
        NUM_NEIGHBORS = 32.0
        MIX = np.pi / 8.0
        INV_SQRT2 = 1.0 / np.sqrt(2.0)
        INV_SQRT3 = 1.0 / np.sqrt(3.0)

        def _forward(node_input, edge_attr, edge_scalar_attr, W1_0e, W1_1o, W_mlp1, W_mlp2, Wp_00, Wp_01, Wp_10, Wp_11, W2_0e, W2_1o, edge_src, edge_dst):
            N = node_input.shape[0]
            x0 = node_input[:, :MUL]
            x1 = node_input[:, MUL:].reshape(N, MUL, 3)
            f0 = x0 @ W1_0e / np.sqrt(MUL)
            f1 = jnp.einsum('nui,uw->nwi', x1, W1_1o) / np.sqrt(MUL)
            feat0, self0 = (f0[:, :MUL], f0[:, MUL:])
            feat1, self1 = (f1[:, :MUL], f1[:, MUL:])
            e0 = feat0[edge_src]
            e1 = feat1[edge_src]
            ea0 = edge_attr[:, :1]
            ea1 = edge_attr[:, 1:4]
            h = jax.nn.gelu(edge_scalar_attr @ W_mlp1 / np.sqrt(RADIAL))
            h = jax.nn.gelu(h @ W_mlp2 / np.sqrt(HID))
            w00 = h @ Wp_00
            w01 = h @ Wp_01
            w10 = h @ Wp_10
            w11 = h @ Wp_11
            out0_a = w00 * e0 * ea0
            out0_b = w11 * jnp.sum(e1 * ea1[:, None, :], -1) * INV_SQRT3
            out1_a = (w01 * e0)[:, :, None] * ea1[:, None, :]
            out1_b = w10[:, :, None] * e1 * ea0[:, :, None]
            mid0 = jnp.concatenate([out0_a, out0_b], axis=1) * INV_SQRT2
            mid1 = jnp.concatenate([out1_a, out1_b], axis=1) * INV_SQRT2
            n0 = jax.ops.segment_sum(mid0, edge_dst, num_segments=N) / np.sqrt(NUM_NEIGHBORS)
            n1 = jax.ops.segment_sum(mid1, edge_dst, num_segments=N) / np.sqrt(NUM_NEIGHBORS)
            conv0 = n0 @ W2_0e / np.sqrt(2 * MUL)
            conv1 = jnp.einsum('nui,uw->nwi', n1, W2_1o) / np.sqrt(2 * MUL)
            c, s = (np.cos(MIX), np.sin(MIX))
            y0 = c * self0 + s * conv0
            y1 = c * self1 + s * conv1
            return jnp.concatenate([y0, y1.reshape(N, MUL * 3)], axis=1)
        return _forward(node_input, edge_attr, edge_scalar_attr, W1_0e, W1_1o, W_mlp1, W_mlp2, Wp_00, Wp_01, Wp_10, Wp_11, W2_0e, W2_1o, edge_src, edge_dst)

    def _L2_gnn_ref(x, edge_index, edge_type, l0_W1, l0_b1, l0_gamma, l0_beta, l0_W2, l0_b2, l0_bias, l1_W1, l1_b1, l1_gamma, l1_beta, l1_W2, l1_b2, l1_bias):
        import jax, jax.numpy as jnp
        import numpy as np
        N = 6250
        E = 100000
        D = 128
        R = 8
        EPS = 1e-05

        def _mk_mlp(key, din, dh, dout, n):
            k1, k2 = jax.random.split(key)
            W1 = jax.random.normal(k1, (n, din, dh), jnp.float32) / np.sqrt(din)
            b1 = jnp.zeros((n, dh), jnp.float32)
            gamma = jnp.ones((n, dh), jnp.float32)
            beta = jnp.zeros((n, dh), jnp.float32)
            W2 = jax.random.normal(k2, (n, dh, dout), jnp.float32) / np.sqrt(dh)
            b2 = jnp.zeros((n, dout), jnp.float32)
            return (W1, b1, gamma, beta, W2, b2)

        def _rgin_conv(x, src, dst, et, W1, b1, gamma, beta, W2, b2, bias):
            n = x.shape[0]
            xs = x[src]
            seg = dst * R + et
            h = jax.ops.segment_sum(xs, seg, num_segments=n * R)
            h = h.reshape(n, R, -1).transpose(1, 0, 2)
            inp = jnp.concatenate([h, x[None]], axis=0)
            z = jnp.einsum('rnd,rdh->rnh', inp, W1) + b1[:, None, :]
            mu = z.mean(axis=1, keepdims=True)
            var = z.var(axis=1, keepdims=True)
            zn = (z - mu) * jax.lax.rsqrt(var + EPS) * gamma[:, None, :] + beta[:, None, :]
            a = jax.nn.relu(zn)
            o = jnp.einsum('rnh,rho->rno', a, W2) + b2[:, None, :]
            return o.sum(axis=0) + bias
        src, dst = (edge_index[0], edge_index[1])
        h = _rgin_conv(x, src, dst, edge_type, l0_W1, l0_b1, l0_gamma, l0_beta, l0_W2, l0_b2, l0_bias)
        h = jax.nn.relu(h)
        out = _rgin_conv(h, src, dst, edge_type, l1_W1, l1_b1, l1_gamma, l1_beta, l1_W2, l1_b2, l1_bias)
        return out

    def _L3_gnn_ref(x, edge_index, batch_size, framework, W1l, b1, W1r, W2l, b2, W2r, W3l, b3, W3r, prelu_w):
        import jax, jax.numpy as jnp
        import numpy as np
        N_NODES = 12500
        N_EDGES = 200000
        D_IN = 128
        D_HID = 128
        D_OUT = 128

        def _sage_conv(x, src, dst, Wl, bl, Wr, n_nodes):
            msg = x[src]
            agg = jax.ops.segment_sum(msg, dst, num_segments=n_nodes)
            cnt = jax.ops.segment_sum(jnp.ones((src.shape[0],), x.dtype), dst, num_segments=n_nodes)[:, None]
            mean = jnp.where(cnt > 0, agg / jnp.maximum(cnt, 1), 0.0)
            return mean @ Wl.T + bl + x @ Wr.T

        def _prelu(x, w):
            return jnp.where(x > 0, x, w * x)
        src, dst = (edge_index[0], edge_index[1])
        n = x.shape[0]
        h = _prelu(_sage_conv(x, src, dst, W1l, b1, W1r, n), prelu_w)
        h = _prelu(_sage_conv(h, src, dst, W2l, b2, W2r, n), prelu_w)
        h = _prelu(_sage_conv(h, src, dst, W3l, b3, W3r, n), prelu_w)
        if framework:
            return h
        else:
            return h[:batch_size]
    edge_index = jnp.stack([src, dst])
    x = _layernorm(x + _L0_gnn_ref(x, edge_index, L0_gnn_W1_l, L0_gnn_b1, L0_gnn_W1_r, L0_gnn_W2_l, L0_gnn_b2, L0_gnn_W2_r), axis=-1)
    x = _layernorm(x + _L1_gnn_ref(x, edge_attr_4, edge_attr_8, L1_gnn_W1_0e, L1_gnn_W1_1o, L1_gnn_W_mlp1, L1_gnn_W_mlp2, L1_gnn_Wp_00, L1_gnn_Wp_01, L1_gnn_Wp_10, L1_gnn_Wp_11, L1_gnn_W2_0e, L1_gnn_W2_1o, src, dst), axis=-1)
    x = _layernorm(x + _L2_gnn_ref(x, edge_index, edge_type_8, L2_gnn_l0_W1, L2_gnn_l0_b1, L2_gnn_l0_gamma, L2_gnn_l0_beta, L2_gnn_l0_W2, L2_gnn_l0_b2, L2_gnn_l0_bias, L2_gnn_l1_W1, L2_gnn_l1_b1, L2_gnn_l1_gamma, L2_gnn_l1_beta, L2_gnn_l1_W2, L2_gnn_l1_b2, L2_gnn_l1_bias), axis=-1)
    x = _layernorm(x + _L3_gnn_ref(x, edge_index, 6250, 1, L3_gnn_W1l, L3_gnn_b1, L3_gnn_W1r, L3_gnn_W2l, L3_gnn_b2, L3_gnn_W2r, L3_gnn_W3l, L3_gnn_b3, L3_gnn_W3r, L3_gnn_prelu_w), axis=-1)
    return x

_drawn_inputs = setup_inputs


def setup_inputs(seed=0):
    import zlib

    import numpy as np

    out = dict(_drawn_inputs(seed))
    spreads = {'L0_gnn_b1': (0.0, 0.1),
     'L0_gnn_b2': (0.0, 0.1),
     'L2_gnn_l0_b1': (0.0, 0.8),
     'L2_gnn_l0_gamma': (1.0, 0.2),
     'L2_gnn_l0_beta': (0.0, 0.1),
     'L2_gnn_l0_b2': (0.0, 0.1),
     'L2_gnn_l0_bias': (0.0, 0.1),
     'L2_gnn_l1_b1': (0.0, 0.8),
     'L2_gnn_l1_gamma': (1.0, 0.2),
     'L2_gnn_l1_beta': (0.0, 0.1),
     'L2_gnn_l1_b2': (0.0, 0.1),
     'L2_gnn_l1_bias': (0.0, 0.1),
     'L3_gnn_b1': (0.0, 0.413),
     'L3_gnn_b2': (0.0, 0.1),
     'L3_gnn_b3': (0.0, 0.1)}
    factors = {}
    for name, (base, spread) in spreads.items():
        noise = np.random.default_rng([zlib.crc32(name.encode()), seed]).standard_normal(out[name].shape)
        drawn = base * np.exp(spread * noise) if base else spread * noise
        out[name] = jnp.asarray(drawn.astype(out[name].dtype))
    for name, factor in factors.items():
        out[name] = (out[name] * factor).astype(out[name].dtype)
    return out
```

```python
from contextlib import ExitStack

import numpy as np

import concourse.bass as bass
from concourse import mybir

ALU = mybir.AluOpType
ACT = mybir.ActivationFunctionType
AX = mybir.AxisListType
F32 = mybir.dt.float32
I32 = mybir.dt.int32

P = 128
N, E, D = 6250, 106250, 128
R = 8
NT = -(-N // P)
NP = NT * P
LAST = N - (NT - 1) * P
S = 8
ET = -(-E // P)
NG = -(-ET // S)
TPP = 8
TROWS = -(-(NG + 2) * S // TPP)
ETP = TROWS * TPP
W = 32
OH = 4
ACCW = NP + W
CHUNK_TILES = [17, 16, 16]
CHUNK_T0 = [0, 17, 33, 49]
CHUNKS = len(CHUNK_TILES)
MUL, RADIAL, HID1 = 32, 8, 64
FAR = 32768.0
EPS = 1e-5
UNIT = 4

assert CHUNK_T0[-1] == NT and (max(CHUNK_TILES) * P + W) * R <= 3 * ACCW

INV_MUL = float(1.0 / np.sqrt(MUL))
COS, SIN = float(np.cos(np.pi / 8.0)), float(np.sin(np.pi / 8.0))
CONV = SIN / float(np.sqrt(2 * MUL) * np.sqrt(32.0) * np.sqrt(2.0))
CONV_DOT = CONV / float(np.sqrt(3.0))


def build(nc, x, x_t, src, dst, dst_tiles, etype, ea4, ea8, w, w_rel, out, layers):
    with ExitStack() as ctx:
        def sb(name, shape, dt=F32):
            return ctx.enter_context(nc.sbuf_tensor(name, shape, dt))

        def sem(name):
            return ctx.enter_context(nc.semaphore(name))

        def table(name):
            return nc.dram_tensor(name, [NP, D], F32, kind="Internal").ap()

        tab_hid = table("tab_hid")
        tab_x1 = table("tab_x1")
        tab_feat = table("tab_feat")
        tab_x2 = table("tab_x2")
        tab_h2 = table("tab_h2")
        tab_x3 = table("tab_x3")
        tab_h3 = [table("tab_h3a"), table("tab_h3b")]
        z_dram = nc.dram_tensor("z_dram", [2, NT, P, (R + 1) * D], F32, kind="Internal").ap()

        arena = sb("arena", [P, 3 * ACCW])
        acc3 = arena[:].rearrange("p (k c) -> p k c", k=3)
        cur = sb("cur", [P, NP])
        rdeg = sb("rdeg", [P, NP])
        src_sb = sb("src_sb", [P, ETP], I32)
        NTYPE = 1 + CHUNKS
        rel_seg = sb("rel_seg", [P, NTYPE, ETP])
        win = sb("win", [1, NTYPE, ETP], I32)
        ptab = sb("ptab", [P, 6 * CHUNKS], I32)
        ring = sb("ring", [P, S, D])
        slot_idx = sb("slot_idx", [P, S], I32)
        onehot = sb("onehot", [P, OH, W * R])
        share = sb("share", [P, 2 * (R + 1) * D + NT * (R + 1) * 6])
        msg = share[:, 0:OH * 3 * D].rearrange("p (s c) -> p s c", s=OH)
        h1 = share[0:HID1, 1536:2048]
        h2 = share[0:HID1, 2048:3072].rearrange("p (b c) -> p b c", b=2)
        attr = share[0:RADIAL, 3072:4096].rearrange("p (b c) -> p b c", b=2)
        relw1 = share[:, 0:(R + 1) * D].rearrange("p (r c) -> p r c", c=D)
        relw2 = share[:, (R + 1) * D:2 * (R + 1) * D].rearrange("p (r c) -> p r c", c=D)
        zst = share[:, 2 * (R + 1) * D:].rearrange("p (t r k) -> p t r k", t=NT, k=6)
        qs = sb("qs", [P, 2, 3, 2, MUL])
        xone = sb("xone", [P, W * R])
        xseg = sb("xseg", [P, 1])
        ident = sb("ident", [P, P])
        ones = sb("ones", [P, P])
        minmax = sb("minmax", [P, 2, TPP])
        iota_w = sb("iota_w", [P, W * R])
        iota_i = sb("iota_i", [P, W * R], I32)
        ea = sb("ea", [P, 2, UNIT, 4])
        t_a = sb("t_a", [P, 2, (R + 1) * D])
        t_b = sb("t_b", [P, 2, D])
        t_x = sb("t_x", [P, 2, D])
        t_y = sb("t_y", [P, 2, 2 * D])
        t_m = sb("t_m", [P, 2, D])
        t_n = sb("t_n", [P, 2, D])
        rowt = sb("rowt", [P, 2, D])
        st6 = sb("st6", [P, 2, 6])
        mv = sb("mv", [P, 2, 2])
        sd = sb("sd", [P, 2, 2])
        zmv = sb("zmv", [P, R + 1, 2])
        bn = sb("bn", [P, 4, R + 1])
        eps_c = sb("eps_c", [P, 1])
        ranges = sb("ranges", [P, 3, CHUNKS])
        ranges_i = sb("ranges_i", [P, CHUNKS], I32)
        ptab_f = sb("ptab_f", [P, 6 * CHUNKS])
        wsb = {k: sb("w_" + k, list(a.shape)) for k, a in w.items()}
        relv = sb("relv", [P, 4, R + 1])
        relbias = sb("relbias", [P, 2])
        ps = ctx.enter_context(nc.psum_tensor("ps", [P, 8, 512], F32))

        loaded, setup_done = sem("loaded"), sem("setup_done")
        iotas, ident_ok, minmax_ok, spread_ok, rows_sum = sem("iotas"), sem("ident_ok"), sem("minmax_ok"), sem("spread_ok"), sem("rows_sum")
        fence = {e: sem("fence_" + e) for e in ("pool", "act", "pe", "dve", "sp")}

        class PassSems:
            def __init__(self, tag):
                self.gathered = [sem(f"gathered{tag}{i}") for i in range(S)]
                self.staged = sem(f"staged{tag}")
                self.onehot = sem(f"onehot{tag}")
                self.used = sem(f"used{tag}")
                self.added = sem(f"added{tag}")

        stat, dyn = PassSems("_s"), PassSems("_d")
        acc_zero = sem("acc_zero")
        x_onehot, x_sum = sem("x_onehot"), sem("x_sum")
        attr_in = [sem("attr_in0"), sem("attr_in1")]
        h1_sum, h1_done, h2_sum, h2_done = sem("h1_sum"), sem("h1_done"), sem("h2_sum"), sem("h2_done")
        rad_sum, scaled = sem("rad_sum"), sem("scaled")
        mean_ok, sum_ok, relu_ok, min_ok, evac_ok = sem("mean_ok"), sem("sum_ok"), sem("relu_ok"), sem("min_ok"), sem("evac_ok")
        turn_ok, row_ok, kept_ok = sem("turn_ok"), sem("row_ok"), sem("kept_ok")
        stored = [sem("stored0"), sem("stored1")]
        x_in = [sem("x_in0"), sem("x_in1")]
        res_ok, lnst_ok, mv_ok, sd_ok, rstd_ok = sem("res_ok"), sem("lnst_ok"), sem("mv_ok"), sem("sd_ok"), sem("rstd_ok")
        back_ok, cur_ok = sem("back_ok"), sem("cur_ok")
        z_sum, z_ok, z_stat, z_act = sem("z_sum"), sem("z_ok"), sem("z_stat"), sem("z_act")
        z_out = [sem("z_out0"), sem("z_out1")]
        z_in = [sem("z_in0"), sem("z_in1")]
        relw_in, bn_mv, bn_sd, bn_ok = sem("relw_in"), sem("bn_mv"), sem("bn_sd"), sem("bn_ok")
        chain = sem("chain")

        ALL = ["L0a", "L0b", "feat", "L1", "L2a", "L2b", "L3a", "L3b", "L3c"]
        order = ALL[:[0, 2, 4, 6, 9][layers]]
        final = order[-1]
        SAGE = ["L0a", "L0b", "L3a", "L3b", "L3c"]
        KEEP = ["L0a", "L2a", "L3a", "L3b"]
        PRELU = ["L3a", "L3b", "L3c"]
        NORM = ["L0b", "L1", "L2b", "L3c"]
        REL = ["L2a", "L2b"]
        PASS = {"L0a": 0, "L0b": NG, "L1": 2 * NG, "L3a": 3 * NG, "L3b": 4 * NG, "L3c": 5 * NG}
        PASS_BLOCKS = {"L0a": 2, "L0b": 1, "L1": 3, "L3a": 1, "L3b": 1, "L3c": 1}
        TABLE = {"L0a": x, "L0b": tab_hid, "L1": tab_feat, "L2a": tab_x2, "L2b": tab_h2,
                 "L3a": tab_x3, "L3b": tab_h3[0], "L3c": tab_h3[1]}
        ROWS = {"L0a": tab_hid, "L0b": tab_x1, "feat": tab_feat, "L1": tab_x2, "L2a": tab_h2,
                "L2b": tab_x3, "L3a": tab_h3[0], "L3b": tab_h3[1], "L3c": None}
        RESIDUAL = {"L0b": x, "L1": tab_x1, "L2b": tab_x2, "L3c": tab_x3}
        PER = [(NT + 1) // 2, NT // 2]

        def count(stage, T, of=ALL):
            return NT * of.index(stage) + T + 1

        def half_count(stage, b, h, of=ALL):
            return 16 * (PER[b] * of.index(stage) + h + 1)

        def before(stage):
            return ALL[ALL.index(stage) - 1]

        def cols(T, n=P):
            return slice(T * P, T * P + n) if isinstance(T, int) else bass.ds(T * P, n)

        def early(T):
            return isinstance(T, int) and T < 2

        def mark(eng, name):
            eng.sem_inc(fence[name], 1)

        def tiles(eng, steps, T0=0, T1=NT):
            lags = max(lag for lag, _ in steps)

            def at(T, i):
                for lag, step in steps:
                    t = T - lag
                    if i is not None:
                        step(i * 2 + t, t % 2, i + t // 2)
                    elif T0 <= t < T1:
                        step(t, t % 2, t // 2)

            first = T0 + 2 + lags
            pairs = (T1 - 1 - first) // 2
            for T in range(T0, first):
                at(T, None)
            with eng.Fori(0, pairs) as i:
                at(first, i)
                at(first + 1, i)
            for T in range(first + 2 * pairs, T1 + lags):
                at(T, None)

        def rows_stored(eng, stage):
            for b in range(2):
                eng.wait_ge(stored[b], half_count(stage, b, PER[b] - 1))

        def chunk_values(eng, layer, c):
            k = 3 * (layer * CHUNKS + c)
            g0 = eng.value_load(ptab[0:1, k:k + 1], min_val=0, max_val=6 * NG)
            g1 = eng.value_load(ptab[0:1, k + 1:k + 2], min_val=1, max_val=6 * NG)
            j0 = eng.value_load(ptab[0:1, k + 2:k + 3], min_val=0, max_val=ET)
            return g0, g1, j0

        def static_groups(eng, name, body, peel_last=False):
            g0 = PASS[name]
            with eng.Fori(0, NG - peel_last) as i:
                body(i + g0, i * S, i)
            if peel_last:
                body(g0 + NG - 1, (NG - 1) * S, NG - 1)

        def chunk_groups(eng, layer, c, body):
            g0, g1, j0 = chunk_values(eng, layer, c)
            with eng.Fori(g0, g1) as g:
                body(g, eng.snap((g - g0) * S + j0).with_bounds(min_val=0, max_val=ETP - S), None)
            return g1

        def window(eng, kind, j):
            v = eng.value_load(win[0:1, kind, bass.ds(j, 1)] if not isinstance(j, int) else win[0:1, kind, j:j + 1],
                               min_val=0, max_val=(NP << 8) + 255)
            return v

        ps_flat = ps[:].rearrange("p b c -> p (b c)")
        X_BANK, H_BANK, RAD_BANK = 7, 4, 5

        def ps_tile(name, s):
            blocks, width = sums_shape(name)
            return ps[:, s % OH, 0:blocks * width]

        def sums_shape(name):
            return (1, W * R) if name in REL else (PASS_BLOCKS[name], W)

        def rad_ps(s):
            return ps[:, RAD_BANK + s % 2, 0:6 * MUL]

        def acc_at(name, node):
            if name in REL:
                return arena[:, bass.ds(node * R, W * R)]
            return acc3[:, 0:PASS_BLOCKS[name], bass.ds(node, W)]

        def shaped(name, ap):
            if name in REL:
                return ap
            return ap.rearrange("p (k c) -> p k c", k=PASS_BLOCKS[name])

        block = ctx.enter_context(nc.Block())

        @block.sync
        def _(sp):
            for to, of in [(src_sb[:], src), (arena[:, 0:ETP].bitcast(I32), dst),
                           (arena[:, ETP:2 * ETP].bitcast(I32), etype),
                           (arena[0:TROWS, 2 * ETP:2 * ETP + TPP * P].bitcast(I32), dst_tiles),
                           (cur[:], x_t), *((wsb[k][:], w[k]) for k in wsb)]:
                sp.dma_start(to, of).then_inc(loaded, 16)

            def z_ap(layer, T):
                if isinstance(T, int):
                    return z_dram[layer, T, :, :]
                return z_dram[layer, bass.ds(T, 1), :, :].rearrange("a p c -> (a p) c")

            def radial_load(u, b):
                if isinstance(u, int):
                    a8, a4 = ea8[:, u * UNIT * P:(u + 1) * UNIT * P], ea4[:, u * UNIT * 4:(u + 1) * UNIT * 4]
                else:
                    a8, a4 = ea8[:, bass.ds(u * (UNIT * P), UNIT * P)], ea4[:, bass.ds(u * (UNIT * 4), UNIT * 4)]
                sp.dma_start(attr[:, b, :], a8).then_inc(attr_in[b], 16)
                sp.dma_start(ea[:, b, :, :].rearrange("p t k -> p (t k)"), a4).then_inc(attr_in[b], 16)

            for stage in order:
                layer = int(stage == "L2b")

                def store_rows(T, b, h):
                    sp.wait_ge(row_ok, count(stage, T))
                    if stage == final:
                        n = LAST if isinstance(T, int) and T == NT - 1 else P
                        sp.dma_start(out[cols(T, n), :], rowt[0:n, b, :]).then_inc(stored[b], 16)
                    else:
                        sp.dma_start(ROWS[stage][cols(T), :], rowt[:, b, :]).then_inc(stored[b], 16)

                def load_residual(T, b, h):
                    if not early(T):
                        sp.wait_ge(res_ok, count(stage, T - 2, NORM))
                    sp.dma_start(t_x[:, b, :], RESIDUAL[stage][cols(T), :]).then_inc(x_in[b], 16)

                def store_z(T, b, h):
                    sp.wait_ge(z_ok, count(stage, T, REL))
                    sp.dma_start(z_ap(layer, T), t_a[:, b, :]).then_inc(z_out[b], 16)

                def load_z(T, b, h):
                    if not early(T):
                        sp.wait_ge(sum_ok, count(stage, T - 2))
                    sp.dma_start(t_a[:, b, :], z_ap(layer, T)).then_inc(z_in[b], 16)

                if stage == "L1":
                    radial_load(0, 0)
                    radial_load(1, 1)
                    with sp.Fori(0, NG) as g:
                        for q in range(2):
                            sp.wait_ge(h1_sum, 2 * g + q + 1)
                            mark(sp, "sp")
                            sp.wait_ge(stat.onehot, (g + PASS["L1"]) * S + UNIT * (q + 1))
                            mark(sp, "sp")
                            radial_load(2 * g + q + 2, q)
                if stage in REL:
                    if layer:
                        sp.wait_ge(evac_ok, count("L2a", NT - 1))
                    else:
                        sp.wait_ge(turn_ok, count("L1", NT - 1))
                    for to, of in ((relw1, "W1"), (relw2, "W2"), (relv[:], "v"), (relbias[:, 0:1], "bias")):
                        sp.dma_start(to, w_rel[layer][of]).then_inc(relw_in, 16)
                    for c in range(CHUNKS):
                        tiles(sp, [(0, store_z)], CHUNK_T0[c], CHUNK_T0[c + 1])
                    for b in range(2):
                        sp.wait_ge(z_out[b], half_count(stage, b, PER[b] - 1, REL))
                    sp.wait_ge(z_stat, count(stage, NT - 1, REL))
                steps = [(0, load_z)] * (stage in REL)
                if stage in NORM:
                    if stage != "L0b":
                        rows_stored(sp, {"L1": "L0b", "L2b": "L1", "L3c": "L2b"}[stage])
                    steps += [(0, load_residual), (3, store_rows)]
                else:
                    steps += [(2, store_rows)]
                tiles(sp, steps)
            rows_stored(sp, final)

        @block.gpsimd
        def _(pool):
            pool.iota(iota_i[:], [[1, W * R]], channel_multiplier=0)
            pool.iota(arena[:, 17000:17000 + P].bitcast(I32), [[1, P]], channel_multiplier=-1)
            pool.iota(arena[:, 17200:17200 + ETP].bitcast(I32), [[1, ETP]], channel_multiplier=0).then_inc(iotas, 1)

            def gathers(name, sems):
                def body(g, j, i):
                    for s in range(S):
                        if s % 2 == 0:
                            pool.wait_ge(sems.staged, g * (S // 2) + s // 2 + 1)
                            mark(pool, "pool")
                        pool.indirect_dma_start(ring[:, s, :], None, TABLE[name],
                                                bass.IndirectOffsetOnAxis(slot_idx[:, s:s + 1], 0)
                                                ).then_inc(sems.gathered[s], 16)
                return body

            for stage in order:
                def keep(T, b, h):
                    pool.wait_ge(evac_ok, count(stage, T))
                    mark(pool, "pool")
                    if stage == "L0a":
                        for k in range(2):
                            last = pool.tensor_copy(acc3[:, 1 + k, cols(T)], t_y[:, b, k * P:(k + 1) * P])
                        last.then_inc(kept_ok, 1)
                    else:
                        pool.tensor_copy(cur[:, cols(T)], t_y[:, b, 0:P]).then_inc(kept_ok, 1)

                if stage == "feat":
                    continue
                if stage != "L0a":
                    rows_stored(pool, before(stage))
                if stage in REL:
                    pool.wait_ge(setup_done, 1)
                    for c in range(CHUNKS):
                        chunk_groups(pool, int(stage == "L2b"), c, gathers(stage, dyn))
                else:
                    static_groups(pool, stage, gathers(stage, stat))
                if stage in KEEP:
                    tiles(pool, [(0, keep)])

        @block.scalar
        def _(act):
            act.wait_ge(setup_done, 1)

            def stage_idx(sems, g, j, s):
                act.wait_ge(sems.used, g * S + s + 2)
                mark(act, "act")
                a = slice(j + s, j + s + 2) if isinstance(j, int) else bass.ds(j + s, 2)
                nc.scalar.copy(slot_idx[:, s % S:s % S + 2], src_sb[:, a]).then_inc(sems.staged, 1)

            def indices(sems):
                def body(g, j, i):
                    for s in range(0, S, 2):
                        stage_idx(sems, g, j, s)
                return body

            def gelu1(u):
                act.wait_ge(h1_sum, u + 1)
                if not isinstance(u, int) or u > 0:
                    act.wait_ge(h2_sum, u)
                mark(act, "act")
                nc.scalar.activation(h1, ps[0:HID1, H_BANK, :], ACT.Gelu_apprx_tanh,
                                     scale=float(1.0 / np.sqrt(RADIAL))).then_inc(h1_done, 1)

            def gelu2(u, b):
                act.wait_ge(h2_sum, u + 1)
                if not isinstance(u, int) or u > 0:
                    act.wait_ge(rad_sum, (u - 1) * UNIT + 1)
                mark(act, "act")
                nc.scalar.activation(h2[:, b, :], ps[0:HID1, H_BANK, :], ACT.Gelu_apprx_tanh,
                                     scale=float(1.0 / np.sqrt(HID1))).then_inc(h2_done, 1)

            def scale_rad(k, s):
                act.wait_ge(rad_sum, k + 1)
                act.wait_ge(stat.onehot, k + (PASS["L1"] * S - 1))
                mark(act, "act")
                for i in range(3):
                    last = nc.scalar.activation(qs[:, s % 2, i, :, :].rearrange("p a c -> p (a c)"), rad_ps(s)[:, 128:192],
                                                ACT.Copy, scale=ea[:, s // UNIT % 2, s % UNIT, 1 + i:2 + i])
                last.then_inc(scaled, 1)

            def radial(g, j, i):
                for s in range(S):
                    u = i * 2 + s // UNIT
                    if s % UNIT == 0:
                        gelu1(u + 1)
                    if s % UNIT == 1:
                        gelu2(u + 1, (s // UNIT + 1) % 2)
                    if s % 2 == 0 and (s + 6 < S or not (isinstance(i, int) and i == NG - 1)):
                        stage_idx(stat, g, j, s + 6)
                    scale_rad(j + s + 1, (s + 1) % S)

            for stage in order:
                layer = int(stage == "L2b")

                if stage == "L1":
                    for s in range(0, 6, 2):
                        stage_idx(stat, PASS["L1"], 0, s)
                    gelu1(0)
                    gelu2(0, 0)
                    scale_rad(0, 0)
                    static_groups(act, stage, radial, peel_last=True)
                elif stage in REL:
                    def bias_z(T, b, h):
                        act.wait_ge(z_sum, count(stage, T, REL))
                        if not early(T):
                            act.wait_ge(z_out[b], half_count(stage, b, h - 1, REL))
                            act.wait_ge(z_stat, count(stage, T - 2, REL))
                        mark(act, "act")
                        for r in range(R + 1):
                            last = nc.scalar.activation(t_a[:, b, r * D:(r + 1) * D],
                                                        ps_flat[:, 1536 * b + r * D:1536 * b + (r + 1) * D],
                                                        ACT.Identity, bias=relv[:, 0, r:r + 1])
                        last.then_inc(z_ok, 1)

                    act.wait_ge(relw_in, 64 * (layer + 1))
                    if layer:
                        act.wait_ge(sum_ok, count("L2a", NT - 1))
                    for c in range(CHUNKS):
                        chunk_groups(act, layer, c, indices(dyn))
                        tiles(act, [(0, bias_z)], CHUNK_T0[c], CHUNK_T0[c + 1])
                    act.wait_ge(bn_mv, layer + 1)
                    nc.scalar.activation(bn[:, 0, :], zmv[:, :, 1], ACT.Sqrt, bias=eps_c[:]).then_inc(bn_sd, 1)
                    act.wait_ge(bn_ok, layer + 1)
                elif stage != "feat":
                    static_groups(act, stage, indices(stat))

                def relu_z(T, b, h):
                    act.wait_ge(z_in[b], (h + 1 + PER[b] * layer) * 16)
                    mark(act, "act")
                    for r in range(R + 1):
                        last = nc.scalar.activation(t_a[:, b, r * D:(r + 1) * D], t_a[:, b, r * D:(r + 1) * D],
                                                    ACT.Relu, bias=bn[:, 3, r:r + 1], scale=bn[:, 2, r:r + 1])
                    last.then_inc(z_act, 1)

                def evacuate(T, b, h):
                    act.wait_ge(sum_ok, count(stage, T))
                    if stage in PRELU:
                        if not early(T):
                            act.wait_ge(evac_ok, count(stage, T - 2))
                        i = PRELU.index(stage)
                        mark(act, "act")
                        nc.scalar.activation(t_b[:, b, :], ps[:, b, 0:P], ACT.Relu, bias=wsb["L3_b"][:, i:i + 1]
                                             ).then_inc(relu_ok, 1)
                        return
                    if not early(T):
                        act.wait_ge(turn_ok, count(stage, T - 2))
                        if stage in KEEP:
                            act.wait_ge(kept_ok, count(stage, T - 2, KEEP))
                    mark(act, "act")
                    to = t_y[:, b, 0:P]
                    if stage == "L0a":
                        for k in range(2):
                            last = nc.scalar.activation(t_y[:, b, k * P:(k + 1) * P], ps[:, b, k * P:(k + 1) * P], ACT.Relu,
                                                        bias=wsb["L0_b1"][:, k:k + 1])
                        last.then_inc(evac_ok, 1)
                    elif stage in ("feat", "L1"):
                        nc.scalar.copy(to, ps[:, b, 0:P]).then_inc(evac_ok, 1)
                    else:
                        bias = wsb["L0_b2"][:, 0:1] if stage == "L0b" else relbias[:, 1:2]
                        nc.scalar.activation(to, ps[:, b, 0:P], ACT.Relu if stage == "L2a" else ACT.Identity,
                                             bias=bias).then_inc(evac_ok, 1)

                def copy_rows(T, b, h):
                    act.wait_ge(turn_ok, count(stage, T))
                    if ALL.index(stage) or not early(T):
                        act.wait_ge(stored[b], half_count(stage, b, h - 1))
                    mark(act, "act")
                    nc.scalar.copy(rowt[:, b, :], ps[:, 2 + b, 0:P]).then_inc(row_ok, 1)

                def root(T, b, h):
                    act.wait_ge(mv_ok, count(stage, T, NORM))
                    if not early(T):
                        act.wait_ge(rstd_ok, count(stage, T - 2, NORM))
                    mark(act, "act")
                    nc.scalar.activation(sd[:, b, 0:1], mv[:, b, 1:2], ACT.Sqrt, bias=eps_c[:]).then_inc(sd_ok, 1)

                def copy_cur(T, b, h):
                    act.wait_ge(back_ok, count(stage, T, NORM))
                    mark(act, "act")
                    nc.scalar.copy(cur[:, cols(T)], ps[:, 4 + b, 0:P]).then_inc(cur_ok, 1)

                steps = []
                if stage in REL:
                    steps.append((0, relu_z))
                steps.append((1 if stage in REL else 0, evacuate))
                if stage in NORM:
                    lag = 2 if stage in REL else 1
                    steps.append((lag, root))
                    if stage != final:
                        steps.append((lag + 2, copy_cur))
                else:
                    steps.append((2 if stage in REL else 1, copy_rows))
                tiles(act, steps)

        @block.tensor
        def _(pe):
            x_n = pe.alloc_register("pe_extra_windows")
            pe.reg_mov(x_n, 0)
            pe.wait_ge(spread_ok, 1)
            for v in range(2):
                for k in range(2):
                    n = ETP // 2
                    last = pe.matmul(ps[:, 2 * v + k, 0:n], ones[0:TROWS, :],
                                     arena[0:TROWS, 5000 + v * ETP + k * n:5000 + v * ETP + (k + 1) * n],
                                     start=True, stop=True)
            last.then_inc(rows_sum, 1)
            pe.wait_ge(setup_done, 1)
            pe.sem_inc(stat.used, S)
            pe.sem_inc(dyn.used, S)

            def sums(name, to, s, hot):
                if name == "L1":
                    for k in range(3):
                        last = pe.matmul(to[:, k * W:(k + 1) * W], msg[:, s % OH, k * D:(k + 1) * D], hot, start=True, stop=True)
                elif name == "L0a":
                    pe.matmul(to[:, 0:W], ring[:, s, :], hot, start=True, stop=True)
                    last = pe.matmul(to[:, W:2 * W], ones[:], hot, start=True, stop=True)
                else:
                    last = pe.matmul(to, ring[:, s, :], hot, start=True, stop=True)
                return last

            def sum_tile(name, kind, sems, g, j, s):
                width = W * R if name in REL else W
                n = window(pe, kind, j + s)
                windows = pe.snap(n & 255)
                pe.wait_ge(sems.gathered[s], (g + 1) * 16)
                pe.wait_ge(sems.onehot, g * S + s + 1)
                with pe.If(windows > 1):
                    with pe.Fori(1, windows):
                        pe.reg_add(x_n, x_n, 1)
                        pe.wait_ge(x_onehot, pe.snap(x_n))
                        mark(pe, "pe")
                        sums(name, ps[:, X_BANK, 0:sums_shape(name)[0] * width], s, xone[:, 0:width]).then_inc(x_sum, 1)
                pe.wait_ge(sems.added, g * S + s + 1)
                mark(pe, "pe")
                sums(name, ps_tile(name, s), s, onehot[:, s % OH, 0:width]).then_inc(sems.used, 1)

            def sum_group(name, kind, sems):
                def body(g, j, i):
                    for s in range(S):
                        sum_tile(name, kind, sems, g, j, s)
                return body

            def hidden1(u, b, h):
                pe.wait_ge(attr_in[b], (h + 1) * 32)
                if not isinstance(u, int):
                    pe.wait_ge(h2_done, u)
                mark(pe, "pe")
                pe.matmul(ps[0:HID1, H_BANK, :], wsb["mlp1"][:], attr[:, b, :], start=True, stop=True).then_inc(h1_sum, 1)

            def hidden2(u):
                pe.wait_ge(h1_done, u + 1)
                mark(pe, "pe")
                pe.matmul(ps[0:HID1, H_BANK, :], wsb["mlp2"][:], h1, start=True, stop=True).then_inc(h2_sum, 1)

            def radial(k, s, u):
                pe.wait_ge(h2_done, u + 1)
                pe.wait_ge(stat.onehot, k + (PASS["L1"] * S - 1))
                mark(pe, "pe")
                pe.matmul(rad_ps(s), h2[:, s // UNIT % 2, s % UNIT * P:(s % UNIT + 1) * P], wsb["mlp3"][:],
                          start=True, stop=True).then_inc(rad_sum, 1)

            def radial_group(g, j, i):
                for s in range(S):
                    q = s // UNIT
                    if s % UNIT == 0:
                        hidden1(i * 2 + q + 1, (q + 1) % 2, i + (q + 1) // 2)
                    if s % UNIT == 1:
                        hidden2(i * 2 + q + 1)
                    radial(j + s + 1, (s + 1) % S, i * 2 + (s + 1) // UNIT)
                    sum_tile("L1", 0, stat, g, j, s)

            for stage in order:
                layer = int(stage == "L2b")
                if stage == "L1":
                    hidden1(0, 0, 0)
                    hidden2(0)
                    radial(0, 0, 0)
                    static_groups(pe, stage, radial_group)
                    for b in range(2):
                        pe.wait_ge(attr_in[b], 32 * (NG + 1))
                    pe.wait_ge(stat.added, (PASS[stage] + NG) * S + OH)
                elif stage in REL:
                    def z_tile(T, b, h):
                        if not (early(T) and layer == 0):
                            pe.wait_ge(z_ok, count(stage, T - 2, REL))
                        t = T - CHUNK_T0[c]
                        mark(pe, "pe")
                        for r in range(R + 1):
                            if r < R:
                                node = t * (P * R) + r
                                rows = arena[:, node:node + (P - 1) * R + 1:R] if isinstance(t, int) else \
                                    arena[:, bass.ds(t * (P * R), P * R)].rearrange("p (n r) -> p n r", r=R)[:, :, r]
                            else:
                                rows = cur[:, cols(T)]
                            last = pe.matmul(ps_flat[:, 1536 * b + r * D:1536 * b + (r + 1) * D], relw1[:, r, :], rows,
                                             start=True, stop=True)
                        last.then_inc(z_sum, 1)

                    pe.wait_ge(relw_in, 64 * (layer + 1))
                    if not layer:
                        pe.wait_ge(cur_ok, count("L1", NT - 1, NORM))
                    else:
                        pe.wait_ge(kept_ok, count("L2a", NT - 1, KEEP))
                    for c in range(CHUNKS):
                        g1 = chunk_groups(pe, layer, c, sum_group(stage, 1 + c, dyn))
                        pe.wait_ge(dyn.added, g1 * S + OH)
                        mark(pe, "pe")
                        tiles(pe, [(0, z_tile)], CHUNK_T0[c], CHUNK_T0[c + 1])
                    pe.wait_ge(z_ok, count(stage, NT - 1, REL))
                elif stage != "feat":
                    static_groups(pe, stage, sum_group(stage, 0, stat))

                def node_sums(T, b, h):
                    if stage in SAGE:
                        pe.wait_ge(mean_ok, count(stage, T, SAGE))
                    elif stage in REL:
                        pe.wait_ge(z_act, count(stage, T, REL))
                    if not early(T):
                        pe.wait_ge(evac_ok, count(stage, T - 2))
                    mark(pe, "pe")
                    mean, to = t_a[:, b, 0:P], ps[:, b, 0:P]
                    if stage == "L0a":
                        for k in range(2):
                            o = ps[:, b, k * P:(k + 1) * P]
                            pe.matmul(o, wsb["L0_W1l"][:, k * P:(k + 1) * P], mean, start=True, stop=False)
                            last = pe.matmul(o, wsb["L0_W1r"][:, k * P:(k + 1) * P], cur[:, cols(T)], start=False, stop=True)
                        last.then_inc(sum_ok, 1)
                    elif stage == "L0b":
                        pe.matmul(to, ident[:], mean, start=True, stop=False)
                        for k in range(2):
                            last = pe.matmul(to, wsb["L0_W2r"][:, k * P:(k + 1) * P], acc3[:, 1 + k, cols(T)],
                                             start=False, stop=(k == 1))
                        last.then_inc(sum_ok, 1)
                    elif stage == "feat":
                        pe.matmul(to, wsb["F"][:], cur[:, cols(T)], start=True, stop=True).then_inc(sum_ok, 1)
                    elif stage == "L1":
                        pe.matmul(to, wsb["Fself"][:], cur[:, cols(T)], start=True, stop=False)
                        for k in range(3):
                            last = pe.matmul(to, wsb["M"][:, k * D:(k + 1) * D], acc3[:, k, cols(T)], start=False, stop=(k == 2))
                        last.then_inc(sum_ok, 1)
                    elif stage in REL:
                        for r in range(R + 1):
                            last = pe.matmul(to, relw2[:, r, :], t_a[:, b, r * D:(r + 1) * D], start=(r == 0), stop=(r == R))
                        last.then_inc(sum_ok, 1)
                    else:
                        i = PRELU.index(stage)
                        pe.matmul(to, wsb["L3_Wl"][:, i * P:(i + 1) * P], mean, start=True, stop=False)
                        pe.matmul(to, wsb["L3_Wr"][:, i * P:(i + 1) * P], cur[:, cols(T)], start=False, stop=True
                                  ).then_inc(sum_ok, 1)

                def turn(T, b, h):
                    pe.wait_ge(evac_ok, count(stage, T))
                    if not early(T):
                        if stage in NORM:
                            pe.wait_ge(res_ok, count(stage, T - 2, NORM))
                        else:
                            pe.wait_ge(row_ok, count(stage, T - 2))
                    mark(pe, "pe")
                    to = ps[:, 2 + b, 0:P]
                    if stage == "L0a":
                        for k in range(2):
                            last = pe.matmul(to, t_y[:, b, k * P:(k + 1) * P], wsb["L0_W2l"][:, k * P:(k + 1) * P],
                                             start=(k == 0), stop=(k == 1))
                    else:
                        last = pe.transpose(to, t_y[:, b, 0:P], ident[:])
                    last.then_inc(turn_ok, 1)

                def back(T, b, h):
                    pe.wait_ge(row_ok, count(stage, T))
                    if not early(T):
                        pe.wait_ge(cur_ok, count(stage, T - 2, NORM))
                    mark(pe, "pe")
                    pe.transpose(ps[:, 4 + b, 0:P], rowt[:, b, :], ident[:]).then_inc(back_ok, 1)

                if stage == "feat":
                    pe.wait_ge(cur_ok, count("L0b", NT - 1, NORM))
                if before(stage) in KEEP and stage not in REL:
                    pe.wait_ge(kept_ok, count(before(stage), NT - 1, KEEP))
                if stage == "L3a":
                    pe.wait_ge(cur_ok, count("L2b", NT - 1, NORM))
                steps = [(0, node_sums), (1, turn)]
                if stage in NORM and stage != final:
                    steps.append((3, back))
                tiles(pe, steps)

        @block.vector
        def _(dve):
            x_n = dve.alloc_register("dve_extra_windows")
            dve.reg_mov(x_n, 0)
            n_chain = [0]

            def then(ins):
                n_chain[0] += 1
                ins.then_inc(chain, 1)
                dve.wait_ge(chain, n_chain[0])

            V = nc.vector

            dve.wait_ge(loaded, 16 * (5 + len(wsb)))
            dve.wait_ge(iotas, 1)

            def area(at, n=ETP, parts=P, dt=F32):
                return arena[0:parts, at:at + n].bitcast(dt)

            dst_i, et_i, tiles_i = area(0, dt=I32), area(ETP, dt=I32), area(2 * ETP, TPP * P, TROWS, I32)
            tiles_f, far = area(3000, TPP * P, TROWS), area(15000, TPP * P, TROWS)
            spread = [area(5000 + v * ETP, ETP, TROWS) for v in range(2)]
            dst_f, seg_f, low, high = area(7000), area(8000), area(9000), area(10000)
            base, t1, t2, number = area(11000), area(12000), area(14000, dt=I32), area(16100)
            t3 = area(13000)
            V.memset(ones[:], 1.0)
            V.memset(eps_c[:], EPS)
            V.memset(msg, 0.0)
            V.tensor_copy(iota_w[:], iota_i[:])
            V.tensor_copy(number, area(17200, dt=I32))
            V.tensor_copy(dst_f, dst_i)
            V.tensor_copy(tiles_f, tiles_i)
            then(V.tensor_scalar(ident[:], area(17000, P, dt=I32), 0.0, None, ALU.is_equal))
            V.tensor_scalar(far, tiles_f, 0.0, FAR, ALU.is_lt, ALU.mult)
            then(V.scalar_tensor_tensor(seg_f, dst_f, float(R), et_i, ALU.mult, ALU.add))
            then(V.tensor_tensor(far, far, tiles_f, ALU.add))
            per_tile = "p (k e) -> p k e"
            V.tensor_reduce(minmax[0:TROWS, 0, :], far.rearrange(per_tile, k=TPP), AX.X, ALU.min)
            then(V.tensor_reduce(minmax[0:TROWS, 1, :], tiles_f.rearrange(per_tile, k=TPP), AX.X, ALU.max))
            for v in range(2):
                last = V.tensor_tensor(spread[v].rearrange("p (q k) -> p q k", k=TPP),
                                       minmax[0:TROWS, v, :].unsqueeze(1).to_broadcast([TROWS, TROWS, TPP]),
                                       ident[0:TROWS, 0:TROWS].unsqueeze(2).to_broadcast([TROWS, TROWS, TPP]), ALU.mult)
            last.then_inc(spread_ok, 1)
            dve.wait_ge(rows_sum, 1)
            for v, row in enumerate((low, high)):
                for k in range(2):
                    last = V.tensor_copy(row[:, k * (ETP // 2):(k + 1) * (ETP // 2)], ps[:, 2 * v + k, 0:ETP // 2])
            then(last)
            for kind in range(NTYPE):
                c0 = 0 if kind == 0 else CHUNK_T0[kind - 1] * P
                c1 = N if kind == 0 else min(N, CHUNK_T0[kind] * P)
                V.tensor_scalar(base, low, float(c0), float(c1 - 1), ALU.max, ALU.min)
                then(V.tensor_scalar(t1, high, 0.0, float(c1 - 1), ALU.max, ALU.min))
                if kind == 0:
                    V.tensor_tensor(rel_seg[:, 0, :], dst_f, base, ALU.subtract)
                else:
                    V.scalar_tensor_tensor(rel_seg[:, kind, :], base, -float(R), seg_f, ALU.mult, ALU.add)
                then(V.tensor_tensor(t1, t1, base, ALU.subtract))
                then(V.tensor_scalar(t2, t1, 0.0, None, ALU.max))
                then(V.tensor_scalar(t2, t2, 5, None, ALU.arith_shift_right))
                then(V.tensor_scalar(t1, t2, 1.0 - 256.0 * c0, None, ALU.add))
                then(V.scalar_tensor_tensor(win[0:1, kind, :], base[0:1], 256.0, t1[0:1], ALU.mult, ALU.add))
                if kind:
                    then(V.tensor_scalar(t1, low, float(c1), None, ALU.is_lt))
                    then(V.scalar_tensor_tensor(t1, high, float(c0), t1, ALU.is_ge, ALU.mult))
                    then(V.scalar_tensor_tensor(t3, number, 1.0, t1, ALU.add, ALU.mult))
                    then(V.tensor_reduce(ranges[:, 1, kind - 1:kind], t3, AX.X, ALU.max))
                    then(V.tensor_scalar(t3, t1, -FAR, FAR, ALU.mult, ALU.add))
                    then(V.tensor_tensor(t3, t3, number, ALU.add))
                    then(V.tensor_reduce(ranges[:, 0, kind - 1:kind], t3, AX.X, ALU.min))
            then(V.tensor_tensor(ranges[:, 0, :], ranges[:, 0, :], ranges[:, 1, :], ALU.min))
            then(V.tensor_tensor(ranges[:, 2, :], ranges[:, 1, :], ranges[:, 0, :], ALU.subtract))
            then(V.tensor_scalar(ranges_i[:], ranges[:, 2, :], 1.0, float(S - 1), ALU.max, ALU.add))
            then(V.tensor_scalar(ranges_i[:], ranges_i[:], 3, None, ALU.arith_shift_right))
            then(V.tensor_copy(ranges[:, 2, :], ranges_i[:]))
            V.memset(ptab_f[:, 0:1], 0.0)
            for k in range(2 * CHUNKS):
                c = k % CHUNKS
                if k:
                    then(V.tensor_copy(ptab_f[:, 3 * k:3 * k + 1], ptab_f[:, 3 * k - 2:3 * k - 1]))
                then(V.tensor_copy(ptab_f[:, 3 * k + 2:3 * k + 3], ranges[:, 0, c:c + 1]))
                then(V.tensor_tensor(ptab_f[:, 3 * k + 1:3 * k + 2], ptab_f[:, 3 * k:3 * k + 1], ranges[:, 2, c:c + 1], ALU.add))
            V.tensor_copy(ptab[:], ptab_f[:])
            V.tensor_scalar(wsb["F"][:], wsb["F"][:], INV_MUL, None, ALU.mult)
            V.tensor_scalar(wsb["Fself"][:], wsb["Fself"][:], COS * INV_MUL, None, ALU.mult)
            V.tensor_scalar(wsb["M"][:, 0:D], wsb["M"][:, 0:D], CONV, None, ALU.mult)
            V.tensor_scalar(wsb["M"][0:96, D:2 * D], wsb["M"][0:96, D:2 * D], CONV, None, ALU.mult)
            V.tensor_scalar(wsb["M"][96:128, D:2 * D], wsb["M"][96:128, D:2 * D], CONV_DOT, None, ALU.mult)
            then(V.tensor_scalar(wsb["M"][:, 2 * D:3 * D], wsb["M"][:, 2 * D:3 * D], CONV_DOT, None, ALU.mult))
            dve.sem_inc(stat.added, OH)
            dve.sem_inc(dyn.added, OH)
            dve.sem_inc(setup_done, 1)

            def hot(to, name, seg):
                V.tensor_scalar(to, iota_w[:, 0:(W * R if name in REL else W)], seg, None, ALU.is_equal)

            def build_tile(name, kind, sems, g, j, s):
                width = W * R if name in REL else W
                dve.wait_ge(sems.used, g * S + s + 1 + S - OH)
                to = onehot[:, s % OH, 0:width]
                ins = V.tensor_scalar(to, iota_w[:, 0:width], rel_seg[:, kind, bass.ds(j + s, 1)], None, ALU.is_equal)
                if name == "L1":
                    dve.wait_ge(sems.gathered[s], (g + 1) * 16)
                    dve.wait_ge(scaled, j + s + 1)
                    m, rad = msg[:, s % OH, :], rad_ps(s)
                    V.scalar_tensor_tensor(m[:, 0:D], rad[:, 0:D], ea[:, s // UNIT % 2, s % UNIT, 0:1], ring[:, s, :],
                                           ALU.mult, ALU.mult)
                    V.tensor_tensor(m[:, D:D + 3 * MUL].rearrange("p (i c) -> p i c", i=3), qs[:, s % 2, :, 0, :],
                                    ring[:, s, 0:MUL].unsqueeze(1).to_broadcast([P, 3, MUL]), ALU.mult)
                    ins = V.tensor_tensor(m[:, D + 3 * MUL:D + 6 * MUL].rearrange("p (i c) -> p i c", i=3), qs[:, s % 2, :, 1, :],
                                          ring[:, s, MUL:4 * MUL].rearrange("p (i c) -> p i c", i=3), ALU.mult)
                ins.then_inc(sems.onehot, 1)
                v = window(dve, kind, j + s)
                top = (NT if name not in REL else CHUNK_TILES[kind - 1]) * P - 1
                node = dve.snap(v >> 8).with_bounds(min_val=0, max_val=top)
                windows = dve.snap(v & 255)
                with dve.If(windows > 1):
                    dve.drain()
                    V.tensor_copy(xseg[:], rel_seg[:, kind, bass.ds(j + s, 1)])
                    with dve.Fori(1, windows) as i:
                        dve.drain()
                        V.tensor_scalar(xseg[:], xseg[:], -float(width), None, ALU.add)
                        dve.drain()
                        V.tensor_scalar(xone[:, 0:width], iota_w[:, 0:width], xseg[:], None, ALU.is_equal).then_inc(x_onehot, 1)
                        dve.reg_add(x_n, x_n, 1)
                        dve.wait_ge(x_sum, dve.snap(x_n))
                        mark(dve, "dve")
                        to = acc_at(name, dve.snap(node + i * W).with_bounds(min_val=0, max_val=top))
                        n = sums_shape(name)[0] * width
                        V.tensor_tensor(to, to, shaped(name, ps[:, X_BANK, 0:n]), ALU.add)
                    dve.drain()
                return node

            def add_tile(name, sems, g, s, node):
                dve.wait_ge(sems.used, g * S + s + 1 + S)
                dve.wait_ge(sems.added, g * S + s + OH)
                to = acc_at(name, node)
                V.tensor_tensor(to, to, shaped(name, ps_tile(name, s)), ALU.add).then_inc(sems.added, 1)

            def pass_group(name, kind, sems):
                def body(g, j, i):
                    nodes = [build_tile(name, kind, sems, g, j, 0)]
                    for s in range(S):
                        if s + 1 < S:
                            nodes.append(build_tile(name, kind, sems, g, j, s + 1))
                        add_tile(name, sems, g, s, nodes[s])
                return body

            for stage in order:
                layer = int(stage == "L2b")
                if stage != "L0a":
                    dve.wait_ge(turn_ok, count(before(stage), NT - 1))
                if stage in REL:
                    def z_stats(T, b, h):
                        dve.wait_ge(z_ok, count(stage, T, REL))
                        n = LAST if isinstance(T, int) and T == NT - 1 else P
                        mark(dve, "dve")
                        for r in range(R + 1):
                            to = zst[:, T, r, :] if isinstance(T, int) else \
                                zst[:, bass.ds(T, 1), r, :].rearrange("p a c -> p (a c)")
                            last = V.bn_stats(to, t_a[:, b, r * D:r * D + n])
                        last.then_inc(z_stat, 1)

                    for c in range(CHUNKS):
                        if c:
                            dve.wait_ge(z_sum, count(stage, CHUNK_T0[c] - 1, REL))
                        then(V.memset(arena[:, 0:(CHUNK_TILES[c] * P + W) * R], 0.0))
                        chunk_groups(dve, layer, c, pass_group(stage, 1 + c, dyn))
                        tiles(dve, [(0, z_stats)], CHUNK_T0[c], CHUNK_T0[c + 1])
                    dve.wait_ge(z_stat, count(stage, NT - 1, REL))
                    dve.wait_ge(relw_in, 64 * (layer + 1))
                    for r in range(R + 1):
                        last = V.bn_aggr(zmv[:, r, :], zst[:, :, r, :])
                    last.then_inc(bn_mv, 1)
                    then(V.tensor_reduce(relbias[:, 1:2], relv[:, 3, :], AX.X, ALU.add))
                    then(V.tensor_tensor(relbias[:, 1:2], relbias[:, 1:2], relbias[:, 0:1], ALU.add))
                    dve.wait_ge(bn_sd, layer + 1)
                    then(V.reciprocal(bn[:, 1, :], bn[:, 0, :]))
                    then(V.tensor_tensor(bn[:, 2, :], relv[:, 1, :], bn[:, 1, :], ALU.mult))
                    then(V.tensor_tensor(bn[:, 3, :], zmv[:, :, 0], bn[:, 2, :], ALU.mult))
                    V.tensor_tensor(bn[:, 3, :], relv[:, 2, :], bn[:, 3, :], ALU.subtract).then_inc(bn_ok, 1)
                elif stage != "feat":
                    then(V.memset(arena[:, 0:PASS_BLOCKS[stage] * ACCW], 0.0))
                    static_groups(dve, stage, pass_group(stage, 0, stat))
                    dve.wait_ge(stat.added, (PASS[stage] + NG) * S + OH)
                    if stage == "L0a":
                        then(V.tensor_scalar(rdeg[:], acc3[:, 1, 0:NP], 1.0, None, ALU.max))
                        then(V.reciprocal(rdeg[:], rdeg[:]))

                def mean(T, b, h):
                    if not early(T):
                        dve.wait_ge(sum_ok, count(stage, T - 2))
                    V.tensor_tensor(t_a[:, b, 0:P], acc3[:, 0, cols(T)], rdeg[:, cols(T)], ALU.mult).then_inc(mean_ok, 1)

                def prelu(T, b, h):
                    i = PRELU.index(stage)
                    dve.wait_ge(relu_ok, count(stage, T, PRELU))
                    if not early(T):
                        dve.wait_ge(evac_ok, count(stage, T - 2))
                    V.tensor_scalar(t_m[:, b, :], ps[:, b, 0:P], wsb["L3_b"][:, i:i + 1], 0.0, ALU.add, ALU.min).then_inc(min_ok, 1)
                    dve.wait_ge(min_ok, count(stage, T, PRELU))
                    if not early(T):
                        dve.wait_ge(turn_ok, count(stage, T - 2))
                        if stage in KEEP:
                            dve.wait_ge(kept_ok, count(stage, T - 2, KEEP))
                    V.scalar_tensor_tensor(t_y[:, b, 0:P], t_m[:, b, :], wsb["prelu_w"][:, 0:1], t_b[:, b, :], ALU.mult, ALU.add).then_inc(evac_ok, 1)

                def norm_stats(T, b, h):
                    dve.wait_ge(turn_ok, count(stage, T))
                    dve.wait_ge(x_in[b], half_count(stage, b, h, NORM))
                    if not early(T):
                        dve.wait_ge(row_ok, count(stage, T - 2))
                    V.tensor_tensor(t_n[:, b, :], ps[:, 2 + b, 0:P], t_x[:, b, :], ALU.add).then_inc(res_ok, 1)
                    dve.wait_ge(res_ok, count(stage, T, NORM))
                    V.bn_stats(st6[:, b, :], t_n[:, b, :]).then_inc(lnst_ok, 1)
                    dve.wait_ge(lnst_ok, count(stage, T, NORM))
                    mark(dve, "dve")
                    V.bn_aggr(mv[:, b, :], st6[:, b, :]).then_inc(mv_ok, 1)

                def normalise(T, b, h):
                    dve.wait_ge(sd_ok, count(stage, T, NORM))
                    V.reciprocal(sd[:, b, 1:2], sd[:, b, 0:1]).then_inc(rstd_ok, 1)
                    dve.wait_ge(rstd_ok, count(stage, T, NORM))
                    dve.wait_ge(stored[b], half_count(stage, b, h - 1))
                    if stage != final and not early(T):
                        dve.wait_ge(back_ok, count(stage, T - 2, NORM))
                    V.tensor_scalar(rowt[:, b, :], t_n[:, b, :], mv[:, b, 0:1], sd[:, b, 1:2],
                                    ALU.subtract, ALU.mult).then_inc(row_ok, 1)

                steps = []
                if stage in SAGE:
                    steps.append((0, mean))
                if stage in PRELU:
                    steps.append((1, prelu))
                if stage in NORM:
                    steps += [(1, norm_stats), (2, normalise)]
                if steps:
                    tiles(dve, steps)


def lay_out(inputs, n_layers):
    def edge_tiles(a):
        return a.reshape(ETP, P).T

    def padded(a, rows, fill=0):
        full = np.full((rows,) + a.shape[1:], fill, a.dtype)
        full[:a.shape[0]] = a
        return full

    a = {k: np.asarray(v) for k, v in inputs.items()}
    EP = ETP * P
    x = padded(a["x"], NP)
    dst = padded(a["dst"], EP, -1)
    arrays = {
        "x": x, "x_t": x.T,
        "src": edge_tiles(padded(a["src"], EP)),
        "dst": edge_tiles(dst), "dst_tiles": dst.reshape(TROWS, TPP * P),
        "etype": edge_tiles(padded(a["edge_type_8"], EP)),
        "ea4": padded(a["edge_attr_4"], EP).reshape(ETP, P, 4).transpose(1, 0, 2).reshape(P, ETP * 4),
        "ea8": padded(a["edge_attr_8"], EP).T,
    }

    def halves(m):
        return m.reshape(2, P, m.shape[1]).transpose(1, 0, 2).reshape(P, -1)

    w00, w01, w10, w11 = (a["L1_gnn_Wp_" + k] for k in ("00", "01", "10", "11"))
    w0, w1 = a["L1_gnn_W1_0e"], a["L1_gnn_W1_1o"]
    c0, c1 = a["L1_gnn_W2_0e"], a["L1_gnn_W2_1o"]
    F, Fself = np.zeros((D, D), np.float32), np.zeros((D, D), np.float32)
    F[:MUL, :MUL], Fself[:MUL, :MUL] = w0[:, :MUL], w0[:, MUL:]
    M = np.zeros((D, 3 * D), np.float32)
    M[:MUL, :MUL] = c0[:MUL]
    for i in range(3):
        b = MUL + MUL * i
        F[MUL + i::3, b:b + MUL] = w1[:, :MUL]
        Fself[MUL + i::3, MUL + i::3] = w1[:, MUL:]
        M[b:b + MUL, MUL + i:D:3] = c1[MUL:]
        M[MUL * i:MUL * (i + 1), D + MUL + i:2 * D:3] = c1[:MUL]
    M[96:128, D:D + MUL] = c0[MUL:]
    M[0:32, 2 * D:2 * D + MUL] = c0[MUL:]
    M[32:64, 2 * D:2 * D + MUL] = c0[MUL:]
    weights = {
        "L0_W1l": a["L0_gnn_W1_l"].T, "L0_W1r": a["L0_gnn_W1_r"].T,
        "L0_b1": a["L0_gnn_b1"].reshape(2, P).T, "L0_b2": a["L0_gnn_b2"].reshape(P, 1),
        "L0_W2l": halves(a["L0_gnn_W2_l"].T), "L0_W2r": halves(a["L0_gnn_W2_r"].T),
        "F": F, "Fself": Fself, "M": M, "mlp1": a["L1_gnn_W_mlp1"], "mlp2": a["L1_gnn_W_mlp2"],
        "mlp3": np.concatenate([w00, w10, w10, w10, w01, w11], axis=1),
        "L3_Wl": np.concatenate([a[f"L3_gnn_W{i}l"].T for i in (1, 2, 3)], axis=1),
        "L3_Wr": np.concatenate([a[f"L3_gnn_W{i}r"].T for i in (1, 2, 3)], axis=1),
        "L3_b": np.stack([a[f"L3_gnn_b{i}"] for i in (1, 2, 3)], axis=1),
        "prelu_w": np.broadcast_to(a["L3_gnn_prelu_w"].reshape(1, 1), (P, 1)),
    }
    rel = []
    for i in range(2):
        p = f"L2_gnn_l{i}_"
        rel.append({
            "W1": a[p + "W1"].transpose(1, 0, 2), "W2": a[p + "W2"].transpose(1, 0, 2),
            "v": np.stack([a[p + k].T for k in ("b1", "gamma", "beta", "b2")], axis=1),
            "bias": a[p + "bias"].reshape(P, 1),
        })
    return arrays, weights, rel


LAYERS = 4


def kernel(**inputs):
    import concourse.bacc as _bacc
    from concourse.bass_utils import run_bass_kernel_spmd as _run

    nc = _bacc.Bacc("TRN2", target_bir_lowering=False, num_devices=1, dynamic_dma_scratch_size=8192)
    arrays, weights, rel = lay_out(inputs, LAYERS)
    feeds = {}

    def feed(name, a):
        a = np.ascontiguousarray(a)
        feeds[f"in_{name}_dram"] = a
        return nc.dram_tensor(f"in_{name}_dram", a.shape, mybir.dt.from_np(a.dtype), kind="ExternalInput").ap()

    args = [feed(k, arrays[k]) for k in ("x", "x_t", "src", "dst", "dst_tiles", "etype", "ea4", "ea8")]
    w = {k: feed("w_" + k, a) for k, a in weights.items()}
    w_rel = [{k: feed(f"rel{i}_{k}", a) for k, a in rel[i].items()} for i in range(2)]
    out = nc.dram_tensor("out_0_dram", (N, D), F32, kind="ExternalOutput").ap()
    build(nc, *args, w, w_rel, out, LAYERS)
    r = _run(nc, [feeds], core_ids=[0])
    return r.results[0]["out_0_dram"]
```

```python
from contextlib import ExitStack

import numpy as np

import concourse.bass as bass
from concourse import mybir

ALU = mybir.AluOpType
ACT = mybir.ActivationFunctionType
AX = mybir.AxisListType
F32 = mybir.dt.float32
I32 = mybir.dt.int32

P = 128
N, E, D = 6250, 106250, 128
R = 8
NT = -(-N // P)
NP = NT * P
LAST = N - (NT - 1) * P
UNIT = 4
G = 4
S = G * UNIT
ET = -(-E // P)
NG = -(-ET // S)
UPP = 2
TROWS = -(-(NG + 1) * G // UPP)
NU = TROWS * UPP
ETP = NU * UNIT
W = 36
W_RECIP = 65536 // W + 1
ACCW = NP + W
CHUNK_TILES = [17, 16, 16]
CHUNK_T0 = [0, 17, 33, 49]
CHUNKS = len(CHUNK_TILES)
MUL, RADIAL, HID1 = 32, 8, 64
FAR = 32768.0
EPS = 1e-5

assert N * W_RECIP < 2 ** 24 and NG * G + 4 <= NU
assert CHUNK_T0[-1] == NT and (max(CHUNK_TILES) * P + W) * R <= 3 * ACCW

INV_MUL = float(1.0 / np.sqrt(MUL))
COS, SIN = float(np.cos(np.pi / 8.0)), float(np.sin(np.pi / 8.0))
CONV = SIN / float(np.sqrt(2 * MUL) * np.sqrt(32.0) * np.sqrt(2.0))
CONV_DOT = CONV / float(np.sqrt(3.0))


def build(nc, x, x_t, src, dst, dst_tiles, etype, ea4, ea8, w, w_rel, out, layers):
    with ExitStack() as ctx:
        def sb(name, shape, dt=F32):
            return ctx.enter_context(nc.sbuf_tensor(name, shape, dt))

        def sem(name):
            return ctx.enter_context(nc.semaphore(name))

        def table(name):
            return nc.dram_tensor(name, [NP, D], F32, kind="Internal").ap()

        tab_hid = table("tab_hid")
        tab_x1 = table("tab_x1")
        tab_feat = table("tab_feat")
        tab_x2 = table("tab_x2")
        tab_h2 = table("tab_h2")
        tab_x3 = table("tab_x3")
        tab_h3 = [table("tab_h3a"), table("tab_h3b")]
        z_dram = nc.dram_tensor("z_dram", [2, NT, P, (R + 1) * D], F32, kind="Internal").ap()

        arena = sb("arena", [P, 3 * ACCW])
        acc3 = arena[:].rearrange("p (k c) -> p k c", k=3)
        cur = sb("cur", [P, NP])
        rdeg = sb("rdeg", [P, NP])
        src_sb = sb("src_sb", [P, ETP], I32)
        NTYPE = 1 + CHUNKS
        rel_seg = sb("rel_seg", [P, NTYPE, ETP])
        win = sb("win", [1, NTYPE, NU], I32)
        ptab = sb("ptab", [P, 6 * CHUNKS], I32)
        ring = sb("ring", [P, S, D])
        slot_idx = sb("slot_idx", [P, S], I32)
        onehot = sb("onehot", [P, 2, UNIT, W * R])
        share = sb("share", [P, 2 * (R + 1) * D + NT * (R + 1) * 6])
        HALF = UNIT // 2 * P
        msg = share[:, 0:2 * UNIT * 2 * D].rearrange("p (b t c) -> p b t c", b=2, t=UNIT)
        dots = share[:, 2048:2048 + UNIT * 3 * MUL].rearrange("p (t i c) -> p t i c", t=UNIT, i=3)
        h1 = share[:, 3072:3072 + HALF]
        h2 = share[:, 3328:3328 + 2 * HALF].rearrange("p (b c) -> p b c", b=2)
        attr = share[0:2 * RADIAL, 3840:3840 + G * HALF].rearrange("p (b c) -> p b c", b=G)
        relw1 = share[:, 0:(R + 1) * D].rearrange("p (r c) -> p r c", c=D)
        relw2 = share[:, (R + 1) * D:2 * (R + 1) * D].rearrange("p (r c) -> p r c", c=D)
        zst = share[:, 2 * (R + 1) * D:].rearrange("p (t r k) -> p t r k", t=NT, k=6)
        xone = sb("xone", [P, W * R])
        xseg = sb("xseg", [P, 1])
        ident = sb("ident", [P, P])
        ones = sb("ones", [P, P])
        minmax = sb("minmax", [P, 2, UPP])
        iota_w = sb("iota_w", [P, W * R])
        iota_i = arena[:, 18500:18500 + W * R].bitcast(I32)
        ea = sb("ea", [P, G, UNIT, 4])
        t_a = sb("t_a", [P, 2, (R + 1) * D])
        qs = t_a[:].rearrange("p b c -> p (b c)")[:, 0:2 * UNIT * 8 * MUL].rearrange(
            "p (b t i a c) -> p b t i a c", b=2, t=UNIT, i=4, a=2)
        t_b = sb("t_b", [P, 2, D])
        t_x = sb("t_x", [P, 2, D])
        t_y = sb("t_y", [P, 2, 2 * D])
        t_m = sb("t_m", [P, 2, D])
        t_n = sb("t_n", [P, 2, D])
        rowt = sb("rowt", [P, 2, D])
        st6 = sb("st6", [P, 2, 6])
        mv = sb("mv", [P, 2, 2])
        sd = sb("sd", [P, 2, 2])
        zmv = sb("zmv", [P, R + 1, 2])
        bn = sb("bn", [P, 4, R + 1])
        eps_c = sb("eps_c", [P, 1])
        ranges = sb("ranges", [P, 3, CHUNKS])
        ranges_i = sb("ranges_i", [P, CHUNKS], I32)
        ptab_f = sb("ptab_f", [P, 6 * CHUNKS])
        wsb = {k: sb("w_" + k, list(a.shape)) for k, a in w.items()}
        relv = sb("relv", [P, 4, R + 1])
        relbias = sb("relbias", [P, 2])
        ps = ctx.enter_context(nc.psum_tensor("ps", [P, 8, 512], F32))

        loaded, setup_done = sem("loaded"), sem("setup_done")
        iotas, ident_ok, minmax_ok, spread_ok, rows_sum = sem("iotas"), sem("ident_ok"), sem("minmax_ok"), sem("spread_ok"), sem("rows_sum")
        fence = {e: sem("fence_" + e) for e in ("pool", "act", "pe", "dve", "sp")}

        class PassSems:
            def __init__(self, tag):
                self.gathered = [sem(f"gathered{tag}{q}") for q in range(G)]
                self.staged = sem(f"staged{tag}")
                self.onehot = sem(f"onehot{tag}")
                self.used = sem(f"used{tag}")
                self.added = sem(f"added{tag}")

        stat, dyn = PassSems("_s"), PassSems("_d")
        acc_zero = sem("acc_zero")
        x_onehot, x_sum = sem("x_onehot"), sem("x_sum")
        attr_in = [sem(f"attr_in{q}") for q in range(G)]
        h1_sum, h1_done, h2_sum, h2_done = sem("h1_sum"), sem("h1_done"), sem("h2_sum"), sem("h2_done")
        rad_sum, scaled, dots_ok = sem("rad_sum"), sem("scaled"), sem("dots_ok")
        mean_ok, sum_ok, relu_ok, min_ok, evac_ok = sem("mean_ok"), sem("sum_ok"), sem("relu_ok"), sem("min_ok"), sem("evac_ok")
        turn_ok, row_ok, kept_ok = sem("turn_ok"), sem("row_ok"), sem("kept_ok")
        stored = [sem("stored0"), sem("stored1")]
        x_in = [sem("x_in0"), sem("x_in1")]
        res_ok, lnst_ok, mv_ok, sd_ok, rstd_ok = sem("res_ok"), sem("lnst_ok"), sem("mv_ok"), sem("sd_ok"), sem("rstd_ok")
        back_ok, cur_ok = sem("back_ok"), sem("cur_ok")
        z_sum, z_ok, z_stat, z_act = sem("z_sum"), sem("z_ok"), sem("z_stat"), sem("z_act")
        z_out = [sem("z_out0"), sem("z_out1")]
        z_in = [sem("z_in0"), sem("z_in1")]
        relw_in, bn_mv, bn_sd, bn_ok = sem("relw_in"), sem("bn_mv"), sem("bn_sd"), sem("bn_ok")
        chain = sem("chain")

        ALL = ["L0a", "L0b", "feat", "L1", "L2a", "L2b", "L3a", "L3b", "L3c"]
        order = ALL[:[0, 2, 4, 6, 9][layers]]
        final = order[-1]
        SAGE = ["L0a", "L0b", "L3a", "L3b", "L3c"]
        KEEP = ["L0a", "L2a", "L3a", "L3b"]
        PRELU = ["L3a", "L3b", "L3c"]
        NORM = ["L0b", "L1", "L2b", "L3c"]
        REL = ["L2a", "L2b"]
        PASS = {"L0a": 0, "L0b": NG, "L1": 2 * NG, "L3a": 3 * NG, "L3b": 4 * NG, "L3c": 5 * NG}
        PASS_BLOCKS = {"L0a": 2, "L0b": 1, "L1": 2, "L3a": 1, "L3b": 1, "L3c": 1}
        TABLE = {"L0a": x, "L0b": tab_hid, "L1": tab_feat, "L2a": tab_x2, "L2b": tab_h2,
                 "L3a": tab_x3, "L3b": tab_h3[0], "L3c": tab_h3[1]}
        ROWS = {"L0a": tab_hid, "L0b": tab_x1, "feat": tab_feat, "L1": tab_x2, "L2a": tab_h2,
                "L2b": tab_x3, "L3a": tab_h3[0], "L3b": tab_h3[1], "L3c": None}
        RESIDUAL = {"L0b": x, "L1": tab_x1, "L2b": tab_x2, "L3c": tab_x3}
        PER = [(NT + 1) // 2, NT // 2]

        def count(stage, T, of=ALL):
            return NT * of.index(stage) + T + 1

        def half_count(stage, b, h, of=ALL):
            return 16 * (PER[b] * of.index(stage) + h + 1)

        def before(stage):
            return ALL[ALL.index(stage) - 1]

        def cols(T, n=P):
            return slice(T * P, T * P + n) if isinstance(T, int) else bass.ds(T * P, n)

        def early(T):
            return isinstance(T, int) and T < 2

        def mark(eng, name):
            eng.sem_inc(fence[name], 1)

        def tiles(eng, steps, T0=0, T1=NT):
            lags = max(lag for lag, _ in steps)

            def at(T, i):
                for lag, step in steps:
                    t = T - lag
                    if i is not None:
                        step(i * 2 + t, t % 2, i + t // 2)
                    elif T0 <= t < T1:
                        step(t, t % 2, t // 2)

            first = T0 + 2 + lags
            pairs = (T1 - 1 - first) // 2
            for T in range(T0, first):
                at(T, None)
            with eng.Fori(0, pairs) as i:
                at(first, i)
                at(first + 1, i)
            for T in range(first + 2 * pairs, T1 + lags):
                at(T, None)

        def rows_stored(eng, stage):
            for b in range(2):
                eng.wait_ge(stored[b], half_count(stage, b, PER[b] - 1))

        def chunk_values(eng, layer, c):
            k = 3 * (layer * CHUNKS + c)
            g0 = eng.value_load(ptab[0:1, k:k + 1], min_val=0, max_val=6 * NG)
            g1 = eng.value_load(ptab[0:1, k + 1:k + 2], min_val=0, max_val=6 * NG)
            u0 = eng.value_load(ptab[0:1, k + 2:k + 3], min_val=0, max_val=NU - G)
            return g0, g1, u0

        def static_groups(eng, name, body, peel_last=False):
            g0 = PASS[name]
            with eng.Fori(0, NG - peel_last) as i:
                body(i + g0, i * G, False)
            if peel_last:
                body(g0 + NG - 1, (NG - 1) * G, True)

        def chunk_groups(eng, layer, c, body, peel_last=False):
            g0, g1, u0 = chunk_values(eng, layer, c)
            end = g1 if peel_last else eng.snap(g1 + 1)
            with eng.Fori(g0, end) as g:
                body(g, eng.snap((g - g0) * G + u0).with_bounds(min_val=0, max_val=NU - (2 if peel_last else 1) * G), False)
            if peel_last:
                body(g1, eng.snap((g1 - g0) * G + u0).with_bounds(min_val=0, max_val=NU - G), True)
            return g1

        def window(eng, kind, u):
            return eng.value_load(win[0:1, kind, u:u + 1] if isinstance(u, int) else win[0:1, kind, bass.ds(u, 1)],
                                  min_val=0, max_val=(NP << 8) + 255)

        ps_flat = ps[:].rearrange("p b c -> p (b c)")
        X_BANK, H_BANK = 7, 4
        RAD_BANKS = (5, 6)

        def sums_shape(name):
            return (1, W * R) if name in REL else (PASS_BLOCKS[name], W)

        def bank(name, q):
            blocks, width = sums_shape(name)
            return ps[:, q, 0:blocks * width]

        def rad_ps(b, t):
            at = (t % 2 * 2 + t // 2) * 4 * MUL
            return ps[:, RAD_BANKS[b], at:at + 4 * MUL]

        def acc_at(name, node):
            if name in REL:
                return arena[:, bass.ds(node * R, W * R)]
            return acc3[:, 0:PASS_BLOCKS[name], bass.ds(node, W)]

        def shaped(name, ap):
            if name in REL:
                return ap
            return ap.rearrange("p (k c) -> p k c", k=PASS_BLOCKS[name])

        block = ctx.enter_context(nc.Block())

        @block.sync
        def _(sp):
            for to, of in [(src_sb[:], src), (arena[:, 0:ETP].bitcast(I32), dst),
                           (arena[:, ETP:2 * ETP].bitcast(I32), etype),
                           (arena[0:TROWS, 2 * ETP:2 * ETP + UPP * UNIT * P].bitcast(I32), dst_tiles),
                           (cur[:], x_t), *((wsb[k][:], w[k]) for k in wsb)]:
                sp.dma_start(to, of).then_inc(loaded, 16)

            def z_ap(layer, T):
                if isinstance(T, int):
                    return z_dram[layer, T, :, :]
                return z_dram[layer, bass.ds(T, 1), :, :].rearrange("a p c -> (a p) c")

            def radial_load(u, q):
                if isinstance(u, int):
                    a8, a4 = ea8[:, u * HALF:(u + 1) * HALF], ea4[:, u * UNIT * 4:(u + 1) * UNIT * 4]
                else:
                    a8, a4 = ea8[:, bass.ds(u * HALF, HALF)], ea4[:, bass.ds(u * (UNIT * 4), UNIT * 4)]
                sp.dma_start(attr[:, q, :], a8).then_inc(attr_in[q], 16)
                sp.dma_start(ea[:, q, :, :].rearrange("p t k -> p (t k)"), a4).then_inc(attr_in[q], 16)

            for stage in order:
                layer = int(stage == "L2b")

                def store_rows(T, b, h):
                    sp.wait_ge(row_ok, count(stage, T))
                    if stage == final:
                        n = LAST if isinstance(T, int) and T == NT - 1 else P
                        sp.dma_start(out[cols(T, n), :], rowt[0:n, b, :]).then_inc(stored[b], 16)
                    else:
                        sp.dma_start(ROWS[stage][cols(T), :], rowt[:, b, :]).then_inc(stored[b], 16)

                def load_residual(T, b, h):
                    if not early(T):
                        sp.wait_ge(res_ok, count(stage, T - 2, NORM))
                    sp.dma_start(t_x[:, b, :], RESIDUAL[stage][cols(T), :]).then_inc(x_in[b], 16)

                def store_z(T, b, h):
                    sp.wait_ge(z_ok, count(stage, T, REL))
                    sp.dma_start(z_ap(layer, T), t_a[:, b, :]).then_inc(z_out[b], 16)

                def load_z(T, b, h):
                    if not early(T):
                        sp.wait_ge(sum_ok, count(stage, T - 2))
                    sp.dma_start(t_a[:, b, :], z_ap(layer, T)).then_inc(z_in[b], 16)

                if stage == "L1":
                    for q in range(G):
                        radial_load(q, q)
                    with sp.Fori(0, NG) as g:
                        for q in range(G):
                            sp.wait_ge(h1_sum, G * g + q + 1)
                            mark(sp, "sp")
                            sp.wait_ge(stat.onehot, (g + PASS["L1"]) * G + q + 1)
                            mark(sp, "sp")
                            radial_load(G * g + q + G, q)
                if stage in REL:
                    if layer:
                        sp.wait_ge(evac_ok, count("L2a", NT - 1))
                    else:
                        sp.wait_ge(turn_ok, count("L1", NT - 1))
                    for to, of in ((relw1, "W1"), (relw2, "W2"), (relv[:], "v"), (relbias[:, 0:1], "bias")):
                        sp.dma_start(to, w_rel[layer][of]).then_inc(relw_in, 16)
                    for c in range(CHUNKS):
                        tiles(sp, [(0, store_z)], CHUNK_T0[c], CHUNK_T0[c + 1])
                    for b in range(2):
                        sp.wait_ge(z_out[b], half_count(stage, b, PER[b] - 1, REL))
                    sp.wait_ge(z_stat, count(stage, NT - 1, REL))
                steps = [(0, load_z)] * (stage in REL)
                if stage in NORM:
                    if stage != "L0b":
                        rows_stored(sp, {"L1": "L0b", "L2b": "L1", "L3c": "L2b"}[stage])
                    steps += [(0, load_residual), (3, store_rows)]
                else:
                    steps += [(2, store_rows)]
                tiles(sp, steps)
            rows_stored(sp, final)

        @block.gpsimd
        def _(pool):
            pool.iota(iota_i, [[1, W * R]], channel_multiplier=0)
            pool.iota(arena[:, 17000:17000 + P].bitcast(I32), [[1, P]], channel_multiplier=-1)
            pool.iota(arena[:, 17200:17200 + NU].bitcast(I32), [[1, NU]], channel_multiplier=0).then_inc(iotas, 1)

            def gathers(name, sems):
                def body(g, u, last):
                    for q in range(G):
                        pool.wait_ge(sems.staged, g * G + q + 1)
                        mark(pool, "pool")
                        for s in range(q * UNIT, (q + 1) * UNIT):
                            pool.indirect_dma_start(ring[:, s, :], None, TABLE[name],
                                                    bass.IndirectOffsetOnAxis(slot_idx[:, s:s + 1], 0)
                                                    ).then_inc(sems.gathered[q], 16)
                return body

            for stage in order:
                def keep(T, b, h):
                    pool.wait_ge(evac_ok, count(stage, T))
                    mark(pool, "pool")
                    if stage == "L0a":
                        for k in range(2):
                            last = pool.tensor_copy(acc3[:, 1 + k, cols(T)], t_y[:, b, k * P:(k + 1) * P])
                        last.then_inc(kept_ok, 1)
                    else:
                        pool.tensor_copy(cur[:, cols(T)], t_y[:, b, 0:P]).then_inc(kept_ok, 1)

                if stage == "feat":
                    continue
                if stage != "L0a":
                    rows_stored(pool, before(stage))
                if stage in REL:
                    pool.wait_ge(setup_done, 1)
                    for c in range(CHUNKS):
                        chunk_groups(pool, int(stage == "L2b"), c, gathers(stage, dyn))
                else:
                    static_groups(pool, stage, gathers(stage, stat))
                if stage in KEEP:
                    tiles(pool, [(0, keep)])

        @block.scalar
        def _(act):
            act.wait_ge(setup_done, 1)

            def stage_idx(sems, g, u, q):
                act.wait_ge(sems.used, g * G + q + 1)
                mark(act, "act")
                q4 = q % G * UNIT
                of = slice((u + q) * UNIT, (u + q + 1) * UNIT) if isinstance(u, int) else bass.ds((u + q) * UNIT, UNIT)
                nc.scalar.copy(slot_idx[:, q4:q4 + UNIT], src_sb[:, of]).then_inc(sems.staged, 1)

            def indices(sems):
                def body(g, u, last):
                    for q in range(G):
                        stage_idx(sems, g, u, q)
                return body

            def gelu1(u):
                act.wait_ge(h1_sum, u + 1)
                if not isinstance(u, int) or u > 0:
                    act.wait_ge(h2_sum, u)
                mark(act, "act")
                nc.scalar.activation(h1, ps[:, H_BANK, 0:HALF], ACT.Gelu_apprx_tanh,
                                     scale=float(1.0 / np.sqrt(RADIAL))).then_inc(h1_done, 1)

            def gelu2(u, b):
                act.wait_ge(h2_sum, u + 1)
                if not isinstance(u, int):
                    act.wait_ge(rad_sum, u)
                mark(act, "act")
                nc.scalar.activation(h2[:, b, :], ps[:, H_BANK, 0:HALF], ACT.Gelu_apprx_tanh,
                                     scale=float(1.0 / np.sqrt(HID1))).then_inc(h2_done, 1)

            def scale_rad(u, q):
                b = q % 2
                act.wait_ge(rad_sum, u + 1)
                act.wait_ge(stat.onehot, u + (PASS["L1"] * G - 1))
                mark(act, "act")
                for t in range(UNIT):
                    for i in range(4):
                        of = rad_ps(b, t)[:, 0:2 * MUL] if i == 0 else rad_ps(b, t)[:, 2 * MUL:4 * MUL]
                        last = nc.scalar.activation(qs[:, b, t, i, :, :].rearrange("p a c -> p (a c)"), of, ACT.Copy,
                                                    scale=ea[:, q % G, t, i:i + 1])
                last.then_inc(scaled, 1)

            def radial(g, u, last):
                for q in range(G):
                    gelu1(u + q + 2)
                    scale_rad(u + q + 1, q + 1)
                    gelu2(u + q + 2, q % 2)
                    if q + 3 < G or not last:
                        stage_idx(stat, g, u, q + 3)

            for stage in order:
                layer = int(stage == "L2b")

                if stage == "L1":
                    for q in range(3):
                        stage_idx(stat, PASS["L1"], 0, q)
                    gelu1(0)
                    gelu2(0, 0)
                    scale_rad(0, 0)
                    gelu1(1)
                    gelu2(1, 1)
                    static_groups(act, stage, radial, peel_last=True)
                elif stage in REL:
                    def bias_z(T, b, h):
                        act.wait_ge(z_sum, count(stage, T, REL))
                        if not early(T):
                            act.wait_ge(z_out[b], half_count(stage, b, h - 1, REL))
                            act.wait_ge(z_stat, count(stage, T - 2, REL))
                        mark(act, "act")
                        for r in range(R + 1):
                            last = nc.scalar.activation(t_a[:, b, r * D:(r + 1) * D],
                                                        ps_flat[:, 1536 * b + r * D:1536 * b + (r + 1) * D],
                                                        ACT.Identity, bias=relv[:, 0, r:r + 1])
                        last.then_inc(z_ok, 1)

                    act.wait_ge(relw_in, 64 * (layer + 1))
                    if layer:
                        act.wait_ge(sum_ok, count("L2a", NT - 1))
                    for c in range(CHUNKS):
                        chunk_groups(act, layer, c, indices(dyn))
                        tiles(act, [(0, bias_z)], CHUNK_T0[c], CHUNK_T0[c + 1])
                    act.wait_ge(bn_mv, layer + 1)
                    nc.scalar.activation(bn[:, 0, :], zmv[:, :, 1], ACT.Sqrt, bias=eps_c[:]).then_inc(bn_sd, 1)
                    act.wait_ge(bn_ok, layer + 1)
                elif stage != "feat":
                    static_groups(act, stage, indices(stat))

                def relu_z(T, b, h):
                    act.wait_ge(z_in[b], (h + 1 + PER[b] * layer) * 16)
                    mark(act, "act")
                    for r in range(R + 1):
                        last = nc.scalar.activation(t_a[:, b, r * D:(r + 1) * D], t_a[:, b, r * D:(r + 1) * D],
                                                    ACT.Relu, bias=bn[:, 3, r:r + 1], scale=bn[:, 2, r:r + 1])
                    last.then_inc(z_act, 1)

                def evacuate(T, b, h):
                    act.wait_ge(sum_ok, count(stage, T))
                    if stage in PRELU:
                        if not early(T):
                            act.wait_ge(evac_ok, count(stage, T - 2))
                        i = PRELU.index(stage)
                        mark(act, "act")
                        nc.scalar.activation(t_b[:, b, :], ps[:, b, 0:P], ACT.Relu, bias=wsb["L3_b"][:, i:i + 1]
                                             ).then_inc(relu_ok, 1)
                        return
                    if not early(T):
                        act.wait_ge(turn_ok, count(stage, T - 2))
                        if stage in KEEP:
                            act.wait_ge(kept_ok, count(stage, T - 2, KEEP))
                    mark(act, "act")
                    to = t_y[:, b, 0:P]
                    if stage == "L0a":
                        for k in range(2):
                            last = nc.scalar.activation(t_y[:, b, k * P:(k + 1) * P], ps[:, b, k * P:(k + 1) * P], ACT.Relu,
                                                        bias=wsb["L0_b1"][:, k:k + 1])
                        last.then_inc(evac_ok, 1)
                    elif stage in ("feat", "L1"):
                        nc.scalar.copy(to, ps[:, b, 0:P]).then_inc(evac_ok, 1)
                    else:
                        bias = wsb["L0_b2"][:, 0:1] if stage == "L0b" else relbias[:, 1:2]
                        nc.scalar.activation(to, ps[:, b, 0:P], ACT.Relu if stage == "L2a" else ACT.Identity,
                                             bias=bias).then_inc(evac_ok, 1)

                def copy_rows(T, b, h):
                    act.wait_ge(turn_ok, count(stage, T))
                    if ALL.index(stage) or not early(T):
                        act.wait_ge(stored[b], half_count(stage, b, h - 1))
                    mark(act, "act")
                    nc.scalar.copy(rowt[:, b, :], ps[:, 2 + b, 0:P]).then_inc(row_ok, 1)

                def root(T, b, h):
                    act.wait_ge(mv_ok, count(stage, T, NORM))
                    if not early(T):
                        act.wait_ge(rstd_ok, count(stage, T - 2, NORM))
                    mark(act, "act")
                    nc.scalar.activation(sd[:, b, 0:1], mv[:, b, 1:2], ACT.Sqrt, bias=eps_c[:]).then_inc(sd_ok, 1)

                def copy_cur(T, b, h):
                    act.wait_ge(back_ok, count(stage, T, NORM))
                    mark(act, "act")
                    nc.scalar.copy(cur[:, cols(T)], ps[:, 4 + b, 0:P]).then_inc(cur_ok, 1)

                steps = []
                if stage in REL:
                    steps.append((0, relu_z))
                steps.append((1 if stage in REL else 0, evacuate))
                if stage in NORM:
                    lag = 2 if stage in REL else 1
                    steps.append((lag, root))
                    if stage != final:
                        steps.append((lag + 2, copy_cur))
                else:
                    steps.append((2 if stage in REL else 1, copy_rows))
                tiles(act, steps)

        @block.tensor
        def _(pe):
            x_n = pe.alloc_register("pe_extra_windows")
            pe.reg_mov(x_n, 0)
            pe.wait_ge(spread_ok, 1)
            for v in range(2):
                last = pe.matmul(ps[:, v, 0:NU], ones[0:TROWS, :], arena[0:TROWS, 5000 + v * NU:5000 + (v + 1) * NU],
                                 start=True, stop=True)
            last.then_inc(rows_sum, 1)
            pe.wait_ge(setup_done, 1)
            pe.sem_inc(stat.used, G)
            pe.sem_inc(dyn.used, G)

            def sums(name, to, q, t, hot, first):
                def product(block, rows, start):
                    return pe.matmul(block, rows, hot, start=start, stop=True, skip_group_check=True)

                row = ring[:, q * UNIT + t, :]
                if name == "L1":
                    for k in range(2):
                        last = product(to[:, k * W:(k + 1) * W], msg[:, q % 2, t, k * D:(k + 1) * D], first and k == 0)
                elif name == "L0a":
                    product(to[:, 0:W], row, first)
                    last = product(to[:, W:2 * W], ones[:], False)
                else:
                    last = product(to, row, first)
                return last

            def sum_unit(name, kind, sems, g, u, q, between=lambda: None):
                width = W * R if name in REL else W
                windows = pe.snap(window(pe, kind, u + q) & 255)
                pe.wait_ge(sems.gathered[q], (g + 1) * (16 * UNIT))
                pe.wait_ge(sems.onehot, g * G + q + 1)
                with pe.If(windows > 1):
                    for t in range(UNIT):
                        with pe.Fori(1, windows):
                            pe.reg_add(x_n, x_n, 1)
                            pe.wait_ge(x_onehot, pe.snap(x_n))
                            mark(pe, "pe")
                            sums(name, ps[:, X_BANK, 0:sums_shape(name)[0] * width], q, t, xone[:, 0:width], True
                                 ).then_inc(x_sum, 1)
                pe.wait_ge(sems.added, g * G + q + 1)
                mark(pe, "pe")
                for t in range(UNIT):
                    if t == UNIT // 2:
                        between()
                    last = sums(name, bank(name, q), q, t, onehot[:, q % 2, t, 0:width], t == 0)
                last.then_inc(sems.used, 1)

            def sum_group(name, kind, sems):
                def body(g, u, last):
                    for q in range(G):
                        sum_unit(name, kind, sems, g, u, q)
                return body

            def hidden1(u, q, h):
                pe.wait_ge(attr_in[q], (h + 1) * 32)
                if not isinstance(u, int) or u > 0:
                    pe.wait_ge(h2_done, u)
                mark(pe, "pe")
                pe.matmul(ps[:, H_BANK, 0:HALF], wsb["mlp1"][:], attr[:, q, :], start=True, stop=True).then_inc(h1_sum, 1)

            def hidden2(u):
                pe.wait_ge(h1_done, u + 1)
                mark(pe, "pe")
                pe.matmul(ps[:, H_BANK, 0:HALF], wsb["mlp2"][:], h1, start=True, stop=True).then_inc(h2_sum, 1)

            def radial(u, b):
                pe.wait_ge(h2_done, u + 1)
                pe.wait_ge(stat.onehot, u + (PASS["L1"] * G - 1))
                mark(pe, "pe")
                for c in range(2):
                    last = pe.matmul(ps[:, RAD_BANKS[b], c * HALF:(c + 1) * HALF], h2[:, b, c * P:(c + 1) * P], wsb["mlp3"][:],
                                     start=True, stop=True)
                last.then_inc(rad_sum, 1)

            def radial_group(i):
                u = i * G
                for q in range(G):
                    hidden1(u + q + 2, (q + 2) % G, i + (q + 2) // G)
                    radial(u + q + 1, (q + 1) % 2)
                    sum_unit("L1", 0, stat, i + PASS["L1"], u, q, lambda: hidden2(u + q + 2))

            for stage in order:
                layer = int(stage == "L2b")
                if stage == "L1":
                    pe.wait_ge(row_ok, count("feat", NT - 1))
                    hidden1(0, 0, 0)
                    hidden2(0)
                    radial(0, 0)
                    hidden1(1, 1, 0)
                    hidden2(1)
                    with pe.Fori(0, NG) as i:
                        radial_group(i)
                    for q in range(G):
                        pe.wait_ge(attr_in[q], 32 * (NG + 1))
                    pe.wait_ge(h2_done, NG * G + 2)
                    pe.wait_ge(scaled, NG * G + 1)
                    pe.wait_ge(stat.added, (PASS[stage] + NG + 1) * G)
                elif stage in REL:
                    def z_tile(T, b, h):
                        if not (early(T) and layer == 0):
                            pe.wait_ge(z_ok, count(stage, T - 2, REL))
                        t = T - CHUNK_T0[c]
                        mark(pe, "pe")
                        for r in range(R + 1):
                            if r < R:
                                node = t * (P * R) + r
                                rows = arena[:, node:node + (P - 1) * R + 1:R] if isinstance(t, int) else \
                                    arena[:, bass.ds(t * (P * R), P * R)].rearrange("p (n r) -> p n r", r=R)[:, :, r]
                            else:
                                rows = cur[:, cols(T)]
                            last = pe.matmul(ps_flat[:, 1536 * b + r * D:1536 * b + (r + 1) * D], relw1[:, r, :], rows,
                                             start=True, stop=True)
                        last.then_inc(z_sum, 1)

                    pe.wait_ge(relw_in, 64 * (layer + 1))
                    if not layer:
                        pe.wait_ge(cur_ok, count("L1", NT - 1, NORM))
                    else:
                        pe.wait_ge(kept_ok, count("L2a", NT - 1, KEEP))
                    for c in range(CHUNKS):
                        g1 = chunk_groups(pe, layer, c, sum_group(stage, 1 + c, dyn))
                        pe.wait_ge(dyn.added, pe.snap(g1 * G + 2 * G))
                        mark(pe, "pe")
                        tiles(pe, [(0, z_tile)], CHUNK_T0[c], CHUNK_T0[c + 1])
                    pe.wait_ge(z_ok, count(stage, NT - 1, REL))
                elif stage != "feat":
                    static_groups(pe, stage, sum_group(stage, 0, stat))

                def node_sums(T, b, h):
                    if stage in SAGE:
                        pe.wait_ge(mean_ok, count(stage, T, SAGE))
                    elif stage in REL:
                        pe.wait_ge(z_act, count(stage, T, REL))
                    if not early(T):
                        pe.wait_ge(evac_ok, count(stage, T - 2))
                    mark(pe, "pe")
                    mean, to = t_a[:, b, 0:P], ps[:, b, 0:P]
                    if stage == "L0a":
                        for k in range(2):
                            o = ps[:, b, k * P:(k + 1) * P]
                            pe.matmul(o, wsb["L0_W1l"][:, k * P:(k + 1) * P], mean, start=True, stop=False)
                            last = pe.matmul(o, wsb["L0_W1r"][:, k * P:(k + 1) * P], cur[:, cols(T)], start=False, stop=True)
                        last.then_inc(sum_ok, 1)
                    elif stage == "L0b":
                        pe.matmul(to, ident[:], mean, start=True, stop=False)
                        for k in range(2):
                            last = pe.matmul(to, wsb["L0_W2r"][:, k * P:(k + 1) * P], acc3[:, 1 + k, cols(T)],
                                             start=False, stop=(k == 1))
                        last.then_inc(sum_ok, 1)
                    elif stage == "feat":
                        pe.matmul(to, wsb["F"][:], cur[:, cols(T)], start=True, stop=True).then_inc(sum_ok, 1)
                    elif stage == "L1":
                        pe.matmul(to, wsb["Fself"][:], cur[:, cols(T)], start=True, stop=False)
                        for k in range(2):
                            last = pe.matmul(to, wsb["M"][:, k * D:(k + 1) * D], acc3[:, k, cols(T)], start=False, stop=(k == 1))
                        last.then_inc(sum_ok, 1)
                    elif stage in REL:
                        for r in range(R + 1):
                            last = pe.matmul(to, relw2[:, r, :], t_a[:, b, r * D:(r + 1) * D], start=(r == 0), stop=(r == R))
                        last.then_inc(sum_ok, 1)
                    else:
                        i = PRELU.index(stage)
                        pe.matmul(to, wsb["L3_Wl"][:, i * P:(i + 1) * P], mean, start=True, stop=False)
                        pe.matmul(to, wsb["L3_Wr"][:, i * P:(i + 1) * P], cur[:, cols(T)], start=False, stop=True
                                  ).then_inc(sum_ok, 1)

                def turn(T, b, h):
                    pe.wait_ge(evac_ok, count(stage, T))
                    if not early(T):
                        if stage in NORM:
                            pe.wait_ge(res_ok, count(stage, T - 2, NORM))
                        else:
                            pe.wait_ge(row_ok, count(stage, T - 2))
                    mark(pe, "pe")
                    to = ps[:, 2 + b, 0:P]
                    if stage == "L0a":
                        for k in range(2):
                            last = pe.matmul(to, t_y[:, b, k * P:(k + 1) * P], wsb["L0_W2l"][:, k * P:(k + 1) * P],
                                             start=(k == 0), stop=(k == 1))
                    else:
                        last = pe.transpose(to, t_y[:, b, 0:P], ident[:])
                    last.then_inc(turn_ok, 1)

                def back(T, b, h):
                    pe.wait_ge(row_ok, count(stage, T))
                    if not early(T):
                        pe.wait_ge(cur_ok, count(stage, T - 2, NORM))
                    mark(pe, "pe")
                    pe.transpose(ps[:, 4 + b, 0:P], rowt[:, b, :], ident[:]).then_inc(back_ok, 1)

                if stage == "feat":
                    pe.wait_ge(cur_ok, count("L0b", NT - 1, NORM))
                if before(stage) in KEEP and stage not in REL:
                    pe.wait_ge(kept_ok, count(before(stage), NT - 1, KEEP))
                if stage == "L3a":
                    pe.wait_ge(cur_ok, count("L2b", NT - 1, NORM))
                steps = [(0, node_sums), (1, turn)]
                if stage in NORM and stage != final:
                    steps.append((3, back))
                tiles(pe, steps)

        @block.vector
        def _(dve):
            x_n = dve.alloc_register("dve_extra_windows")
            dve.reg_mov(x_n, 0)
            n_chain = [0]

            def then(ins):
                n_chain[0] += 1
                ins.then_inc(chain, 1)
                dve.wait_ge(chain, n_chain[0])

            V = nc.vector

            dve.wait_ge(loaded, 16 * (5 + len(wsb)))
            dve.wait_ge(iotas, 1)

            def area(at, n=ETP, parts=P, dt=F32):
                return arena[0:parts, at:at + n].bitcast(dt)

            UE = UNIT * P
            dst_i, et_i, tiles_i = area(0, dt=I32), area(ETP, dt=I32), area(2 * ETP, UPP * UE, TROWS, I32)
            tiles_f, far = area(3000, UPP * UE, TROWS), area(15000, UPP * UE, TROWS)
            spread = [area(5000 + v * NU, NU, TROWS) for v in range(2)]
            dst_f, seg_f, low, high = area(7000), area(8000), area(9000, NU), area(10000, NU)
            base, t1, t2, number = area(11000, NU), area(12000, NU), area(14000, NU, dt=I32), area(16100, NU)
            t3 = area(13000, NU)
            V.memset(ones[:], 1.0)
            V.memset(eps_c[:], EPS)
            V.tensor_copy(iota_w[:], iota_i)
            V.tensor_copy(number, area(17200, NU, dt=I32))
            V.tensor_copy(dst_f, dst_i)
            V.tensor_copy(tiles_f, tiles_i)
            then(V.tensor_scalar(ident[:], area(17000, P, dt=I32), 0.0, None, ALU.is_equal))
            V.tensor_scalar(far, tiles_f, 0.0, FAR, ALU.is_lt, ALU.mult)
            then(V.scalar_tensor_tensor(seg_f, dst_f, float(R), et_i, ALU.mult, ALU.add))
            then(V.tensor_tensor(far, far, tiles_f, ALU.add))
            per_unit = "p (k e) -> p k e"
            V.tensor_reduce(minmax[0:TROWS, 0, :], far.rearrange(per_unit, k=UPP), AX.X, ALU.min)
            then(V.tensor_reduce(minmax[0:TROWS, 1, :], tiles_f.rearrange(per_unit, k=UPP), AX.X, ALU.max))
            for v in range(2):
                last = V.tensor_tensor(spread[v].rearrange("p (q k) -> p q k", k=UPP),
                                       minmax[0:TROWS, v, :].unsqueeze(1).to_broadcast([TROWS, TROWS, UPP]),
                                       ident[0:TROWS, 0:TROWS].unsqueeze(2).to_broadcast([TROWS, TROWS, UPP]), ALU.mult)
            last.then_inc(spread_ok, 1)
            dve.wait_ge(rows_sum, 1)
            for v, row in enumerate((low, high)):
                last = V.tensor_copy(row, ps[:, v, 0:NU])
            then(last)
            def tiles_of(ap):
                return ap.rearrange("p (u t) -> p u t", t=UNIT)

            for kind in range(NTYPE):
                c0 = 0 if kind == 0 else CHUNK_T0[kind - 1] * P
                c1 = N if kind == 0 else min(N, CHUNK_T0[kind] * P)
                V.tensor_scalar(base, low, float(c0), float(c1 - 1), ALU.max, ALU.min)
                then(V.tensor_scalar(t1, high, 0.0, float(c1 - 1), ALU.max, ALU.min))
                bases = base.unsqueeze(2).to_broadcast([P, NU, UNIT])
                if kind == 0:
                    V.tensor_tensor(tiles_of(rel_seg[:, 0, :]), tiles_of(dst_f), bases, ALU.subtract)
                else:
                    V.scalar_tensor_tensor(tiles_of(rel_seg[:, kind, :]), bases, -float(R), tiles_of(seg_f), ALU.mult, ALU.add)
                then(V.tensor_tensor(t1, t1, base, ALU.subtract))
                then(V.tensor_scalar(t2, t1, 0.0, float(W_RECIP), ALU.max, ALU.mult))
                then(V.tensor_scalar(t2, t2, 16, None, ALU.arith_shift_right))
                then(V.tensor_scalar(t1, t2, 1.0 - 256.0 * c0, None, ALU.add))
                then(V.scalar_tensor_tensor(win[0:1, kind, :], base[0:1], 256.0, t1[0:1], ALU.mult, ALU.add))
                if kind:
                    then(V.tensor_scalar(t1, low, float(c1), None, ALU.is_lt))
                    then(V.scalar_tensor_tensor(t1, high, float(c0), t1, ALU.is_ge, ALU.mult))
                    then(V.scalar_tensor_tensor(t3, number, 1.0, t1, ALU.add, ALU.mult))
                    then(V.tensor_reduce(ranges[:, 1, kind - 1:kind], t3, AX.X, ALU.max))
                    then(V.tensor_scalar(t3, t1, -FAR, FAR, ALU.mult, ALU.add))
                    then(V.tensor_tensor(t3, t3, number, ALU.add))
                    then(V.tensor_reduce(ranges[:, 0, kind - 1:kind], t3, AX.X, ALU.min))
            then(V.tensor_tensor(ranges[:, 0, :], ranges[:, 0, :], ranges[:, 1, :], ALU.min))
            then(V.tensor_tensor(ranges[:, 2, :], ranges[:, 1, :], ranges[:, 0, :], ALU.subtract))
            then(V.tensor_scalar(ranges_i[:], ranges[:, 2, :], 1.0, float(G - 1), ALU.max, ALU.add))
            then(V.tensor_scalar(ranges_i[:], ranges_i[:], 2, None, ALU.arith_shift_right))
            then(V.tensor_copy(ranges[:, 2, :], ranges_i[:]))
            then(V.memset(ptab_f[:, 0:1], 0.0))
            for k in range(2 * CHUNKS):
                c = k % CHUNKS
                if k:
                    then(V.tensor_scalar(ptab_f[:, 3 * k:3 * k + 1], ptab_f[:, 3 * k - 2:3 * k - 1], 1.0, None, ALU.add))
                V.tensor_copy(ptab_f[:, 3 * k + 2:3 * k + 3], ranges[:, 0, c:c + 1])
                then(V.scalar_tensor_tensor(ptab_f[:, 3 * k + 1:3 * k + 2], ranges[:, 2, c:c + 1], -1.0,
                                            ptab_f[:, 3 * k:3 * k + 1], ALU.add, ALU.add))
            V.tensor_copy(ptab[:], ptab_f[:])
            V.tensor_scalar(wsb["F"][:], wsb["F"][:], INV_MUL, None, ALU.mult)
            V.tensor_scalar(wsb["Fself"][:], wsb["Fself"][:], COS * INV_MUL, None, ALU.mult)
            V.tensor_scalar(wsb["M"][:, 0:D], wsb["M"][:, 0:D], CONV, None, ALU.mult)
            V.tensor_scalar(wsb["M"][0:96, D:2 * D], wsb["M"][0:96, D:2 * D], CONV, None, ALU.mult)
            then(V.tensor_scalar(wsb["M"][96:128, D:2 * D], wsb["M"][96:128, D:2 * D], CONV_DOT, None, ALU.mult))
            dve.sem_inc(stat.added, G)
            dve.sem_inc(dyn.added, G)
            dve.sem_inc(setup_done, 1)

            def build_unit(name, kind, sems, g, u, q):
                width, b, place = W * R if name in REL else W, q % 2, q % G
                dve.wait_ge(sems.used, g * G + q + (G - 1))
                segs = rel_seg[:, kind, (u + q) * UNIT:(u + q + 1) * UNIT] if isinstance(u, int) else \
                    rel_seg[:, kind, bass.ds((u + q) * UNIT, UNIT)]
                ins = V.tensor_tensor(onehot[:, b, :, 0:width], iota_w[:, 0:width].unsqueeze(1).to_broadcast([P, UNIT, width]),
                                      segs.unsqueeze(2).to_broadcast([P, UNIT, width]), ALU.is_equal)
                if name == "L1":
                    if not isinstance(u, int) or u + q > 0:
                        dve.wait_ge(sems.onehot, u + q + PASS["L1"] * G)
                    dve.wait_ge(sems.gathered[place], (g + (q // G + 1)) * (16 * UNIT))
                    dve.wait_ge(scaled, u + q + 1)
                    rows = ring[:, place * UNIT:(place + 1) * UNIT, :]
                    scalar, vector = rows[:, :, 0:MUL], rows[:, :, MUL:4 * MUL].rearrange("p t (i c) -> p t i c", i=3)
                    scalar3, w10 = [a.unsqueeze(2).to_broadcast([P, UNIT, 3, MUL]) for a in (scalar, qs[:, b, :, 0, 1, :])]

                    def threes(c):
                        return msg[:, b, :, c:c + 3 * MUL].rearrange("p t (i c) -> p t i c", i=3)

                    V.tensor_tensor(dots, qs[:, b, :, 1:4, 1, :], vector, ALU.mult).then_inc(dots_ok, 1)
                    V.tensor_tensor(msg[:, b, :, 0:MUL], qs[:, b, :, 0, 0, :], scalar, ALU.mult)
                    V.tensor_tensor(threes(MUL), w10, vector, ALU.mult)
                    V.tensor_tensor(threes(D), qs[:, b, :, 1:4, 0, :], scalar3, ALU.mult)
                    dve.wait_ge(dots_ok, u + q + 1)
                    mark(dve, "dve")
                    ins = V.tensor_reduce(msg[:, b, :, D + 3 * MUL:D + 4 * MUL], dots.rearrange("p t i c -> p t c i"),
                                          AX.X, ALU.add)
                ins.then_inc(sems.onehot, 1)

            def add_unit(name, kind, sems, g, u, q):
                width = W * R if name in REL else W
                v = window(dve, kind, u + q)
                top = (NT if name not in REL else CHUNK_TILES[kind - 1]) * P - 1
                node = dve.snap(v >> 8).with_bounds(min_val=0, max_val=top)
                windows = dve.snap(v & 255)
                with dve.If(windows > 1):
                    for t in range(UNIT):
                        dve.drain()
                        tile = (u + q) * UNIT + t
                        V.tensor_copy(xseg[:], rel_seg[:, kind, tile:tile + 1] if isinstance(u, int) else
                                      rel_seg[:, kind, bass.ds(tile, 1)])
                        with dve.Fori(1, windows) as i:
                            dve.drain()
                            V.tensor_scalar(xseg[:], xseg[:], -float(width), None, ALU.add)
                            dve.drain()
                            V.tensor_scalar(xone[:, 0:width], iota_w[:, 0:width], xseg[:], None, ALU.is_equal).then_inc(x_onehot, 1)
                            dve.reg_add(x_n, x_n, 1)
                            dve.wait_ge(x_sum, dve.snap(x_n))
                            mark(dve, "dve")
                            to = acc_at(name, dve.snap(node + i * W).with_bounds(min_val=0, max_val=top))
                            n = sums_shape(name)[0] * width
                            V.tensor_tensor(to, to, shaped(name, ps[:, X_BANK, 0:n]), ALU.add)
                    dve.drain()
                dve.wait_ge(sems.used, g * G + q + 1 + G)
                dve.wait_ge(sems.added, g * G + q + G)
                to = acc_at(name, node)
                V.tensor_tensor(to, to, shaped(name, bank(name, q)), ALU.add).then_inc(sems.added, 1)

            def pass_group(name, kind, sems):
                def body(g, u, last):
                    for q in range(G):
                        if q + 1 < G or not last:
                            build_unit(name, kind, sems, g, u, q + 1)
                        add_unit(name, kind, sems, g, u, q)
                return body

            for stage in order:
                layer = int(stage == "L2b")
                if stage != "L0a":
                    dve.wait_ge(turn_ok, count(before(stage), NT - 1))
                if stage in REL:
                    def z_stats(T, b, h):
                        dve.wait_ge(z_ok, count(stage, T, REL))
                        n = LAST if isinstance(T, int) and T == NT - 1 else P
                        mark(dve, "dve")
                        for r in range(R + 1):
                            to = zst[:, T, r, :] if isinstance(T, int) else \
                                zst[:, bass.ds(T, 1), r, :].rearrange("p a c -> p (a c)")
                            last = V.bn_stats(to, t_a[:, b, r * D:r * D + n])
                        last.then_inc(z_stat, 1)

                    for c in range(CHUNKS):
                        if c:
                            dve.wait_ge(z_sum, count(stage, CHUNK_T0[c] - 1, REL))
                        then(V.memset(arena[:, 0:(CHUNK_TILES[c] * P + W) * R], 0.0))
                        g0, _, u0 = chunk_values(dve, layer, c)
                        build_unit(stage, 1 + c, dyn, g0, u0, 0)
                        chunk_groups(dve, layer, c, pass_group(stage, 1 + c, dyn), peel_last=True)
                        tiles(dve, [(0, z_stats)], CHUNK_T0[c], CHUNK_T0[c + 1])
                    dve.wait_ge(z_stat, count(stage, NT - 1, REL))
                    dve.wait_ge(relw_in, 64 * (layer + 1))
                    for r in range(R + 1):
                        last = V.bn_aggr(zmv[:, r, :], zst[:, :, r, :])
                    last.then_inc(bn_mv, 1)
                    then(V.tensor_reduce(relbias[:, 1:2], relv[:, 3, :], AX.X, ALU.add))
                    then(V.tensor_tensor(relbias[:, 1:2], relbias[:, 1:2], relbias[:, 0:1], ALU.add))
                    dve.wait_ge(bn_sd, layer + 1)
                    then(V.reciprocal(bn[:, 1, :], bn[:, 0, :]))
                    then(V.tensor_tensor(bn[:, 2, :], relv[:, 1, :], bn[:, 1, :], ALU.mult))
                    then(V.tensor_tensor(bn[:, 3, :], zmv[:, :, 0], bn[:, 2, :], ALU.mult))
                    V.tensor_tensor(bn[:, 3, :], relv[:, 2, :], bn[:, 3, :], ALU.subtract).then_inc(bn_ok, 1)
                elif stage != "feat":
                    then(V.memset(arena[:, 0:PASS_BLOCKS[stage] * ACCW], 0.0))
                    build_unit(stage, 0, stat, PASS[stage], 0, 0)
                    static_groups(dve, stage, pass_group(stage, 0, stat), peel_last=True)
                    dve.wait_ge(stat.added, (PASS[stage] + NG + 1) * G)
                    if stage == "L0a":
                        then(V.tensor_scalar(rdeg[:], acc3[:, 1, 0:NP], 1.0, None, ALU.max))
                        then(V.reciprocal(rdeg[:], rdeg[:]))

                def mean(T, b, h):
                    if not early(T):
                        dve.wait_ge(sum_ok, count(stage, T - 2))
                    V.tensor_tensor(t_a[:, b, 0:P], acc3[:, 0, cols(T)], rdeg[:, cols(T)], ALU.mult).then_inc(mean_ok, 1)

                def prelu(T, b, h):
                    i = PRELU.index(stage)
                    dve.wait_ge(relu_ok, count(stage, T, PRELU))
                    if not early(T):
                        dve.wait_ge(evac_ok, count(stage, T - 2))
                    V.tensor_scalar(t_m[:, b, :], ps[:, b, 0:P], wsb["L3_b"][:, i:i + 1], 0.0, ALU.add, ALU.min).then_inc(min_ok, 1)
                    dve.wait_ge(min_ok, count(stage, T, PRELU))
                    if not early(T):
                        dve.wait_ge(turn_ok, count(stage, T - 2))
                        if stage in KEEP:
                            dve.wait_ge(kept_ok, count(stage, T - 2, KEEP))
                    V.scalar_tensor_tensor(t_y[:, b, 0:P], t_m[:, b, :], wsb["prelu_w"][:, 0:1], t_b[:, b, :], ALU.mult, ALU.add).then_inc(evac_ok, 1)

                def norm_stats(T, b, h):
                    dve.wait_ge(turn_ok, count(stage, T))
                    dve.wait_ge(x_in[b], half_count(stage, b, h, NORM))
                    if not early(T):
                        dve.wait_ge(row_ok, count(stage, T - 2))
                    V.tensor_tensor(t_n[:, b, :], ps[:, 2 + b, 0:P], t_x[:, b, :], ALU.add).then_inc(res_ok, 1)
                    dve.wait_ge(res_ok, count(stage, T, NORM))
                    V.bn_stats(st6[:, b, :], t_n[:, b, :]).then_inc(lnst_ok, 1)
                    dve.wait_ge(lnst_ok, count(stage, T, NORM))
                    mark(dve, "dve")
                    V.bn_aggr(mv[:, b, :], st6[:, b, :]).then_inc(mv_ok, 1)

                def normalise(T, b, h):
                    dve.wait_ge(sd_ok, count(stage, T, NORM))
                    V.reciprocal(sd[:, b, 1:2], sd[:, b, 0:1]).then_inc(rstd_ok, 1)
                    dve.wait_ge(rstd_ok, count(stage, T, NORM))
                    dve.wait_ge(stored[b], half_count(stage, b, h - 1))
                    if stage != final and not early(T):
                        dve.wait_ge(back_ok, count(stage, T - 2, NORM))
                    V.tensor_scalar(rowt[:, b, :], t_n[:, b, :], mv[:, b, 0:1], sd[:, b, 1:2],
                                    ALU.subtract, ALU.mult).then_inc(row_ok, 1)

                steps = []
                if stage in SAGE:
                    steps.append((0, mean))
                if stage in PRELU:
                    steps.append((1, prelu))
                if stage in NORM:
                    steps += [(1, norm_stats), (2, normalise)]
                if steps:
                    tiles(dve, steps)


def lay_out(inputs, n_layers):
    def edge_tiles(a):
        return a.reshape(ETP, P).T

    def padded(a, rows, fill=0):
        full = np.full((rows,) + a.shape[1:], fill, a.dtype)
        full[:a.shape[0]] = a
        return full

    a = {k: np.asarray(v) for k, v in inputs.items()}
    EP = ETP * P
    x = padded(a["x"], NP)
    dst = padded(a["dst"], EP, -1)
    arrays = {
        "x": x, "x_t": x.T,
        "src": edge_tiles(padded(a["src"], EP)),
        "dst": edge_tiles(dst), "dst_tiles": dst.reshape(TROWS, UPP * UNIT * P),
        "etype": edge_tiles(padded(a["edge_type_8"], EP)),
        "ea4": padded(a["edge_attr_4"], EP).reshape(ETP, P, 4).transpose(1, 0, 2).reshape(P, ETP * 4),
        "ea8": padded(a["edge_attr_8"], EP).reshape(NU, 2, UNIT // 2 * P, RADIAL).transpose(1, 3, 0, 2).reshape(2 * RADIAL, -1),
    }

    def twice(m):
        k, n = m.shape
        full = np.zeros((2 * k, 2 * n), m.dtype)
        full[:k, :n], full[k:, n:] = m, m
        return full

    def halves(m):
        return m.reshape(2, P, m.shape[1]).transpose(1, 0, 2).reshape(P, -1)

    w00, w01, w10, w11 = (a["L1_gnn_Wp_" + k] for k in ("00", "01", "10", "11"))
    w0, w1 = a["L1_gnn_W1_0e"], a["L1_gnn_W1_1o"]
    c0, c1 = a["L1_gnn_W2_0e"], a["L1_gnn_W2_1o"]
    F, Fself = np.zeros((D, D), np.float32), np.zeros((D, D), np.float32)
    F[:MUL, :MUL], Fself[:MUL, :MUL] = w0[:, :MUL], w0[:, MUL:]
    M = np.zeros((D, 2 * D), np.float32)
    M[:MUL, :MUL] = c0[:MUL]
    for i in range(3):
        b = MUL + MUL * i
        F[MUL + i::3, b:b + MUL] = w1[:, :MUL]
        Fself[MUL + i::3, MUL + i::3] = w1[:, MUL:]
        M[b:b + MUL, MUL + i:D:3] = c1[MUL:]
        M[MUL * i:MUL * (i + 1), D + MUL + i:2 * D:3] = c1[:MUL]
    M[96:128, D:D + MUL] = c0[MUL:]
    weights = {
        "L0_W1l": a["L0_gnn_W1_l"].T, "L0_W1r": a["L0_gnn_W1_r"].T,
        "L0_b1": a["L0_gnn_b1"].reshape(2, P).T, "L0_b2": a["L0_gnn_b2"].reshape(P, 1),
        "L0_W2l": halves(a["L0_gnn_W2_l"].T), "L0_W2r": halves(a["L0_gnn_W2_r"].T),
        "F": F, "Fself": Fself, "M": M, "mlp1": twice(a["L1_gnn_W_mlp1"]), "mlp2": twice(a["L1_gnn_W_mlp2"]),
        "mlp3": twice(np.concatenate([w00, w10, w01, w11], axis=1)),
        "L3_Wl": np.concatenate([a[f"L3_gnn_W{i}l"].T for i in (1, 2, 3)], axis=1),
        "L3_Wr": np.concatenate([a[f"L3_gnn_W{i}r"].T for i in (1, 2, 3)], axis=1),
        "L3_b": np.stack([a[f"L3_gnn_b{i}"] for i in (1, 2, 3)], axis=1),
        "prelu_w": np.broadcast_to(a["L3_gnn_prelu_w"].reshape(1, 1), (P, 1)),
    }
    rel = []
    for i in range(2):
        p = f"L2_gnn_l{i}_"
        rel.append({
            "W1": a[p + "W1"].transpose(1, 0, 2), "W2": a[p + "W2"].transpose(1, 0, 2),
            "v": np.stack([a[p + k].T for k in ("b1", "gamma", "beta", "b2")], axis=1),
            "bias": a[p + "bias"].reshape(P, 1),
        })
    return arrays, weights, rel


LAYERS = 4


def kernel(**inputs):
    import concourse.bacc as _bacc
    from concourse.bass_utils import run_bass_kernel_spmd as _run

    nc = _bacc.Bacc("TRN2", target_bir_lowering=False, num_devices=1, dynamic_dma_scratch_size=8192)
    arrays, weights, rel = lay_out(inputs, LAYERS)
    feeds = {}

    def feed(name, a):
        a = np.ascontiguousarray(a)
        feeds[f"in_{name}_dram"] = a
        return nc.dram_tensor(f"in_{name}_dram", a.shape, mybir.dt.from_np(a.dtype), kind="ExternalInput").ap()

    args = [feed(k, arrays[k]) for k in ("x", "x_t", "src", "dst", "dst_tiles", "etype", "ea4", "ea8")]
    w = {k: feed("w_" + k, a) for k, a in weights.items()}
    w_rel = [{k: feed(f"rel{i}_{k}", a) for k, a in rel[i].items()} for i in range(2)]
    out = nc.dram_tensor("out_0_dram", (N, D), F32, kind="ExternalOutput").ap()
    build(nc, *args, w, w_rel, out, LAYERS)
    r = _run(nc, [feeds], core_ids=[0])
    return r.results[0]["out_0_dram"]
```

```python
from contextlib import ExitStack

import numpy as np

import concourse.bass as bass
from concourse import mybir

ALU = mybir.AluOpType
ACT = mybir.ActivationFunctionType
AX = mybir.AxisListType
F32 = mybir.dt.float32
I32 = mybir.dt.int32

P = 128
N, E, D = 6250, 106250, 128
R = 8
NT = -(-N // P)
NP = NT * P
LAST = N - (NT - 1) * P
UNIT = 4
G = 4
S = G * UNIT
ET = -(-E // P)
NG = -(-ET // S)
UPP = 2
TROWS = -(-(NG + 1) * G // UPP)
NU = TROWS * UPP
ETP = NU * UNIT
W = 36
W_RECIP = 65536 // W + 1
ACCW = NP + W
CHUNK_TILES = [17, 16, 16]
CHUNK_T0 = [0, 17, 33, 49]
CHUNKS = len(CHUNK_TILES)
ACT_RELUS = 4
MUL, RADIAL, HID1 = 32, 8, 64
FAR = 32768.0
EPS = 1e-5

assert N * W_RECIP < 2 ** 24 and NG * G + 4 <= NU
assert CHUNK_T0[-1] == NT and (max(CHUNK_TILES) * P + W) * R <= 3 * ACCW

INV_MUL = float(1.0 / np.sqrt(MUL))
COS, SIN = float(np.cos(np.pi / 8.0)), float(np.sin(np.pi / 8.0))
CONV = SIN / float(np.sqrt(2 * MUL) * np.sqrt(32.0) * np.sqrt(2.0))
CONV_DOT = CONV / float(np.sqrt(3.0))


def build(nc, x, x_t, src, dst, dst_tiles, etype, ea4, ea8, w, w_rel, out, layers):
    with ExitStack() as ctx:
        def sb(name, shape, dt=F32):
            return ctx.enter_context(nc.sbuf_tensor(name, shape, dt))

        def sem(name):
            return ctx.enter_context(nc.semaphore(name))

        def table(name):
            return nc.dram_tensor(name, [NP, D], F32, kind="Internal").ap()

        tab_hid = table("tab_hid")
        tab_x1 = table("tab_x1")
        tab_feat = table("tab_feat")
        tab_x2 = table("tab_x2")
        tab_h2 = table("tab_h2")
        tab_x3 = table("tab_x3")
        tab_h3 = [table("tab_h3a"), table("tab_h3b")]
        h2_dram = nc.dram_tensor("h2_dram", [P, NG * S * P // 2], F32, kind="Internal").ap()
        z_dram = nc.dram_tensor("z_dram", [2, NT, P, (R + 1) * D], F32, kind="Internal").ap()

        assert 2 * UNIT * W == 2 * (R + 1) * D // R
        arena = sb("arena", [P, 3 * ACCW])
        acc3 = arena[:].rearrange("p (k c) -> p k c", k=3)
        cur = sb("cur", [P, NP])
        rdeg = sb("rdeg", [P, NP])
        src_sb = sb("src_sb", [P, ETP], I32)
        NTYPE = 1 + CHUNKS
        rel_seg = sb("rel_seg", [P, NTYPE, ETP])
        win = sb("win", [1, NTYPE, NU], I32)
        ptab = sb("ptab", [P, 6 * CHUNKS], I32)
        ring = sb("ring", [P, S, D])
        slot_idx = sb("slot_idx", [P, S], I32)
        onehot = sb("onehot", [P, 2, UNIT, W * R])
        share = sb("share", [P, 2 * (R + 1) * D + NT * (R + 1) * 6])
        HALF = UNIT // 2 * P
        msg = share[:, 0:2 * UNIT * 2 * D].rearrange("p (b t c) -> p b t c", b=2, t=UNIT)
        dots = share[:, 2048:2048 + UNIT * 3 * MUL].rearrange("p (t i c) -> p t i c", t=UNIT, i=3)
        h2_in = share[:, 3840:3840 + G * HALF].rearrange("p (b c) -> p b c", b=G)
        h1 = share[:, 0:2 * HALF].rearrange("p (b c) -> p b c", b=2)
        h2 = share[:, 2 * HALF:4 * HALF].rearrange("p (b c) -> p b c", b=2)
        attr = share[0:2 * RADIAL, 3840:3840 + G * HALF].rearrange("p (b c) -> p b c", b=G)
        relw1 = share[:, 0:(R + 1) * D].rearrange("p (r c) -> p r c", c=D)
        relw2 = share[:, (R + 1) * D:2 * (R + 1) * D].rearrange("p (r c) -> p r c", c=D)
        zst = share[:, 2 * (R + 1) * D:].rearrange("p (t r k) -> p t r k", t=NT, k=6)
        xone = sb("xone", [P, W * R])
        xseg = sb("xseg", [P, 1])
        ident = sb("ident", [P, P])
        ones = sb("ones", [P, P])
        zeros = sb("zeros", [P, P])
        minmax = sb("minmax", [P, 2, UPP])
        iota_w = sb("iota_w", [P, W * R])
        zb = arena[:, 0:4 * (R + 1) * D].rearrange("p (q c) -> p q c", q=4)
        iota_i = arena[:, 18500:18500 + W * R].bitcast(I32)
        ea = sb("ea", [P, G, UNIT, 4])
        t_a = sb("t_a", [P, 2, (R + 1) * D])
        qs = t_a[:].rearrange("p b c -> p (b c)")[:, 0:2 * UNIT * 8 * MUL].rearrange(
            "p (b t i a c) -> p b t i a c", b=2, t=UNIT, i=4, a=2)
        t_b = sb("t_b", [P, 2, D])
        t_x = sb("t_x", [P, 4, D])
        t_y = sb("t_y", [P, 2, 2 * D])
        t_m = sb("t_m", [P, 2, D])
        t_n = sb("t_n", [P, 4, D])
        rowt = sb("rowt", [P, 4, D])
        st6 = sb("st6", [P, 2, 6])
        mv = sb("mv", [P, 2, 2])
        sd = sb("sd", [P, 2, 2])
        zmv = sb("zmv", [P, R + 1, 2])
        bn = sb("bn", [P, 4, R + 1])
        eps_c = sb("eps_c", [P, 1])
        ranges = sb("ranges", [P, 3, CHUNKS])
        ranges_i = sb("ranges_i", [P, CHUNKS], I32)
        ptab_f = sb("ptab_f", [P, 6 * CHUNKS])
        wsb = {k: sb("w_" + k, list(a.shape)) for k, a in w.items()}
        relv = sb("relv", [P, 4, R + 1])
        relbias = sb("relbias", [P, 2])
        ps = ctx.enter_context(nc.psum_tensor("ps", [P, 8, 512], F32))

        src_in, edges_in, weights_in, setup_done = sem("src_in"), sem("edges_in"), sem("weights_in"), sem("setup_done")
        iotas, ident_ok, minmax_ok, spread_ok, rows_sum = sem("iotas"), sem("ident_ok"), sem("minmax_ok"), sem("spread_ok"), sem("rows_sum")
        fence = {e: sem("fence_" + e) for e in ("pool", "act", "pe", "dve", "sp")}

        class PassSems:
            def __init__(self, tag):
                self.gathered = [sem(f"gathered{tag}{q}") for q in range(G)]
                self.staged = sem(f"staged{tag}")
                self.onehot = sem(f"onehot{tag}")
                self.used = sem(f"used{tag}")
                self.added = sem(f"added{tag}")

        stat, dyn = PassSems("_s"), PassSems("_d")
        acc_zero = sem("acc_zero")
        x_onehot, x_sum = sem("x_onehot"), sem("x_sum")
        attr_in, radial_in = [sem(f"attr_in{q}") for q in range(G)], [sem(f"radial_in{q}") for q in range(G)]
        h2_stored = [sem("h2_stored0"), sem("h2_stored1")]
        h1_sum, h1_done, h2_sum, h2_done = sem("h1_sum"), sem("h1_done"), sem("h2_sum"), sem("h2_done")
        rad_sum, scaled, dots_ok = sem("rad_sum"), sem("scaled"), sem("dots_ok")
        mean_ok, sum_ok, relu_ok, min_ok, evac_ok = sem("mean_ok"), sem("sum_ok"), sem("relu_ok"), sem("min_ok"), sem("evac_ok")
        turn_ok, row_ok, kept_ok = sem("turn_ok"), sem("row_ok"), sem("kept_ok")
        stored = [sem(f"stored{q}") for q in range(4)]
        x_in = [sem(f"x_in{q}") for q in range(4)]
        feat_ok, feat_stored = sem("feat_ok"), [sem(f"feat_stored{q}") for q in range(4)]
        feat_sum, rdeg_ok, cleared = sem("feat_sum"), sem("rdeg_ok"), [sem("cleared0"), sem("cleared1")]
        res_ok, lnst_ok, mv_ok, sd_ok, rstd_ok = sem("res_ok"), sem("lnst_ok"), sem("mv_ok"), sem("sd_ok"), sem("rstd_ok")
        back_ok, cur_ok = sem("back_ok"), sem("cur_ok")
        z_sum, z_ok, z_stat, z_act = sem("z_sum"), sem("z_ok"), sem("z_stat"), sem("z_act")
        z_scaled, z_dve = sem("z_scaled"), sem("z_dve")
        z_out = [sem(f"z_out{q}") for q in range(4)]
        z_in = [sem(f"z_in{q}") for q in range(4)]
        relw_in, bn_mv, bn_sd, bn_ok = sem("relw_in"), sem("bn_mv"), sem("bn_sd"), sem("bn_ok")
        chain = sem("chain")

        ALL = ["L0a", "L0b", "L1", "L2a", "L2b", "L3a", "L3b", "L3c"]
        order = ALL[:[0, 2, 3, 5, 8][layers]]
        final = order[-1]
        SAGE = ["L0a", "L0b", "L3a", "L3b", "L3c"]
        KEEP = ["L0a", "L2a", "L3a", "L3b"]
        PRELU = ["L3a", "L3b", "L3c"]
        NORM = ["L0b", "L1", "L2b", "L3c"]
        REL = ["L2a", "L2b"]
        ZEROED = ["L0a", "L1", "L2a", "L2b"]
        PASS = {"L0a": 0, "L0b": NG, "L1": 2 * NG, "L3a": 3 * NG, "L3b": 4 * NG, "L3c": 5 * NG}
        PASS_BLOCKS = {"L0a": 2, "L0b": 1, "L1": 2, "L3a": 1, "L3b": 1, "L3c": 1}
        TABLE = {"L0a": x, "L0b": tab_hid, "L1": tab_feat, "L2a": tab_x2, "L2b": tab_h2,
                 "L3a": tab_x3, "L3b": tab_h3[0], "L3c": tab_h3[1]}
        ROWS = {"L0a": tab_hid, "L0b": tab_x1, "L1": tab_x2, "L2a": tab_h2,
                "L2b": tab_x3, "L3a": tab_h3[0], "L3b": tab_h3[1], "L3c": None}
        RESIDUAL = {"L0b": x, "L1": tab_x1, "L2b": tab_x2, "L3c": tab_x3}
        PER4 = [len(range(q, NT, 4)) for q in range(4)]

        def count(stage, T, of=ALL):
            return NT * of.index(stage) + T + 1

        def place_count(stage, q, k, of=ALL):
            return 16 * (PER4[q] * of.index(stage) + k + 1)

        def before(stage):
            return ALL[ALL.index(stage) - 1]

        def feat_rows(q):
            return t_a[:, q % 2, P * (1 + q // 2):P * (2 + q // 2)]

        def feats_stored(eng):
            for q in range(4):
                eng.wait_ge(feat_stored[q], 16 * PER4[q])

        def cols(T, n=P):
            return slice(T * P, T * P + n) if isinstance(T, int) else bass.ds(T * P, n)

        def early(T, buffers=2):
            return isinstance(T, int) and T < buffers

        def mark(eng, name):
            eng.sem_inc(fence[name], 1)

        def tiles(eng, steps, T0=0, T1=NT):
            lags = max(lag for lag, _ in steps)

            def at(T, i):
                for lag, step in steps:
                    t = T - lag
                    if i is not None:
                        step(i * 4 + t, t % 2, i * 2 + t // 2, t % 4, i + t // 4)
                    elif T0 <= t < T1:
                        step(t, t % 2, t // 2, t % 4, t // 4)

            first = T0 + 4 + lags
            fours = (T1 - 1 - first) // 4
            for T in range(T0, first):
                at(T, None)
            with eng.Fori(0, fours) as i:
                for T in range(first, first + 4):
                    at(T, i)
            for T in range(first + 4 * fours, T1 + lags):
                at(T, None)

        def rows_stored(eng, stage):
            for q in range(4):
                eng.wait_ge(stored[q], place_count(stage, q, PER4[q] - 1))

        def chunk_values(eng, layer, c):
            k = 3 * (layer * CHUNKS + c)
            g0 = eng.value_load(ptab[0:1, k:k + 1], min_val=0, max_val=6 * NG)
            g1 = eng.value_load(ptab[0:1, k + 1:k + 2], min_val=0, max_val=6 * NG)
            u0 = eng.value_load(ptab[0:1, k + 2:k + 3], min_val=0, max_val=NU - G)
            return g0, g1, u0

        def static_groups(eng, name, body, peel_last=False):
            g0 = PASS[name]
            with eng.Fori(0, NG - peel_last) as i:
                body(i + g0, i * G, False)
            if peel_last:
                body(g0 + NG - 1, (NG - 1) * G, True)

        def chunk_groups(eng, layer, c, body, peel_last=False):
            g0, g1, u0 = chunk_values(eng, layer, c)
            end = g1 if peel_last else eng.snap(g1 + 1)
            with eng.Fori(g0, end) as g:
                body(g, eng.snap((g - g0) * G + u0).with_bounds(min_val=0, max_val=NU - (2 if peel_last else 1) * G), False)
            if peel_last:
                body(g1, eng.snap((g1 - g0) * G + u0).with_bounds(min_val=0, max_val=NU - G), True)
            return g1

        def first_group(eng, layer, c, body):
            g0, _, u0 = chunk_values(eng, layer, c)
            body(g0, u0, False)

        def later_groups(eng, layer, c, body):
            g0, g1, u0 = chunk_values(eng, layer, c)
            with eng.Fori(g0, g1) as g:
                body(eng.snap(g + 1), eng.snap((g - g0) * G + u0).with_bounds(min_val=0, max_val=NU - 2 * G) + G, False)

        def acc_halves(stage):
            if stage in REL:
                total = (CHUNK_TILES[0] * P + W) * R
                return arena[:, 0:total // 2], arena[:, total // 2:total]
            return arena[:, 0:ACCW], arena[:, ACCW:PASS_BLOCKS[stage] * ACCW]

        def z_ring(q):
            n = (R + 1) * D
            return t_a[:, q, :] if q < 2 else onehot[:].rearrange("p b t c -> p (b t c)")[:, (q - 2) * n:(q - 1) * n]

        def half_of_acc(t, half):
            n = P * R // 2
            at = t * (2 * n) + half * n
            return arena[:, at:at + n] if isinstance(t, int) else arena[:, bass.ds(at, n)]

        def window(eng, kind, u):
            return eng.value_load(win[0:1, kind, u:u + 1] if isinstance(u, int) else win[0:1, kind, bass.ds(u, 1)],
                                  min_val=0, max_val=(NP << 8) + 255)

        ps_flat = ps[:].rearrange("p b c -> p (b c)")
        X_BANK, H1_BANK, H2_BANK = 7, 4, 5
        RAD_BANKS = (5, 6)

        def sums_shape(name):
            return (1, W * R) if name in REL else (PASS_BLOCKS[name], W)

        def bank(name, q):
            blocks, width = sums_shape(name)
            return ps[:, q, 0:blocks * width]

        def rad_ps(b, t):
            at = (t % 2 * 2 + t // 2) * 4 * MUL
            return ps[:, RAD_BANKS[b], at:at + 4 * MUL]

        def acc_at(name, node):
            if name in REL:
                return arena[:, bass.ds(node * R, W * R)]
            return acc3[:, 0:PASS_BLOCKS[name], bass.ds(node, W)]

        def shaped(name, ap):
            if name in REL:
                return ap
            return ap.rearrange("p (k c) -> p k c", k=PASS_BLOCKS[name])

        block = ctx.enter_context(nc.Block())

        @block.sync
        def _(sp):
            sp.dma_start(src_sb[:], src).then_inc(src_in, 16)
            for to, of in [(arena[:, 0:ETP].bitcast(I32), dst),
                           (arena[:, ETP:2 * ETP].bitcast(I32), etype),
                           (arena[0:TROWS, 2 * ETP:2 * ETP + UPP * UNIT * P].bitcast(I32), dst_tiles)]:
                sp.dma_start(to, of).then_inc(edges_in, 16)
            for to, of in [(cur[:], x_t), *((wsb[k][:], w[k]) for k in wsb)]:
                sp.dma_start(to, of).then_inc(weights_in, 16)

            def z_ap(layer, T):
                if isinstance(T, int):
                    return z_dram[layer, T, :, :]
                return z_dram[layer, bass.ds(T, 1), :, :].rearrange("a p c -> (a p) c")

            def unit_cols(u, n):
                return slice(u * n, (u + 1) * n) if isinstance(u, int) else bass.ds(u * n, n)

            def load_attr(u, q):
                sp.dma_start(attr[:, q, :], ea8[:, unit_cols(u, HALF)]).then_inc(attr_in[q], 16)

            def load_radial(u, q):
                sp.dma_start(h2_in[:, q, :], h2_dram[:, unit_cols(u, HALF)]).then_inc(radial_in[q], 16)
                sp.dma_start(ea[:, q, :, :].rearrange("p t k -> p (t k)"), ea4[:, unit_cols(u, UNIT * 4)]
                             ).then_inc(radial_in[q], 16)

            for stage in order:
                layer = int(stage == "L2b")

                def store_rows(T, b, h, q, k):
                    sp.wait_ge(row_ok, count(stage, T))
                    if stage == final:
                        n = LAST if isinstance(T, int) and T == NT - 1 else P
                        sp.dma_start(out[cols(T, n), :], rowt[0:n, q, :]).then_inc(stored[q], 16)
                    else:
                        sp.dma_start(ROWS[stage][cols(T), :], rowt[:, q, :]).then_inc(stored[q], 16)

                def store_feat(T, b, h, q, k):
                    sp.wait_ge(feat_ok, T + 1)
                    sp.dma_start(tab_feat[cols(T), :], feat_rows(q)).then_inc(feat_stored[q], 16)

                def store_z(T, b, h, q, k):
                    sp.wait_ge(z_ok, count(stage, T, REL))
                    sp.dma_start(z_ap(layer, T), z_ring(q)).then_inc(z_out[q], 16)

                def load_z(T, b, h, q, k):
                    if not early(T, 4):
                        sp.wait_ge(sum_ok, count(stage, T - 4))
                    sp.dma_start(zb[:, q, :], z_ap(layer, T)).then_inc(z_in[q], 16)

                if stage == "L0b" and layers > 1:
                    for q in range(G):
                        load_attr(q, q)
                    with sp.Fori(0, NG) as i:
                        for q in range(G):
                            u = i * G + q
                            sp.wait_ge(h1_sum, u + 1)
                            mark(sp, "sp")
                            load_attr(u + G, q)
                            sp.wait_ge(h2_done, u + 1)
                            mark(sp, "sp")
                            sp.dma_start(h2_dram[:, unit_cols(u, HALF)], h2[:, q % 2, :]).then_inc(h2_stored[q % 2], 16)
                if stage == "L1":
                    for b in range(2):
                        sp.wait_ge(h2_stored[b], 16 * NG * G // 2)
                    for q in range(G):
                        sp.wait_ge(attr_in[q], 16 * (NG + 1))
                        load_radial(q, q)
                    with sp.Fori(0, NG - 1) as i:
                        for q in range(G):
                            sp.wait_ge(rad_sum, i * G + q + 1)
                            mark(sp, "sp")
                            sp.wait_ge(stat.onehot, (i + PASS["L1"]) * G + q + 1)
                            mark(sp, "sp")
                            load_radial(i * G + q + G, q)
                if stage in REL:
                    if layer:
                        sp.wait_ge(evac_ok, count("L2a", NT - 1))
                    else:
                        sp.wait_ge(turn_ok, count("L1", NT - 1))
                    for to, of in ((relw1, "W1"), (relw2, "W2"), (relv[:], "v"), (relbias[:, 0:1], "bias")):
                        sp.dma_start(to, w_rel[layer][of]).then_inc(relw_in, 16)
                    for c in range(CHUNKS):
                        tiles(sp, [(0, store_z)], CHUNK_T0[c], CHUNK_T0[c + 1])
                    for q in range(4):
                        sp.wait_ge(z_out[q], place_count(stage, q, PER4[q] - 1, REL))
                steps = [(0, load_z)] * (stage in REL)
                if stage in NORM:
                    steps += [(7 if stage in REL else 5, store_rows)]
                    if stage == "L0b" and layers > 1:
                        steps.append((7, store_feat))
                else:
                    steps += [(6 if stage in REL else 3, store_rows)]
                tiles(sp, steps)
            rows_stored(sp, final)
            if layers > 1:
                feats_stored(sp)

        @block.gpsimd
        def _(pool):
            pool.iota(iota_i, [[1, W * R]], channel_multiplier=0)
            pool.iota(arena[:, 17000:17000 + P].bitcast(I32), [[1, P]], channel_multiplier=-1)
            pool.iota(arena[:, 17200:17200 + NU].bitcast(I32), [[1, NU]], channel_multiplier=0).then_inc(iotas, 1)

            def gathers(name, sems):
                def body(g, u, last):
                    for q in range(G):
                        pool.wait_ge(sems.staged, g * G + q + 1)
                        mark(pool, "pool")
                        for s in range(q * UNIT, (q + 1) * UNIT):
                            pool.indirect_dma_start(ring[:, s, :], None, TABLE[name],
                                                    bass.IndirectOffsetOnAxis(slot_idx[:, s:s + 1], 0)
                                                    ).then_inc(sems.gathered[q], 16)
                return body

            for stage in order:
                def keep(T, b, h, q, k):
                    pool.wait_ge(evac_ok, count(stage, T))
                    mark(pool, "pool")
                    if stage == "L0a":
                        for k in range(2):
                            last = pool.tensor_copy(acc3[:, 1 + k, cols(T)], t_y[:, b, k * P:(k + 1) * P])
                        last.then_inc(kept_ok, 1)
                    else:
                        pool.tensor_copy(cur[:, cols(T)], t_y[:, b, 0:P]).then_inc(kept_ok, 1)

                if stage != "L0a":
                    rows_stored(pool, before(stage))
                if stage == "L1":
                    feats_stored(pool)
                if stage in REL:
                    pool.wait_ge(setup_done, 1)
                    for c in range(CHUNKS):
                        layer = int(stage == "L2b")
                        if c == 0:
                            first_group(pool, layer, c, gathers(stage, dyn))
                        later_groups(pool, layer, c, gathers(stage, dyn))
                        if c + 1 == CHUNKS:
                            continue
                        first_group(pool, layer, c + 1, gathers(stage, dyn))

                        def clear(T, b, h, q, k):
                            pool.wait_ge(z_sum, count(stage, T, REL))
                            mark(pool, "pool")
                            pool.tensor_copy(half_of_acc(T - CHUNK_T0[c], 0).rearrange("p (r n) -> p r n", n=P),
                                             zeros[:].unsqueeze(1).to_broadcast([P, R // 2, P])).then_inc(cleared[0], 1)

                        tiles(pool, [(0, clear)], CHUNK_T0[c], CHUNK_T0[c + 1])
                else:
                    static_groups(pool, stage, gathers(stage, stat))
                def load_residual(T, b, h, q, k):
                    if not early(T, 4):
                        pool.wait_ge(res_ok, count(stage, T - 4, NORM))
                    mark(pool, "pool")
                    pool.dma_start(t_x[:, q, :], RESIDUAL[stage][cols(T), :]).then_inc(x_in[q], 16)

                if stage in KEEP:
                    tiles(pool, [(0, keep)])
                elif stage in NORM:
                    tiles(pool, [(0, load_residual)])

        @block.scalar
        def _(act):
            act.wait_ge(src_in, 16)

            def stage_idx(sems, g, u, q):
                act.wait_ge(sems.used, g * G + q + 1)
                mark(act, "act")
                q4 = q % G * UNIT
                of = slice((u + q) * UNIT, (u + q + 1) * UNIT) if isinstance(u, int) else bass.ds((u + q) * UNIT, UNIT)
                nc.scalar.copy(slot_idx[:, q4:q4 + UNIT], src_sb[:, of]).then_inc(sems.staged, 1)

            def zero_acc(stage):
                to = acc_halves(stage)[1]
                nc.scalar.copy(to, zeros[:, 0:1].to_broadcast(list(to.shape))).then_inc(acc_zero, 1)

            def indices(sems):
                def body(g, u, last):
                    for q in range(G):
                        stage_idx(sems, g, u, q)
                return body

            def gelu1(u, b):
                act.wait_ge(h1_sum, u + 1)
                if not isinstance(u, int) or u > 1:
                    act.wait_ge(h2_sum, u - 1)
                mark(act, "act")
                nc.scalar.activation(h1[:, b, :], ps[:, H1_BANK, 0:HALF], ACT.Gelu_apprx_tanh,
                                     scale=float(1.0 / np.sqrt(RADIAL))).then_inc(h1_done, 1)

            def gelu2(u, b, h):
                act.wait_ge(h2_sum, u + 1)
                if not isinstance(h, int) or h > 0:
                    act.wait_ge(h2_stored[b], h * 16)
                mark(act, "act")
                nc.scalar.activation(h2[:, b, :], ps[:, H2_BANK, 0:HALF], ACT.Gelu_apprx_tanh,
                                     scale=float(1.0 / np.sqrt(HID1))).then_inc(h2_done, 1)

            def hidden_group(i, last):
                for q in range(G):
                    u = i * G + q
                    gelu1(u + 1, (q + 1) % 2)
                    gelu2(u, q % 2, i * 2 + q // 2)
                    if q + 3 < G or not last:
                        stage_idx(stat, i + PASS["L0b"], i * G, q + 3)

            def scale_rad(u, q):
                b = q % 2
                act.wait_ge(rad_sum, u + 1)
                act.wait_ge(stat.onehot, u + (PASS["L1"] * G - 1))
                mark(act, "act")
                for t in range(UNIT):
                    for i in range(4):
                        of = rad_ps(b, t)[:, 0:2 * MUL] if i == 0 else rad_ps(b, t)[:, 2 * MUL:4 * MUL]
                        last = nc.scalar.activation(qs[:, b, t, i, :, :].rearrange("p a c -> p (a c)"), of, ACT.Copy,
                                                    scale=ea[:, q % G, t, i:i + 1])
                last.then_inc(scaled, 1)

            def radial(g, u, last):
                for q in range(G):
                    if q + 1 < G or not last:
                        scale_rad(u + q + 1, q + 1)
                    if q + 3 < G or not last:
                        stage_idx(stat, g, u, q + 3)

            for stage in order:
                layer = int(stage == "L2b")

                if stage == "L1":
                    feats_stored(act)
                    for q in range(3):
                        stage_idx(stat, PASS["L1"], 0, q)
                    zero_acc(stage)
                    scale_rad(0, 0)
                    static_groups(act, stage, radial, peel_last=True)
                elif stage == "L0b" and layers > 1:
                    for q in range(3):
                        stage_idx(stat, PASS["L0b"], 0, q)
                    gelu1(0, 0)
                    hidden_group(0, False)
                    with act.Fori(1, NG - 1) as i:
                        hidden_group(i, False)
                    hidden_group(NG - 1, True)
                elif stage in REL:
                    def bias_z(T, b, h, q, k):
                        act.wait_ge(z_sum, count(stage, T, REL))
                        if not early(T, 4):
                            act.wait_ge(z_out[q], place_count(stage, q, k - 1, REL))
                            act.wait_ge(z_stat, count(stage, T - 4, REL))
                        mark(act, "act")
                        for r in range(R + 1):
                            last = nc.scalar.activation(z_ring(q)[:, r * D:(r + 1) * D],
                                                        ps_flat[:, 1536 * b + r * D:1536 * b + (r + 1) * D],
                                                        ACT.Identity, bias=relv[:, 0, r:r + 1])
                        last.then_inc(z_ok, 1)

                    for c in range(CHUNKS):
                        if c == 0:
                            first_group(act, layer, c, indices(dyn))
                            zero_acc(stage)
                            act.wait_ge(relw_in, 64 * (layer + 1))
                        later_groups(act, layer, c, indices(dyn))
                        if c + 1 < CHUNKS:
                            first_group(act, layer, c + 1, indices(dyn))
                        tiles(act, [(0, bias_z)], CHUNK_T0[c], CHUNK_T0[c + 1])
                    act.wait_ge(bn_mv, layer + 1)
                    nc.scalar.activation(bn[:, 0, :], zmv[:, :, 1], ACT.Sqrt, bias=eps_c[:]).then_inc(bn_sd, 1)
                    act.wait_ge(bn_ok, layer + 1)
                elif stage == "L0a":
                    indices(stat)(0, 0, False)
                    act.wait_ge(setup_done, 1)
                    zero_acc(stage)
                    with act.Fori(1, NG) as i:
                        indices(stat)(i, i * G, False)
                else:
                    static_groups(act, stage, indices(stat))

                def relu_z(T, b, h, q, k):
                    act.wait_ge(z_in[q], (k + 1 + PER4[q] * layer) * 16)
                    mark(act, "act")
                    for r in range(ACT_RELUS):
                        last = nc.scalar.activation(zb[:, q, r * D:(r + 1) * D], zb[:, q, r * D:(r + 1) * D],
                                                    ACT.Relu, bias=bn[:, 3, r:r + 1], scale=bn[:, 2, r:r + 1])
                    last.then_inc(z_act, 1)

                def evacuate(T, b, h, q, k):
                    act.wait_ge(sum_ok, count(stage, T))
                    if stage in PRELU:
                        if not early(T):
                            act.wait_ge(evac_ok, count(stage, T - 2))
                        i = PRELU.index(stage)
                        mark(act, "act")
                        nc.scalar.activation(t_b[:, b, :], ps[:, b, 0:P], ACT.Relu, bias=wsb["L3_b"][:, i:i + 1]
                                             ).then_inc(relu_ok, 1)
                        return
                    if not early(T):
                        act.wait_ge(turn_ok, count(stage, T - 2))
                        if stage in KEEP:
                            act.wait_ge(kept_ok, count(stage, T - 2, KEEP))
                    mark(act, "act")
                    to = t_y[:, b, 0:P]
                    if stage == "L0a":
                        for k in range(2):
                            last = nc.scalar.activation(t_y[:, b, k * P:(k + 1) * P], ps[:, b, k * P:(k + 1) * P], ACT.Relu,
                                                        bias=wsb["L0_b1"][:, k:k + 1])
                        last.then_inc(evac_ok, 1)
                    elif stage == "L1":
                        nc.scalar.copy(to, ps[:, b, 0:P]).then_inc(evac_ok, 1)
                    else:
                        bias = wsb["L0_b2"][:, 0:1] if stage == "L0b" else relbias[:, 1:2]
                        nc.scalar.activation(to, ps[:, b, 0:P], ACT.Relu if stage == "L2a" else ACT.Identity,
                                             bias=bias).then_inc(evac_ok, 1)

                def copy_rows(T, b, h, q, k):
                    act.wait_ge(turn_ok, count(stage, T))
                    if ALL.index(stage) or not early(T, 4):
                        act.wait_ge(stored[q], place_count(stage, q, k - 1))
                    mark(act, "act")
                    nc.scalar.copy(rowt[:, q, :], ps[:, 2 + b, 0:P]).then_inc(row_ok, 1)

                def root(T, b, h, q, k):
                    act.wait_ge(mv_ok, count(stage, T, NORM))
                    if not early(T):
                        act.wait_ge(rstd_ok, count(stage, T - 2, NORM))
                    mark(act, "act")
                    nc.scalar.activation(sd[:, b, 0:1], mv[:, b, 1:2], ACT.Sqrt, bias=eps_c[:]).then_inc(sd_ok, 1)

                def copy_cur(T, b, h, q, k):
                    act.wait_ge(back_ok, count(stage, T, NORM))
                    if stage == "L0b" and not early(T):
                        act.wait_ge(feat_sum, T - 1)
                    mark(act, "act")
                    if stage == "L0b":
                        nc.scalar.copy(t_m[:, b, :], ps[:, 4 + b, 0:P])
                    nc.scalar.copy(cur[:, cols(T)], ps[:, 4 + b, 0:P]).then_inc(cur_ok, 1)

                def copy_feat(T, b, h, q, k):
                    act.wait_ge(feat_sum, T + 1)
                    if not early(T, 4):
                        act.wait_ge(feat_stored[q], k * 16)
                    mark(act, "act")
                    nc.scalar.copy(feat_rows(q), ps[:, 6 + b, 0:P]).then_inc(feat_ok, 1)

                steps = []
                if stage in REL:
                    steps.append((0, relu_z))
                steps.append((1 if stage in REL else 0, evacuate))
                if stage in NORM:
                    lag = 3 if stage in REL or stage in PRELU else 2
                    steps.append((lag, root))
                    if stage != final:
                        steps.append((lag + 3, copy_cur))
                        if stage == "L0b":
                            steps.append((lag + 4, copy_feat))
                else:
                    steps.append((3 if stage in REL or stage in PRELU else 2, copy_rows))
                tiles(act, steps)

        @block.tensor
        def _(pe):
            x_n = pe.alloc_register("pe_extra_windows")
            pe.reg_mov(x_n, 0)
            pe.sem_inc(stat.used, G)
            pe.sem_inc(dyn.used, G)
            pe.wait_ge(spread_ok, 1)
            for v in range(2):
                last = pe.matmul(ps[:, v, 0:NU], ones[0:TROWS, :], arena[0:TROWS, 5000 + v * NU:5000 + (v + 1) * NU],
                                 start=True, stop=True)
            last.then_inc(rows_sum, 1)
            pe.wait_ge(setup_done, 1)

            def sums(name, to, q, t, hot, first):
                def product(block, rows, start):
                    return pe.matmul(block, rows, hot, start=start, stop=True, skip_group_check=True)

                row = ring[:, q * UNIT + t, :]
                if name == "L1":
                    for k in range(2):
                        last = product(to[:, k * W:(k + 1) * W], msg[:, q % 2, t, k * D:(k + 1) * D], first and k == 0)
                elif name == "L0a":
                    product(to[:, 0:W], row, first)
                    last = product(to[:, W:2 * W], ones[:], False)
                else:
                    last = product(to, row, first)
                return last

            def sum_unit(name, kind, sems, g, u, q, between=lambda: None):
                width = W * R if name in REL else W
                windows = pe.snap(window(pe, kind, u + q) & 255)
                pe.wait_ge(sems.gathered[q], (g + 1) * (16 * UNIT))
                pe.wait_ge(sems.onehot, g * G + q + 1)
                with pe.If(windows > 1):
                    for t in range(UNIT):
                        with pe.Fori(1, windows):
                            pe.reg_add(x_n, x_n, 1)
                            pe.wait_ge(x_onehot, pe.snap(x_n))
                            mark(pe, "pe")
                            sums(name, ps[:, X_BANK, 0:sums_shape(name)[0] * width], q, t, xone[:, 0:width], True
                                 ).then_inc(x_sum, 1)
                pe.wait_ge(sems.added, g * G + q + 1)
                mark(pe, "pe")
                for t in range(UNIT):
                    if t == UNIT // 2:
                        between()
                    last = sums(name, bank(name, q), q, t, onehot[:, q % 2, t, 0:width], t == 0)
                last.then_inc(sems.used, 1)

            def sum_group(name, kind, sems):
                def body(g, u, last):
                    for q in range(G):
                        sum_unit(name, kind, sems, g, u, q)
                return body

            def hidden1(u, q, h):
                pe.wait_ge(attr_in[q], (h + 1) * 16)
                if not isinstance(u, int) or u > 0:
                    pe.wait_ge(h1_done, u)
                mark(pe, "pe")
                pe.matmul(ps[:, H1_BANK, 0:HALF], wsb["mlp1"][:], attr[:, q, :], start=True, stop=True).then_inc(h1_sum, 1)

            def hidden2(u, b):
                pe.wait_ge(h1_done, u + 1)
                if not isinstance(u, int) or u > 0:
                    pe.wait_ge(h2_done, u)
                mark(pe, "pe")
                pe.matmul(ps[:, H2_BANK, 0:HALF], wsb["mlp2"][:], h1[:, b, :], start=True, stop=True).then_inc(h2_sum, 1)

            def hidden_group(i):
                for q in range(G):
                    u = i * G + q
                    hidden1(u + 1, (q + 1) % G, i + (q + 1) // G)
                    sum_unit("L0b", 0, stat, i + PASS["L0b"], i * G, q, lambda: hidden2(u, q % 2))

            def radial(u, q, h):
                pe.wait_ge(radial_in[q], (h + 1) * 32)
                pe.wait_ge(stat.onehot, u + (PASS["L1"] * G - 1))
                mark(pe, "pe")
                for c in range(2):
                    last = pe.matmul(ps[:, RAD_BANKS[q % 2], c * HALF:(c + 1) * HALF], h2_in[:, q, c * P:(c + 1) * P],
                                     wsb["mlp3"][:], start=True, stop=True)
                last.then_inc(rad_sum, 1)

            def radial_group(i, last):
                for q in range(G):
                    if q + 1 < G or not last:
                        radial(i * G + q + 1, (q + 1) % G, i + (q + 1) // G)
                    sum_unit("L1", 0, stat, i + PASS["L1"], i * G, q)

            for stage in order:
                layer = int(stage == "L2b")
                if stage == "L1":
                    pe.wait_ge(feat_ok, NT)
                    pe.wait_ge(cur_ok, count("L0b", NT - 1, NORM))
                    radial(0, 0, 0)
                    with pe.Fori(0, NG - 1) as i:
                        radial_group(i, False)
                    radial_group(NG - 1, True)
                    pe.wait_ge(stat.added, (PASS[stage] + NG + 1) * G)
                elif stage == "L0b" and layers > 1:
                    hidden1(0, 0, 0)
                    hidden_group(0)
                    with pe.Fori(1, NG) as i:
                        hidden_group(i)
                    pe.wait_ge(h1_done, NG * G + 1)
                elif stage in REL:
                    def z_tile(T, b, h, q, k):
                        if not (early(T) and layer == 0):
                            pe.wait_ge(z_ok, count(stage, T - 2, REL))
                        t = T - CHUNK_T0[c]
                        mark(pe, "pe")
                        for r in range(R + 1):
                            if r < R:
                                node = t * (P * R) + r
                                rows = arena[:, node:node + (P - 1) * R + 1:R] if isinstance(t, int) else \
                                    arena[:, bass.ds(t * (P * R), P * R)].rearrange("p (n r) -> p n r", r=R)[:, :, r]
                            else:
                                rows = cur[:, cols(T)]
                            last = pe.matmul(ps_flat[:, 1536 * b + r * D:1536 * b + (r + 1) * D], relw1[:, r, :], rows,
                                             start=True, stop=True)
                        last.then_inc(z_sum, 1)

                    pe.wait_ge(relw_in, 64 * (layer + 1))
                    if not layer:
                        pe.wait_ge(cur_ok, count("L1", NT - 1, NORM))
                    else:
                        pe.wait_ge(kept_ok, count("L2a", NT - 1, KEEP))
                    for c in range(CHUNKS):
                        g1 = chunk_groups(pe, layer, c, sum_group(stage, 1 + c, dyn))
                        pe.wait_ge(dyn.added, pe.snap(g1 * G + 2 * G))
                        mark(pe, "pe")
                        tiles(pe, [(0, z_tile)], CHUNK_T0[c], CHUNK_T0[c + 1])
                    pe.wait_ge(z_ok, count(stage, NT - 1, REL))
                else:
                    static_groups(pe, stage, sum_group(stage, 0, stat))

                def node_sums(T, b, h, q, k):
                    if stage in SAGE:
                        pe.wait_ge(mean_ok, count(stage, T, SAGE))
                    elif stage in REL:
                        pe.wait_ge(z_act, count(stage, T, REL))
                        pe.wait_ge(z_dve, count(stage, T, REL))
                    if not early(T):
                        pe.wait_ge(evac_ok, count(stage, T - 2))
                    mark(pe, "pe")
                    mean, to = t_a[:, b, 0:P], ps[:, b, 0:P]
                    if stage == "L0a":
                        for k in range(2):
                            o = ps[:, b, k * P:(k + 1) * P]
                            pe.matmul(o, wsb["L0_W1l"][:, k * P:(k + 1) * P], mean, start=True, stop=False)
                            last = pe.matmul(o, wsb["L0_W1r"][:, k * P:(k + 1) * P], cur[:, cols(T)], start=False, stop=True)
                        last.then_inc(sum_ok, 1)
                    elif stage == "L0b":
                        pe.matmul(to, ident[:], mean, start=True, stop=False)
                        for k in range(2):
                            last = pe.matmul(to, wsb["L0_W2r"][:, k * P:(k + 1) * P], acc3[:, 1 + k, cols(T)],
                                             start=False, stop=(k == 1))
                        last.then_inc(sum_ok, 1)
                    elif stage == "L1":
                        pe.matmul(to, wsb["Fself"][:], cur[:, cols(T)], start=True, stop=False)
                        for k in range(2):
                            last = pe.matmul(to, wsb["M"][:, k * D:(k + 1) * D], acc3[:, k, cols(T)], start=False, stop=(k == 1))
                        last.then_inc(sum_ok, 1)
                    elif stage in REL:
                        for r in range(R + 1):
                            last = pe.matmul(to, relw2[:, r, :], zb[:, q, r * D:(r + 1) * D], start=(r == 0), stop=(r == R))
                        last.then_inc(sum_ok, 1)
                    else:
                        i = PRELU.index(stage)
                        pe.matmul(to, wsb["L3_Wl"][:, i * P:(i + 1) * P], mean, start=True, stop=False)
                        pe.matmul(to, wsb["L3_Wr"][:, i * P:(i + 1) * P], cur[:, cols(T)], start=False, stop=True
                                  ).then_inc(sum_ok, 1)

                def turn(T, b, h, q, k):
                    pe.wait_ge(evac_ok, count(stage, T))
                    if not early(T):
                        if stage in NORM:
                            pe.wait_ge(res_ok, count(stage, T - 2, NORM))
                        else:
                            pe.wait_ge(row_ok, count(stage, T - 2))
                    mark(pe, "pe")
                    to = ps[:, 2 + b, 0:P]
                    if stage == "L0a":
                        for k in range(2):
                            last = pe.matmul(to, t_y[:, b, k * P:(k + 1) * P], wsb["L0_W2l"][:, k * P:(k + 1) * P],
                                             start=(k == 0), stop=(k == 1))
                    else:
                        last = pe.transpose(to, t_y[:, b, 0:P], ident[:])
                    last.then_inc(turn_ok, 1)

                def back(T, b, h, q, k):
                    pe.wait_ge(row_ok, count(stage, T))
                    if not early(T):
                        pe.wait_ge(cur_ok, count(stage, T - 2, NORM))
                    mark(pe, "pe")
                    pe.transpose(ps[:, 4 + b, 0:P], rowt[:, q, :], ident[:]).then_inc(back_ok, 1)

                def feat(T, b, h, q, k):
                    pe.wait_ge(cur_ok, count(stage, T, NORM))
                    if not early(T):
                        pe.wait_ge(feat_ok, T - 1)
                    mark(pe, "pe")
                    pe.matmul(ps[:, 6 + b, 0:P], t_m[:, b, :], wsb["F"][:], start=True, stop=True).then_inc(feat_sum, 1)

                if before(stage) in KEEP and stage not in REL:
                    pe.wait_ge(kept_ok, count(before(stage), NT - 1, KEEP))
                if stage == "L3a":
                    pe.wait_ge(cur_ok, count("L2b", NT - 1, NORM))
                steps = [(0, node_sums), (2 if stage in PRELU else 1, turn)]
                if stage in NORM and stage != final:
                    steps.append((5, back))
                    if stage == "L0b":
                        steps.append((6, feat))
                tiles(pe, steps)

        @block.vector
        def _(dve):
            x_n = dve.alloc_register("dve_extra_windows")
            dve.reg_mov(x_n, 0)
            n_chain = [0]

            def then(ins):
                n_chain[0] += 1
                ins.then_inc(chain, 1)
                dve.wait_ge(chain, n_chain[0])

            V = nc.vector

            dve.wait_ge(edges_in, 16 * 3)
            dve.wait_ge(iotas, 1)

            def area(at, n=ETP, parts=P, dt=F32):
                return arena[0:parts, at:at + n].bitcast(dt)

            UE = UNIT * P
            dst_i, et_i, tiles_i = area(0, dt=I32), area(ETP, dt=I32), area(2 * ETP, UPP * UE, TROWS, I32)
            tiles_f, far = area(3000, UPP * UE, TROWS), area(15000, UPP * UE, TROWS)
            spread = [area(5000 + v * NU, NU, TROWS) for v in range(2)]
            dst_f, seg_f, low, high = area(7000), area(8000), area(9000, NU), area(9300, NU)
            number = area(16100, NU)
            base, t1, t2, t3, t4 = [area(at, NTYPE * NU, dt=dt).rearrange("p (k u) -> p k u", k=NTYPE) for at, dt in
                                    ((11000, F32), (12000, F32), (14000, I32), (13000, F32), (9600, F32))]
            first_node = [0] + [t * P for t in CHUNK_T0[:-1]]
            end_node = [N] + [min(N, t * P) for t in CHUNK_T0[1:]]
            V.memset(ones[:], 1.0)
            V.memset(zeros[:], 0.0)
            V.memset(eps_c[:], EPS)
            V.tensor_copy(iota_w[:], iota_i)
            V.tensor_copy(number, area(17200, NU, dt=I32))
            V.tensor_copy(dst_f, dst_i)
            V.tensor_copy(tiles_f, tiles_i)
            then(V.tensor_scalar(ident[:], area(17000, P, dt=I32), 0.0, None, ALU.is_equal))
            V.tensor_scalar(far, tiles_f, 0.0, FAR, ALU.is_lt, ALU.mult)
            then(V.scalar_tensor_tensor(seg_f, dst_f, float(R), et_i, ALU.mult, ALU.add))
            then(V.tensor_tensor(far, far, tiles_f, ALU.add))
            per_unit = "p (k e) -> p k e"
            V.tensor_reduce(minmax[0:TROWS, 0, :], far.rearrange(per_unit, k=UPP), AX.X, ALU.min)
            then(V.tensor_reduce(minmax[0:TROWS, 1, :], tiles_f.rearrange(per_unit, k=UPP), AX.X, ALU.max))
            for v in range(2):
                last = V.tensor_tensor(spread[v].rearrange("p (q k) -> p q k", k=UPP),
                                       minmax[0:TROWS, v, :].unsqueeze(1).to_broadcast([TROWS, TROWS, UPP]),
                                       ident[0:TROWS, 0:TROWS].unsqueeze(2).to_broadcast([TROWS, TROWS, UPP]), ALU.mult)
            last.then_inc(spread_ok, 1)
            dve.wait_ge(rows_sum, 1)
            for v, row in enumerate((low, high)):
                last = V.tensor_copy(row, ps[:, v, 0:NU])
            then(last)

            def tiles_of(ap):
                return ap.rearrange("p (u t) -> p u t", t=UNIT)

            for k, (c0, c1) in enumerate(zip(first_node, end_node)):
                V.tensor_scalar(base[:, k, :], low, float(c0), float(c1 - 1), ALU.max, ALU.min)
                last = V.tensor_scalar(t1[:, k, :], high, 0.0, float(c1 - 1), ALU.max, ALU.min)
            then(last)
            for k in range(NTYPE):
                bases = base[:, k, :].unsqueeze(2).to_broadcast([P, NU, UNIT])
                if k == 0:
                    V.tensor_tensor(tiles_of(rel_seg[:, 0, :]), tiles_of(dst_f), bases, ALU.subtract)
                else:
                    V.scalar_tensor_tensor(tiles_of(rel_seg[:, k, :]), bases, -float(R), tiles_of(seg_f), ALU.mult, ALU.add)
            then(V.tensor_tensor(t1, t1, base, ALU.subtract))
            then(V.tensor_scalar(t2, t1, 0.0, float(W_RECIP), ALU.max, ALU.mult))
            then(V.tensor_scalar(t2, t2, 16, None, ALU.arith_shift_right))
            for k, (c0, c1) in enumerate(zip(first_node, end_node)):
                V.tensor_scalar(t1[:, k, :], t2[:, k, :], 1.0 - 256.0 * c0, None, ALU.add)
                last = V.tensor_scalar(t4[:, k, :], low, float(c1), None, ALU.is_lt)
            then(last)
            V.scalar_tensor_tensor(win[0:1, :, :], base[0:1], 256.0, t1[0:1], ALU.mult, ALU.add)
            for k in range(1, NTYPE):
                last = V.scalar_tensor_tensor(t4[:, k, :], high, float(first_node[k]), t4[:, k, :], ALU.is_ge, ALU.mult)
            then(last)
            has, part, numbers = t4[:, 1:, :], t3[:, 1:, :], number.unsqueeze(1).to_broadcast([P, CHUNKS, NU])
            then(V.scalar_tensor_tensor(part, numbers, 1.0, has, ALU.add, ALU.mult))
            then(V.tensor_reduce(ranges[:, 1, :], part, AX.X, ALU.max))
            then(V.tensor_scalar(part, has, -FAR, FAR, ALU.mult, ALU.add))
            then(V.tensor_tensor(part, part, numbers, ALU.add))
            then(V.tensor_reduce(ranges[:, 0, :], part, AX.X, ALU.min))
            then(V.tensor_tensor(ranges[:, 0, :], ranges[:, 0, :], ranges[:, 1, :], ALU.min))
            then(V.tensor_tensor(ranges[:, 2, :], ranges[:, 1, :], ranges[:, 0, :], ALU.subtract))
            then(V.tensor_scalar(ranges_i[:], ranges[:, 2, :], 1.0, float(G - 1), ALU.max, ALU.add))
            then(V.tensor_scalar(ranges_i[:], ranges_i[:], 2, None, ALU.arith_shift_right))
            then(V.tensor_copy(ranges[:, 2, :], ranges_i[:]))
            then(V.memset(ptab_f[:, 0:1], 0.0))
            for k in range(2 * CHUNKS):
                c = k % CHUNKS
                if k:
                    then(V.tensor_scalar(ptab_f[:, 3 * k:3 * k + 1], ptab_f[:, 3 * k - 2:3 * k - 1], 1.0, None, ALU.add))
                V.tensor_copy(ptab_f[:, 3 * k + 2:3 * k + 3], ranges[:, 0, c:c + 1])
                then(V.scalar_tensor_tensor(ptab_f[:, 3 * k + 1:3 * k + 2], ranges[:, 2, c:c + 1], -1.0,
                                            ptab_f[:, 3 * k:3 * k + 1], ALU.add, ALU.add))
            V.tensor_copy(ptab[:], ptab_f[:])
            dve.wait_ge(weights_in, 16 * (1 + len(wsb)))
            V.tensor_scalar(wsb["F"][:], wsb["F"][:], INV_MUL, None, ALU.mult)
            V.tensor_scalar(wsb["Fself"][:], wsb["Fself"][:], COS * INV_MUL, None, ALU.mult)
            V.tensor_scalar(wsb["M"][:, 0:D], wsb["M"][:, 0:D], CONV, None, ALU.mult)
            V.tensor_scalar(wsb["M"][0:96, D:2 * D], wsb["M"][0:96, D:2 * D], CONV, None, ALU.mult)
            then(V.tensor_scalar(wsb["M"][96:128, D:2 * D], wsb["M"][96:128, D:2 * D], CONV_DOT, None, ALU.mult))
            dve.sem_inc(stat.added, G)
            dve.sem_inc(dyn.added, G)
            dve.sem_inc(setup_done, 1)

            def build_unit(name, kind, sems, g, u, q):
                width, b, place = W * R if name in REL else W, q % 2, q % G
                dve.wait_ge(sems.used, g * G + q + (G - 1))
                segs = rel_seg[:, kind, (u + q) * UNIT:(u + q + 1) * UNIT] if isinstance(u, int) else \
                    rel_seg[:, kind, bass.ds((u + q) * UNIT, UNIT)]
                ins = V.tensor_tensor(onehot[:, b, :, 0:width], iota_w[:, 0:width].unsqueeze(1).to_broadcast([P, UNIT, width]),
                                      segs.unsqueeze(2).to_broadcast([P, UNIT, width]), ALU.is_equal)
                if name == "L1":
                    if not isinstance(u, int) or u + q > 0:
                        dve.wait_ge(sems.onehot, u + q + PASS["L1"] * G)
                    dve.wait_ge(sems.gathered[place], (g + (q // G + 1)) * (16 * UNIT))
                    dve.wait_ge(scaled, u + q + 1)
                    rows = ring[:, place * UNIT:(place + 1) * UNIT, :]
                    scalar, vector = rows[:, :, 0:MUL], rows[:, :, MUL:4 * MUL].rearrange("p t (i c) -> p t i c", i=3)
                    scalar3, w10 = [a.unsqueeze(2).to_broadcast([P, UNIT, 3, MUL]) for a in (scalar, qs[:, b, :, 0, 1, :])]

                    def threes(c):
                        return msg[:, b, :, c:c + 3 * MUL].rearrange("p t (i c) -> p t i c", i=3)

                    V.tensor_tensor(dots, qs[:, b, :, 1:4, 1, :], vector, ALU.mult).then_inc(dots_ok, 1)
                    V.tensor_tensor(msg[:, b, :, 0:MUL], qs[:, b, :, 0, 0, :], scalar, ALU.mult)
                    V.tensor_tensor(threes(MUL), w10, vector, ALU.mult)
                    V.tensor_tensor(threes(D), qs[:, b, :, 1:4, 0, :], scalar3, ALU.mult)
                    dve.wait_ge(dots_ok, u + q + 1)
                    mark(dve, "dve")
                    ins = V.tensor_reduce(msg[:, b, :, D + 3 * MUL:D + 4 * MUL], dots.rearrange("p t i c -> p t c i"),
                                          AX.X, ALU.add)
                ins.then_inc(sems.onehot, 1)

            def add_unit(name, kind, sems, g, u, q):
                width = W * R if name in REL else W
                v = window(dve, kind, u + q)
                top = (NT if name not in REL else CHUNK_TILES[kind - 1]) * P - 1
                node = dve.snap(v >> 8).with_bounds(min_val=0, max_val=top)
                windows = dve.snap(v & 255)
                with dve.If(windows > 1):
                    for t in range(UNIT):
                        dve.drain()
                        tile = (u + q) * UNIT + t
                        V.tensor_copy(xseg[:], rel_seg[:, kind, tile:tile + 1] if isinstance(u, int) else
                                      rel_seg[:, kind, bass.ds(tile, 1)])
                        with dve.Fori(1, windows) as i:
                            dve.drain()
                            V.tensor_scalar(xseg[:], xseg[:], -float(width), None, ALU.add)
                            dve.drain()
                            V.tensor_scalar(xone[:, 0:width], iota_w[:, 0:width], xseg[:], None, ALU.is_equal).then_inc(x_onehot, 1)
                            dve.reg_add(x_n, x_n, 1)
                            dve.wait_ge(x_sum, dve.snap(x_n))
                            mark(dve, "dve")
                            to = acc_at(name, dve.snap(node + i * W).with_bounds(min_val=0, max_val=top))
                            n = sums_shape(name)[0] * width
                            V.tensor_tensor(to, to, shaped(name, ps[:, X_BANK, 0:n]), ALU.add)
                    dve.drain()
                dve.wait_ge(sems.used, g * G + q + 1 + G)
                dve.wait_ge(sems.added, g * G + q + G)
                to = acc_at(name, node)
                V.tensor_tensor(to, to, shaped(name, bank(name, q)), ALU.add).then_inc(sems.added, 1)

            def pass_group(name, kind, sems):
                def body(g, u, last):
                    for q in range(G):
                        if q + 1 < G or not last:
                            build_unit(name, kind, sems, g, u, q + 1)
                        add_unit(name, kind, sems, g, u, q)
                return body

            for stage in order:
                layer = int(stage == "L2b")
                if stage != "L0a":
                    dve.wait_ge(turn_ok, count(before(stage), NT - 1))
                if stage in REL:
                    def z_stats(T, b, h, q, k):
                        dve.wait_ge(z_ok, count(stage, T, REL))
                        n = LAST if isinstance(T, int) and T == NT - 1 else P
                        mark(dve, "dve")
                        for r in range(R + 1):
                            to = zst[:, T, r, :] if isinstance(T, int) else \
                                zst[:, bass.ds(T, 1), r, :].rearrange("p a c -> p (a c)")
                            last = V.bn_stats(to, z_ring(q)[:, r * D:r * D + n])
                        last.then_inc(z_stat, 1)
                        if c + 1 < CHUNKS:
                            V.tensor_copy(half_of_acc(T - CHUNK_T0[c], 1).rearrange("p (r n) -> p r n", n=P),
                                          zeros[:].unsqueeze(1).to_broadcast([P, R // 2, P])).then_inc(cleared[1], 1)

                    for c in range(CHUNKS):
                        if c:
                            for half in range(2):
                                dve.wait_ge(cleared[half], layer * CHUNK_T0[CHUNKS - 1] + CHUNK_T0[c])
                            start = CHUNK_TILES[c] * P * R
                            then(V.memset(arena[:, start:start + W * R], 0.0))
                        else:
                            then(V.memset(acc_halves(stage)[0], 0.0))
                            dve.wait_ge(acc_zero, ZEROED.index(stage) + 1)
                        g0, _, u0 = chunk_values(dve, layer, c)
                        build_unit(stage, 1 + c, dyn, g0, u0, 0)
                        chunk_groups(dve, layer, c, pass_group(stage, 1 + c, dyn), peel_last=True)
                        tiles(dve, [(0, z_stats)], CHUNK_T0[c], CHUNK_T0[c + 1])
                        for q in range(2, 4):
                            dve.wait_ge(z_out[q], 16 * (PER4[q] * layer + len(range(q, CHUNK_T0[c + 1], 4))))
                    dve.wait_ge(z_stat, count(stage, NT - 1, REL))
                    dve.wait_ge(relw_in, 64 * (layer + 1))
                    for r in range(R + 1):
                        last = V.bn_aggr(zmv[:, r, :], zst[:, :, r, :])
                    last.then_inc(bn_mv, 1)
                    then(V.tensor_reduce(relbias[:, 1:2], relv[:, 3, :], AX.X, ALU.add))
                    then(V.tensor_tensor(relbias[:, 1:2], relbias[:, 1:2], relbias[:, 0:1], ALU.add))
                    dve.wait_ge(bn_sd, layer + 1)
                    then(V.reciprocal(bn[:, 1, :], bn[:, 0, :]))
                    then(V.tensor_tensor(bn[:, 2, :], relv[:, 1, :], bn[:, 1, :], ALU.mult))
                    then(V.tensor_tensor(bn[:, 3, :], zmv[:, :, 0], bn[:, 2, :], ALU.mult))
                    V.tensor_tensor(bn[:, 3, :], relv[:, 2, :], bn[:, 3, :], ALU.subtract).then_inc(bn_ok, 1)
                else:
                    then(V.memset(acc_halves(stage)[0], 0.0))
                    if stage in ZEROED:
                        dve.wait_ge(acc_zero, ZEROED.index(stage) + 1)
                    build_unit(stage, 0, stat, PASS[stage], 0, 0)
                    static_groups(dve, stage, pass_group(stage, 0, stat), peel_last=True)
                    dve.wait_ge(stat.added, (PASS[stage] + NG + 1) * G)
                    if stage == "L0a":
                        then(V.tensor_scalar(rdeg[:], acc3[:, 1, 0:NP], 1.0, None, ALU.max))

                def scale_z(T, b, h, q, k):
                    dve.wait_ge(z_in[q], (k + 1 + PER4[q] * layer) * 16)
                    for r in range(ACT_RELUS, R + 1):
                        last = V.tensor_scalar(zb[:, q, r * D:(r + 1) * D], zb[:, q, r * D:(r + 1) * D],
                                               bn[:, 2, r:r + 1], bn[:, 3, r:r + 1], ALU.mult, ALU.add)
                    last.then_inc(z_scaled, 1)

                def relu_z(T, b, h, q, k):
                    dve.wait_ge(z_scaled, count(stage, T, REL))
                    V.tensor_scalar(zb[:, q, ACT_RELUS * D:], zb[:, q, ACT_RELUS * D:], 0.0, None, ALU.max).then_inc(z_dve, 1)

                def invert_degree(T, b, h, q, k):
                    mark(dve, "dve")
                    V.reciprocal(rdeg[:, cols(T)], rdeg[:, cols(T)]).then_inc(rdeg_ok, 1)

                def mean(T, b, h, q, k):
                    if not early(T):
                        dve.wait_ge(sum_ok, count(stage, T - 2))
                    if stage == "L0a":
                        dve.wait_ge(rdeg_ok, T + 1)
                    V.tensor_tensor(t_a[:, b, 0:P], acc3[:, 0, cols(T)], rdeg[:, cols(T)], ALU.mult).then_inc(mean_ok, 1)

                def prelu_min(T, b, h, q, k):
                    i = PRELU.index(stage)
                    dve.wait_ge(relu_ok, count(stage, T, PRELU))
                    if not early(T):
                        dve.wait_ge(evac_ok, count(stage, T - 2))
                    V.tensor_scalar(t_m[:, b, :], ps[:, b, 0:P], wsb["L3_b"][:, i:i + 1], 0.0, ALU.add, ALU.min).then_inc(min_ok, 1)

                def prelu_sum(T, b, h, q, k):
                    dve.wait_ge(min_ok, count(stage, T, PRELU))
                    if not early(T):
                        dve.wait_ge(turn_ok, count(stage, T - 2))
                        if stage in KEEP:
                            dve.wait_ge(kept_ok, count(stage, T - 2, KEEP))
                    V.scalar_tensor_tensor(t_y[:, b, 0:P], t_m[:, b, :], wsb["prelu_w"][:, 0:1], t_b[:, b, :], ALU.mult, ALU.add).then_inc(evac_ok, 1)

                def add_residual(T, b, h, q, k):
                    dve.wait_ge(turn_ok, count(stage, T))
                    dve.wait_ge(x_in[q], place_count(stage, q, k, NORM))
                    if not early(T, 4):
                        dve.wait_ge(row_ok, count(stage, T - 4))
                    V.tensor_tensor(t_n[:, q, :], ps[:, 2 + b, 0:P], t_x[:, q, :], ALU.add).then_inc(res_ok, 1)

                def norm_stats(T, b, h, q, k):
                    dve.wait_ge(res_ok, count(stage, T, NORM))
                    if not early(T):
                        dve.wait_ge(mv_ok, count(stage, T - 2, NORM))
                    V.bn_stats(st6[:, b, :], t_n[:, q, :]).then_inc(lnst_ok, 1)

                def norm_aggr(T, b, h, q, k):
                    dve.wait_ge(lnst_ok, count(stage, T, NORM))
                    if not early(T):
                        dve.wait_ge(row_ok, count(stage, T - 2))
                    mark(dve, "dve")
                    V.bn_aggr(mv[:, b, :], st6[:, b, :]).then_inc(mv_ok, 1)

                def invert_root(T, b, h, q, k):
                    dve.wait_ge(sd_ok, count(stage, T, NORM))
                    if not early(T):
                        dve.wait_ge(row_ok, count(stage, T - 2))
                    V.reciprocal(sd[:, b, 1:2], sd[:, b, 0:1]).then_inc(rstd_ok, 1)

                def normalise(T, b, h, q, k):
                    dve.wait_ge(rstd_ok, count(stage, T, NORM))
                    dve.wait_ge(stored[q], place_count(stage, q, k - 1))
                    if stage != final and not early(T, 4):
                        dve.wait_ge(back_ok, count(stage, T - 4, NORM))
                    V.tensor_scalar(rowt[:, q, :], t_n[:, q, :], mv[:, b, 0:1], sd[:, b, 1:2],
                                    ALU.subtract, ALU.mult).then_inc(row_ok, 1)

                if stage in REL:
                    dve.wait_ge(bn_ok, layer + 1)
                lag = 3 if stage in PRELU else 2
                all_steps = [("norm", lag + 2, invert_root), ("sage", 1 if stage == "L0a" else 0, mean), ("rel", 0, scale_z),
                             ("first", 0, invert_degree), ("norm", lag, add_residual), ("prelu", 1, prelu_min),
                             ("norm", lag + 2, normalise), ("rel", 0, relu_z), ("norm", lag, norm_stats),
                             ("prelu", 1, prelu_sum), ("norm", lag, norm_aggr)]
                part = {"norm": stage in NORM, "sage": stage in SAGE, "rel": stage in REL, "first": stage == "L0a",
                        "prelu": stage in PRELU}
                steps = [(n, step) for kind, n, step in all_steps if part[kind]]
                if steps:
                    tiles(dve, steps)


def lay_out(inputs, n_layers):
    def edge_tiles(a):
        return a.reshape(ETP, P).T

    def padded(a, rows, fill=0):
        full = np.full((rows,) + a.shape[1:], fill, a.dtype)
        full[:a.shape[0]] = a
        return full

    a = {k: np.asarray(v) for k, v in inputs.items()}
    EP = ETP * P
    x = padded(a["x"], NP)
    dst = padded(a["dst"], EP, -1)
    arrays = {
        "x": x, "x_t": x.T,
        "src": edge_tiles(padded(a["src"], EP)),
        "dst": edge_tiles(dst), "dst_tiles": dst.reshape(TROWS, UPP * UNIT * P),
        "etype": edge_tiles(padded(a["edge_type_8"], EP)),
        "ea4": padded(a["edge_attr_4"], EP).reshape(ETP, P, 4).transpose(1, 0, 2).reshape(P, ETP * 4),
        "ea8": padded(a["edge_attr_8"], EP).reshape(NU, 2, UNIT // 2 * P, RADIAL).transpose(1, 3, 0, 2).reshape(2 * RADIAL, -1),
    }

    def twice(m):
        k, n = m.shape
        full = np.zeros((2 * k, 2 * n), m.dtype)
        full[:k, :n], full[k:, n:] = m, m
        return full

    def halves(m):
        return m.reshape(2, P, m.shape[1]).transpose(1, 0, 2).reshape(P, -1)

    w00, w01, w10, w11 = (a["L1_gnn_Wp_" + k] for k in ("00", "01", "10", "11"))
    w0, w1 = a["L1_gnn_W1_0e"], a["L1_gnn_W1_1o"]
    c0, c1 = a["L1_gnn_W2_0e"], a["L1_gnn_W2_1o"]
    F, Fself = np.zeros((D, D), np.float32), np.zeros((D, D), np.float32)
    F[:MUL, :MUL], Fself[:MUL, :MUL] = w0[:, :MUL], w0[:, MUL:]
    M = np.zeros((D, 2 * D), np.float32)
    M[:MUL, :MUL] = c0[:MUL]
    for i in range(3):
        b = MUL + MUL * i
        F[MUL + i::3, b:b + MUL] = w1[:, :MUL]
        Fself[MUL + i::3, MUL + i::3] = w1[:, MUL:]
        M[b:b + MUL, MUL + i:D:3] = c1[MUL:]
        M[MUL * i:MUL * (i + 1), D + MUL + i:2 * D:3] = c1[:MUL]
    M[96:128, D:D + MUL] = c0[MUL:]
    weights = {
        "L0_W1l": a["L0_gnn_W1_l"].T, "L0_W1r": a["L0_gnn_W1_r"].T,
        "L0_b1": a["L0_gnn_b1"].reshape(2, P).T, "L0_b2": a["L0_gnn_b2"].reshape(P, 1),
        "L0_W2l": halves(a["L0_gnn_W2_l"].T), "L0_W2r": halves(a["L0_gnn_W2_r"].T),
        "F": F, "Fself": Fself, "M": M, "mlp1": twice(a["L1_gnn_W_mlp1"]), "mlp2": twice(a["L1_gnn_W_mlp2"]),
        "mlp3": twice(np.concatenate([w00, w10, w01, w11], axis=1)),
        "L3_Wl": np.concatenate([a[f"L3_gnn_W{i}l"].T for i in (1, 2, 3)], axis=1),
        "L3_Wr": np.concatenate([a[f"L3_gnn_W{i}r"].T for i in (1, 2, 3)], axis=1),
        "L3_b": np.stack([a[f"L3_gnn_b{i}"] for i in (1, 2, 3)], axis=1),
        "prelu_w": np.broadcast_to(a["L3_gnn_prelu_w"].reshape(1, 1), (P, 1)),
    }
    rel = []
    for i in range(2):
        p = f"L2_gnn_l{i}_"
        rel.append({
            "W1": a[p + "W1"].transpose(1, 0, 2), "W2": a[p + "W2"].transpose(1, 0, 2),
            "v": np.stack([a[p + k].T for k in ("b1", "gamma", "beta", "b2")], axis=1),
            "bias": a[p + "bias"].reshape(P, 1),
        })
    return arrays, weights, rel


LAYERS = 4


def kernel(**inputs):
    import concourse.bacc as _bacc
    from concourse.bass_utils import run_bass_kernel_spmd as _run

    nc = _bacc.Bacc("TRN2", target_bir_lowering=False, num_devices=1, dynamic_dma_scratch_size=8192)
    arrays, weights, rel = lay_out(inputs, LAYERS)
    feeds = {}

    def feed(name, a):
        a = np.ascontiguousarray(a)
        feeds[f"in_{name}_dram"] = a
        return nc.dram_tensor(f"in_{name}_dram", a.shape, mybir.dt.from_np(a.dtype), kind="ExternalInput").ap()

    args = [feed(k, arrays[k]) for k in ("x", "x_t", "src", "dst", "dst_tiles", "etype", "ea4", "ea8")]
    w = {k: feed("w_" + k, a) for k, a in weights.items()}
    w_rel = [{k: feed(f"rel{i}_{k}", a) for k, a in rel[i].items()} for i in range(2)]
    out = nc.dram_tensor("out_0_dram", (N, D), F32, kind="ExternalOutput").ap()
    build(nc, *args, w, w_rel, out, LAYERS)
    r = _run(nc, [feeds], core_ids=[0])
    return r.results[0]["out_0_dram"]
```
